# Optimizing a Trainium2 kernel written in Bass

```python
import numpy as np
import jax
import jax.numpy as jnp

def _softmax(x, axis=-1):
    return jax.nn.softmax(x, axis=axis)

def _gelu(x):
    return jax.nn.gelu(x, approximate=True)

def _silu(x):
    return jax.nn.silu(x)

def _sigmoid(x):
    return jax.nn.sigmoid(x)

def _layernorm(x, axis=-1, eps=1e-05):
    m = jnp.mean(x, axis=axis, keepdims=True)
    v = jnp.var(x, axis=axis, keepdims=True)
    return (x - m) / jnp.sqrt(v + eps)

def _scatter_add(tgt, idx, src, axis=0):
    return tgt.at[idx].add(src)

def _segment_sum(src, seg, n):
    return jax.ops.segment_sum(src, seg, n)
kernel_name = 'mk_gnn_preln_d1_gnn_r8_af5081'

def setup_inputs(seed: int=0):
    np.random.seed(seed)
    _w = jnp.asarray

    def _rec_inputs():
        import jax
        import jax.numpy as jnp
        _gk = jax.random.key(seed)
        x = -0.000202 + 1 * jax.random.normal(jax.random.fold_in(_gk, 1), (12500, 128), jnp.float32)
        src = jax.random.randint(jax.random.fold_in(_gk, 2), (200000,), 0, 12500, jnp.int32)
        dst = jax.random.randint(jax.random.fold_in(_gk, 3), (200000,), 0, 12500, jnp.int32)
        _o = jnp.argsort(dst, stable=True)
        src = src[_o]
        dst = dst[_o]
        return (x, src, dst)
    x, src, dst = _rec_inputs()

    def _L0_gnn_setup():
        import jax, jax.numpy as jnp
        import numpy as np
        N, E, F, H, L = (6250, 75000, 128, 128, 5)
        key = jax.random.key(seed)
        ks = jax.random.split(key, 16)
        s = 1.0 / np.sqrt(H)
        u = lambda k, shape: jax.random.uniform(k, shape, jnp.float32, -s, s)
        return {'x': jax.random.normal(ks[0], (N, F), jnp.float32), 'edge_index': jax.random.randint(ks[1], (2, E), 0, N, jnp.int64), 'enc_w1': u(ks[2], (H, F)), 'enc_b1': u(ks[3], (H,)), 'enc_w2': u(ks[4], (H, H)), 'enc_b2': u(ks[5], (H,)), 'conv_w': u(ks[6], (L, H, H)), 'gru_wih': u(ks[7], (3 * H, H)), 'gru_whh': u(ks[8], (3 * H, H)), 'gru_bih': u(ks[9], (3 * H,)), 'gru_bhh': u(ks[10], (3 * H,)), 'dec_w1': u(ks[11], (H, H)), 'dec_b1': u(ks[12], (H,)), 'dec_w2': u(ks[13], (F, H)), 'dec_b2': u(ks[14], (F,))}
    _L0_gnn_all = _L0_gnn_setup()
    _L0_gnn_in = {k: v for k, v in _L0_gnn_all.items() if k in ('enc_w1', 'enc_b1', 'enc_w2', 'enc_b2', 'conv_w', 'gru_wih', 'gru_whh', 'gru_bih', 'gru_bhh', 'dec_w1', 'dec_b1', 'dec_w2', 'dec_b2')}
    del _L0_gnn_all
    return {'x': x, 'src': src, 'dst': dst, 'L0_gnn_enc_w1': _L0_gnn_in['enc_w1'], 'L0_gnn_enc_b1': _L0_gnn_in['enc_b1'], 'L0_gnn_enc_w2': _L0_gnn_in['enc_w2'], 'L0_gnn_enc_b2': _L0_gnn_in['enc_b2'], 'L0_gnn_conv_w': _L0_gnn_in['conv_w'], 'L0_gnn_gru_wih': _L0_gnn_in['gru_wih'], 'L0_gnn_gru_whh': _L0_gnn_in['gru_whh'], 'L0_gnn_gru_bih': _L0_gnn_in['gru_bih'], 'L0_gnn_gru_bhh': _L0_gnn_in['gru_bhh'], 'L0_gnn_dec_w1': _L0_gnn_in['dec_w1'], 'L0_gnn_dec_b1': _L0_gnn_in['dec_b1'], 'L0_gnn_dec_w2': _L0_gnn_in['dec_w2'], 'L0_gnn_dec_b2': _L0_gnn_in['dec_b2']}

def reference(x, src, dst, L0_gnn_enc_w1, L0_gnn_enc_b1, L0_gnn_enc_w2, L0_gnn_enc_b2, L0_gnn_conv_w, L0_gnn_gru_wih, L0_gnn_gru_whh, L0_gnn_gru_bih, L0_gnn_gru_bhh, L0_gnn_dec_w1, L0_gnn_dec_b1, L0_gnn_dec_w2, L0_gnn_dec_b2):
    import jax
    import jax.numpy as jnp

    def _L0_gnn_ref(x, edge_index, enc_w1, enc_b1, enc_w2, enc_b2, conv_w, gru_wih, gru_whh, gru_bih, gru_bhh, dec_w1, dec_b1, dec_w2, dec_b2):
        import jax, jax.numpy as jnp
        import numpy as np
        N, E, F, H, L = (6250, 75000, 128, 128, 5)
        src, dst = (edge_index[0], edge_index[1])
        n_nodes = x.shape[0]
        h = jnp.maximum(x @ enc_w1.T + enc_b1, 0.0) @ enc_w2.T + enc_b2

        def step(h, w):
            m = h @ w
            agg = jax.ops.segment_sum(m[src], dst, num_segments=n_nodes)
            gi = agg @ gru_wih.T + gru_bih
            gh = h @ gru_whh.T + gru_bhh
            ir, iz, i_n = jnp.split(gi, 3, axis=1)
            hr, hz, h_n = jnp.split(gh, 3, axis=1)
            r = jax.nn.sigmoid(ir + hr)
            z = jax.nn.sigmoid(iz + hz)
            n = jnp.tanh(i_n + r * h_n)
            return ((1.0 - z) * n + z * h, None)
        h, _ = jax.lax.scan(step, h, conv_w)
        h = jnp.maximum(h, 0.0)
        out = jnp.maximum(h @ dec_w1.T + dec_b1, 0.0) @ dec_w2.T + dec_b2
        return jax.nn.sigmoid(out)
    edge_index = jnp.stack([src, dst])
    h = jnp.maximum(_layernorm(x, axis=-1), 0.0)
    x = x + _L0_gnn_ref(h, edge_index, L0_gnn_enc_w1, L0_gnn_enc_b1, L0_gnn_enc_w2, L0_gnn_enc_b2, L0_gnn_conv_w, L0_gnn_gru_wih, L0_gnn_gru_whh, L0_gnn_gru_bih, L0_gnn_gru_bhh, L0_gnn_dec_w1, L0_gnn_dec_b1, L0_gnn_dec_w2, L0_gnn_dec_b2)
    return x

_drawn_inputs = setup_inputs


def setup_inputs(seed=0):
    import zlib

    import numpy as np

    out = dict(_drawn_inputs(seed))
    spreads = {}
    factors = {'L0_gnn_enc_w1': 3.444,
     'L0_gnn_enc_b1': 5.835,
     'L0_gnn_enc_w2': 3.867,
     'L0_gnn_enc_b2': 9.198,
     'L0_gnn_conv_w': 4.2,
     'L0_gnn_gru_wih': 2.715,
     'L0_gnn_gru_whh': 21.298,
     'L0_gnn_gru_bih': 200.0,
     'L0_gnn_gru_bhh': 200.0,
     'L0_gnn_dec_b1': 8.0,
     'L0_gnn_dec_b2': 4.985}
    for name, (base, spread) in spreads.items():
        noise = np.random.default_rng([zlib.crc32(name.encode()), seed]).standard_normal(out[name].shape)
        drawn = base * np.exp(spread * noise) if base else spread * noise
        out[name] = jnp.asarray(drawn.astype(out[name].dtype))
    for name, factor in factors.items():
        out[name] = (out[name] * factor).astype(out[name].dtype)
    return out
```

```python
from contextlib import ExitStack

import concourse.bass as bass
from concourse import mybir

P = 128
F32 = mybir.dt.float32
I32 = mybir.dt.int32
ALU = mybir.AluOpType
ACT = mybir.ActivationFunctionType
AX_X = mybir.AxisListType.X

N_NODES = 12500
N_EDGES = 200000
LAYERS = 5
H = 128

CHUNK = 512
CHUNKS = -(-N_NODES // CHUNK)
LAST = CHUNKS - 1
LAST_J = -(-(N_NODES - LAST * CHUNK) // P)
NODES_PAD = LAST * CHUNK + LAST_J * P
NODE_TILES = NODES_PAD // P

TILES = -(-N_EDGES // P)
GT = 8
GROUPS = -(-TILES // GT)
GROUP_NODES = NODES_PAD // GROUPS
MARGIN = 64
WINDOW = GROUP_NODES + 2 * MARGIN
STEPS = CHUNK // GROUP_NODES
TAIL_GROUPS = GROUPS - LAST * STEPS
SLOTS = 4
AGG_COLS = (GROUPS - 1) * GROUP_NODES + WINDOW
DUMP_ROWS = P
EPS = 1e-5

assert GROUP_NODES * GROUPS == NODES_PAD and GROUPS % SLOTS == 0 and STEPS % SLOTS == 0
assert MARGIN + NODES_PAD <= AGG_COLS and MARGIN <= GROUP_NODES

W_ENC1, W_ENC2, W_IH, W_HH, W_DEC1, W_DEC2, W_CONV = 0, 1, 2, 5, 8, 9, 10
W_BLOCKS = W_CONV + LAYERS
B_ENC1, B_ENC2, B_IH, B_HH, B_DEC1 = 0, 1, 2, 5, 8
B_COLS = 9
R, Z, N = 0, 1, 2
N_CONSTS = 8
STEP_OUTSIDE = 10
STEP_LN = 19


def tiles_of(group):
    return min(GT, TILES - group * GT)


def wait(engine, semaphore, value):
    if not isinstance(value, int) or value > 0:
        engine.wait_ge(semaphore, value)


def gnn(nc, x, src, dst, weights, biases, dec_b2, out):
    table = [nc.dram_tensor(f"table{i}", (NODES_PAD, H), F32, kind="Internal").ap() for i in range(2)]
    sums = nc.dram_tensor("sums", (NODES_PAD + DUMP_ROWS, H), F32, kind="Internal").ap()

    def chunk_rows(rows, c, j):
        if j == CHUNK // P:
            return rows[0:LAST * CHUNK, :].rearrange("(c p j) f -> c p (j f)", p=P, j=j)[c, :, :]
        return rows[LAST * CHUNK:NODES_PAD, :].rearrange("(p j) f -> p (j f)", j=j)

    ctx = ExitStack()
    with ctx:
        def sb(name, shape, dt=F32):
            return ctx.enter_context(nc.sbuf_tensor(name, shape, dt))

        def ps(name):
            return ctx.enter_context(nc.psum_tensor(name, [P, CHUNK], F32))

        def sem(name):
            return ctx.enter_context(nc.semaphore(name))

        state = sb("state", [P, NODES_PAD])
        agg = sb("agg", [P, AGG_COLS])
        x_rows = agg
        w = sb("w", [P, W_BLOCKS * H])
        b = sb("b", [P, B_COLS])
        b_rz = sb("b_rz", [P, 2])
        b2_row = sb("b2_row", [1, H])
        b2_all = sb("b2_all", [P, H])
        ones_all = sb("ones_all", [P, P])
        identity = sb("identity", [P, P])
        src_all = sb("src_all", [P, GROUPS * GT], I32)
        dst_all = sb("dst_all", [P, GROUPS * GT], I32)
        dst_rel = sb("dst_rel", [P, GROUPS * GT])
        base_i = sb("base_i", [P, GROUPS * GT], I32)
        base_f = sb("base_f", [P, GROUPS * GT])
        cols_i = sb("cols_i", [P, WINDOW], I32)
        cols_f = sb("cols_f", [P, WINDOW])
        outside = sb("outside", [P, 2])
        n_outside = sb("n_outside", [1, 1], I32)
        src_stage = sb("src_stage", [P, STEPS * GT], I32)
        dst_stage = sb("dst_stage", [P, STEPS * GT])
        messages = sb("messages", [P, SLOTS, GT, H])
        selection = sb("selection", [P, 2, GT, WINDOW])
        gate_r = sb("gate_r", [P, CHUNK])
        gate_z = sb("gate_z", [P, CHUNK])
        pre_n = sb("pre_n", [P, CHUNK])
        gate_n = sb("gate_n", [P, CHUNK])
        diff = sb("diff", [P, CHUNK])
        h_new = sb("h_new", [P, CHUNK])
        table_stage = sb("table_stage", [P, CHUNK])
        x_stage = sb("x_stage", [P, CHUNK])
        lower = sb("lower", [P, P])
        dump_i = sb("dump_i", [P, 1], I32)
        dump = sb("dump", [P, 1])
        tile_src = sb("tile_src", [P, 1], I32)
        tile_dst = sb("tile_dst", [P, 1])
        tile_row = sb("tile_row", [P, 1])
        tile_dup = sb("tile_dup", [P, 1])
        tile_index = sb("tile_index", [P, 1], I32)
        tile_diag = selection[:, 0, 0, 0:P]
        tile_equal = selection[:, 0, 1, 0:P]
        tile_before = selection[:, 0, 2, 0:P]
        tile_messages = messages[:, 0, 0, :]
        tile_sums = messages[:, 0, 1, :]
        sum_rows = messages[:, 1, 0:CHUNK // H, :].rearrange("p t f -> p (t f)")
        stats = sb("stats", [P, NODE_TILES, 6])
        mean = sb("mean", [P, NODE_TILES])
        rstd = sb("rstd", [P, NODE_TILES])
        ln_a = sb("ln_a", [P, NODE_TILES])
        ln_b = sb("ln_b", [P, NODE_TILES])
        x_norm, xT, encT = gate_r, gate_z, gate_n
        relu_h, decT, out_stage = gate_r, diff, table_stage

        agg_ps = [ps("agg_ps0"), ps("agg_ps1")]
        r_ps, z_ps, hn_ps, in_ps = ps("r_ps"), ps("z_ps"), ps("hn_ps"), ps("in_ps")
        table_ps, dec_ps = ps("table_ps"), ps("dec_ps")
        tr_ps, enc1_ps, enc2_ps = r_ps, z_ps, hn_ps

        loaded = sem("loaded")
        x_loaded = sem("x_loaded")
        consts = sem("consts")
        prep = sem("prep")
        prep_sum = sem("prep_sum")
        n_ready = sem("n_ready")
        ln_std = sem("ln_std")
        normed = sem("normed")
        transposed = sem("transposed")
        xT_ready = sem("xT_ready")
        enc1_done = sem("enc1_done")
        encT_ready = sem("encT_ready")
        enc2_done = sem("enc2_done")
        h0_ready = sem("h0_ready")
        src_staged = sem("src_staged")
        gathered = [sem(f"gathered{i}") for i in range(SLOTS)]
        pool_turns = sem("pool_turns")
        dst_staged = sem("dst_staged")
        selected = sem("selected")
        summed = sem("summed")
        agg_added = sem("agg_added")
        gates_ps = sem("gates_ps")
        gates_rz = sem("gates_rz")
        cand = sem("cand")
        gru = sem("gru")
        h_stored = sem("h_stored")
        table_sum = sem("table_sum")
        table_out = sem("table_out")
        table_stored = sem("table_stored")
        relu_ready = sem("relu_ready")
        dec1_done = sem("dec1_done")
        decT_ready = sem("decT_ready")
        dec2_done = sem("dec2_done")
        dec_biased = sem("dec_biased")
        dec_sig = sem("dec_sig")
        x_again = sem("x_again")
        out_ready = sem("out_ready")
        out_stored = sem("out_stored")

        g_zeros = sem("g_zeros")
        g_cleared = sem("g_cleared")
        g_src = sem("g_src")
        g_gathered = sem("g_gathered")
        g_step = sem("g_step")
        g_product = sem("g_product")
        g_scattered = sem("g_scattered")
        g_rows = sem("g_rows")
        g_turned = sem("g_turned")
        g_agg = sem("g_agg")

        block = ctx.enter_context(nc.Block())

        def wblock(k):
            return w[:, k * H:(k + 1) * H]

        def slot_done(layer, slot, uses):
            tiles = sum(tiles_of(g) for g in range(slot, GROUPS, SLOTS))
            return 16 * (layer * tiles + GT * uses) if not isinstance(uses, int) else 16 * (
                layer * tiles + min(GT * uses, tiles))

        G_STEPS = 10

        def any_outside(engine):
            engine.wait_ge(n_ready, 1)
            return engine.value_load(n_outside[0:1, 0:1], min_val=0, max_val=2 * P) > 0

        @block.sync
        def _(sp):
            full = LAST * CHUNK
            sp.dma_start(x_rows[:, 0:full].rearrange("p (c n) -> p c n", n=CHUNK),
                         x[0:full, :].rearrange("(c p j) f -> p c (j f)", p=P, j=CHUNK // P)).then_inc(x_loaded, 16)
            sp.dma_start(x_rows[:, full:NODES_PAD], chunk_rows(x, LAST, LAST_J)).then_inc(x_loaded, 16)

            def store_table(t, u, c, j):
                sp.wait_ge(table_out, u + 1)
                sp.dma_start(chunk_rows(table[t], c, j), table_stage[:, 0:j * H]).then_inc(table_stored, 16)

            def store_out(c, j):
                wait(sp, out_ready, c)
                sp.dma_start(x_stage[:, 0:j * H], chunk_rows(x, c, j)).then_inc(x_again, 16)
                sp.wait_ge(out_ready, c + 1)
                sp.dma_start(chunk_rows(out, c, j), out_stage[:, 0:j * H]).then_inc(out_stored, 16)

            with sp.Fori(0, LAST) as c:
                store_table(0, c, c, CHUNK // P)
            store_table(0, LAST, LAST, LAST_J)

            def finish(layer, c, j):
                if layer < LAYERS - 1:
                    store_table((layer + 1) % 2, CHUNKS * (layer + 1) + c, c, j)
                else:
                    store_out(c, j)

            def fast():
                for layer in range(LAYERS):
                    finish(layer, 0, CHUNK // P)
                    with sp.Fori(1, LAST) as c:
                        finish(layer, c, CHUNK // P)
                    finish(layer, LAST, LAST_J)

            def general():
                def load_sums(layer, c, j):
                    wait(sp, g_turned, layer * CHUNKS + c)
                    sp.dma_start(sum_rows[:, 0:j * H], chunk_rows(sums[0:NODES_PAD, :], c, j)).then_inc(g_rows, 16)

                for layer in range(LAYERS):
                    sp.wait_ge(g_zeros, layer + 1)
                    sp.dma_start(sums.rearrange("(p r) f -> p (r f)", p=P), agg[:, :]).then_inc(g_cleared, 16)
                    sp.wait_ge(g_scattered, 16 * TILES * (layer + 1))
                    load_sums(layer, 0, CHUNK // P)
                    finish(layer, 0, CHUNK // P)
                    with sp.Fori(1, LAST) as c:
                        load_sums(layer, c, CHUNK // P)
                        finish(layer, c, CHUNK // P)
                    load_sums(layer, LAST, LAST_J)
                    finish(layer, LAST, LAST_J)

            with sp.If(any_outside(sp)):
                general()
            with sp.Else():
                fast()
            sp.wait_ge(out_stored, 16 * CHUNKS)

        @block.gpsimd
        def _(pool):
            nc.gpsimd.iota(base_i[:, :].rearrange("p (g t) -> p g t", t=GT), pattern=[[GROUP_NODES, GROUPS], [0, GT]],
                           base=-MARGIN, channel_multiplier=0).then_inc(consts, 1)
            nc.gpsimd.iota(cols_i[:, :], pattern=[[1, WINDOW]], base=0, channel_multiplier=0).then_inc(consts, 1)
            nc.gpsimd.memset(ones_all[:, :], 1.0).then_inc(consts, 1)
            nc.gpsimd.memset(identity[:, :], 0.0).then_inc(consts, 1)
            nc.gpsimd.memset(lower[:, :], 1.0).then_inc(consts, 1)
            nc.gpsimd.iota(dump_i[:, :], pattern=[[0, 1]], base=NODES_PAD, channel_multiplier=1).then_inc(consts, 1)
            pool.wait_ge(consts, N_CONSTS - 2)
            nc.gpsimd.affine_select(out=identity[:, :], in_=identity[:, :], compare_op=ALU.not_equal, fill=1.0,
                                    base=0, pattern=[[-1, P]], channel_multiplier=1).then_inc(consts, 1)
            nc.gpsimd.affine_select(out=lower[:, :], in_=lower[:, :], compare_op=ALU.is_gt, fill=0.0,
                                    base=0, pattern=[[-1, P]], channel_multiplier=1).then_inc(consts, 1)

            def gather_half(layer, c, half, steps):
                at, n = half * SLOTS * GT, len(steps) * GT
                columns = bass.ds(c * (STEPS * GT) + at, n)
                nc.gpsimd.tensor_copy(src_stage[:, at:at + n], src_all[:, columns]).then_inc(src_staged, 1)
                pool.wait_ge(src_staged, 2 * CHUNKS * layer + 2 * c + half + 1)
                pool.sem_inc(pool_turns, 1)
                for s in steps:
                    slot = s % SLOTS
                    wait(pool, summed, layer * GROUPS + c * STEPS + (s - SLOTS + 1))
                    pool.sem_inc(pool_turns, 1)
                    n_tiles = tiles_of(c * STEPS + s) if isinstance(c, int) else GT
                    for t in range(n_tiles):
                        k = s * GT + t
                        nc.gpsimd.indirect_dma_start(
                            messages[:, slot, t, :], None, table[layer % 2],
                            bass.IndirectOffsetOnAxis(ap=src_stage[:, k:k + 1], axis=0)).then_inc(gathered[slot], 16)

            def fast():
                for layer in range(LAYERS):
                    pool.wait_ge(table_stored, 16 * CHUNKS * (layer + 1))
                    gather_half(layer, 0, 0, range(SLOTS))
                    gather_half(layer, 0, 1, range(SLOTS, STEPS))
                    with pool.Fori(1, LAST) as c:
                        gather_half(layer, c, 0, range(SLOTS))
                        gather_half(layer, c, 1, range(SLOTS, STEPS))
                    gather_half(layer, LAST, 0, range(TAIL_GROUPS))
                    pool.sem_inc(src_staged, 1)

            def general():
                def one_tile(layer, k):
                    wait(pool, g_scattered, 16 * (layer * TILES + k))
                    pool.sem_inc(pool_turns, 1)
                    nc.gpsimd.tensor_copy(tile_src[:, :], src_all[:, bass.ds(k, 1)]).then_inc(g_src, 1)
                    pool.wait_ge(g_src, layer * TILES + k + 1)
                    pool.sem_inc(pool_turns, 1)
                    nc.gpsimd.indirect_dma_start(tile_messages, None, table[layer % 2],
                                                 bass.IndirectOffsetOnAxis(ap=tile_src[:, 0:1], axis=0)).then_inc(g_gathered, 16)
                    pool.wait_ge(g_step, G_STEPS * (layer * TILES + k + 1))
                    pool.sem_inc(pool_turns, 1)
                    nc.gpsimd.indirect_dma_start(sums, bass.IndirectOffsetOnAxis(ap=tile_index[:, 0:1], axis=0),
                                                 tile_sums, None, compute_op=ALU.add).then_inc(g_scattered, 16)

                for layer in range(LAYERS):
                    pool.wait_ge(table_stored, 16 * CHUNKS * (layer + 1))
                    pool.wait_ge(g_cleared, 16 * (layer + 1))
                    one_tile(layer, 0)
                    with pool.Fori(1, TILES) as k:
                        one_tile(layer, k)

            pool.wait_ge(loaded, 16 * 5)
            with pool.If(any_outside(pool)):
                general()
            with pool.Else():
                fast()

        @block.scalar
        def _(act):
            act.dma_start(w[:, :], weights).then_inc(loaded, 16)
            act.dma_start(b[:, :], biases).then_inc(loaded, 16)
            act.dma_start(b2_row[:, :], dec_b2).then_inc(loaded, 16)
            act.dma_start(src_all[:, :], src).then_inc(loaded, 16)
            act.dma_start(dst_all[:, :], dst).then_inc(loaded, 16)
            act.wait_ge(prep, STEP_LN)
            nc.scalar.activation(ln_b[:, :], ln_b[:, :], ACT.Sqrt).then_inc(ln_std, 1)
            act.wait_ge(loaded, 16 * 5)

            def encode(c, j):
                n = j * P
                act.wait_ge(transposed, c + 1)
                wait(act, enc1_done, c)
                nc.scalar.activation(xT[:, 0:n].rearrange("f (p j) -> f j p", j=j),
                                     tr_ps[:, 0:n].rearrange("f (j p) -> f j p", j=j), ACT.Relu).then_inc(xT_ready, 1)
                act.wait_ge(enc1_done, c + 1)
                wait(act, enc2_done, c)
                nc.scalar.activation(encT[:, 0:n], enc1_ps[:, 0:n], ACT.Relu,
                                     bias=b[:, B_ENC1:B_ENC1 + 1]).then_inc(encT_ready, 1)
                act.wait_ge(enc2_done, c + 1)
                wait(act, table_sum, c)
                wait(act, h_stored, c)
                nc.scalar.activation(h_new[:, 0:n], enc2_ps[:, 0:n], ACT.Identity,
                                     bias=b[:, B_ENC2:B_ENC2 + 1]).then_inc(h0_ready, 1)

            with act.Fori(0, LAST) as c:
                encode(c, CHUNK // P)
            encode(LAST, LAST_J)

            def gates(v, c, j):
                n = j * P
                act.wait_ge(gates_ps, 4 * v + 1)
                wait(act, gru, 5 * v)
                nc.scalar.activation(gate_r[:, 0:n], r_ps[:, 0:n], ACT.Sigmoid, bias=b_rz[:, R:R + 1]).then_inc(gates_rz, 1)
                act.wait_ge(gates_ps, 4 * v + 2)
                nc.scalar.activation(gate_z[:, 0:n], z_ps[:, 0:n], ACT.Sigmoid, bias=b_rz[:, Z:Z + 1]).then_inc(gates_rz, 1)
                act.wait_ge(gru, 5 * v + 2)
                nc.scalar.activation(gate_n[:, 0:n], pre_n[:, 0:n], ACT.Tanh, bias=b[:, B_IH + N:B_IH + N + 1]).then_inc(cand, 1)

            def make_table(v, c, j):
                n = j * P
                act.wait_ge(gru, 5 * v + 5)
                nc.scalar.activation(state[:, bass.ds(c * CHUNK, n)], h_new[:, 0:n], ACT.Copy).then_inc(h_stored, 1)
                act.wait_ge(table_sum, v + CHUNKS + 1)
                act.wait_ge(table_stored, 16 * (v + CHUNKS))
                nc.scalar.activation(table_stage[:, 0:n], table_ps[:, 0:n], ACT.Copy).then_inc(table_out, 1)

            def decode(v, c, j):
                n = j * P
                act.wait_ge(gru, 5 * v + 5)
                wait(act, dec1_done, c)
                nc.scalar.activation(relu_h[:, 0:n], h_new[:, 0:n], ACT.Relu).then_inc(relu_ready, 1)
                act.wait_ge(dec1_done, c + 1)
                wait(act, dec2_done, c)
                nc.scalar.activation(decT[:, 0:n], table_ps[:, 0:n], ACT.Relu, bias=b[:, B_DEC1:B_DEC1 + 1]).then_inc(decT_ready, 1)
                act.wait_ge(dec_biased, c + 1)
                nc.scalar.activation(out_stage[:, 0:n], out_stage[:, 0:n], ACT.Sigmoid).then_inc(dec_sig, 1)

            for layer in range(LAYERS):
                finish = make_table if layer < LAYERS - 1 else decode
                v = layer * CHUNKS
                with act.Fori(0, LAST) as c:
                    gates(c + v, c, CHUNK // P)
                    finish(c + v, c, CHUNK // P)
                gates(LAST + v, LAST, LAST_J)
                finish(LAST + v, LAST, LAST_J)

        @block.vector
        def _(dve):
            n_prep = [0]

            def done(instruction):
                n_prep[0] += 1
                instruction.then_inc(prep, 1)
                dve.wait_ge(prep, n_prep[0])

            dve.wait_ge(loaded, 16 * 5)
            dve.wait_ge(consts, N_CONSTS)
            done(nc.vector.tensor_tensor(b_rz[:, :], b[:, B_IH:B_IH + 2], b[:, B_HH:B_HH + 2], ALU.add))
            done(nc.vector.tensor_copy(cols_f[:, :], cols_i[:, :]))
            done(nc.vector.tensor_copy(base_f[:, :], base_i[:, :]))
            done(nc.vector.tensor_copy(dst_rel[:, :], dst_all[:, :]))
            done(nc.vector.tensor_tensor(dst_rel[:, :], dst_rel[:, :], base_f[:, :], ALU.subtract))
            done(nc.vector.tensor_copy(dump[:, :], dump_i[:, :]))
            done(nc.vector.tensor_reduce(outside[:, 0:1], dst_rel[:, :], AX_X, ALU.min))
            done(nc.vector.tensor_reduce(outside[:, 1:2], dst_rel[:, :], AX_X, ALU.max))
            done(nc.vector.tensor_scalar(outside[:, 0:1], outside[:, 0:1], 0.0, None, ALU.is_lt))
            done(nc.vector.tensor_scalar(outside[:, 1:2], outside[:, 1:2], float(WINDOW - 1), None, ALU.is_gt))
            assert n_prep[0] == STEP_OUTSIDE
            dve.wait_ge(prep_sum, 1)
            nc.vector.tensor_copy(n_outside[:, :], table_ps[0:1, 0:1]).then_inc(n_ready, 1)
            dve.wait_ge(prep_sum, 2)
            done(nc.vector.tensor_copy(b2_all[:, :], dec_ps[:, 0:H]))

            dve.wait_ge(x_loaded, 16 * 2)

            def stats_of(c, j):
                for t in range(j):
                    nc.vector.bn_stats(stats[:, bass.ds(c * (CHUNK // P) + t, 1), :].rearrange("p a s -> p (a s)"),
                                       x_rows[:, bass.ds(c * CHUNK + t * H, H)])

            with dve.Fori(0, LAST) as c:
                stats_of(c, CHUNK // P)
            for t in range(LAST_J):
                k = LAST * CHUNK // P + t
                last = nc.vector.bn_stats(stats[:, k, :], x_rows[:, k * H:(k + 1) * H])
            done(last)
            m_even, m_odd, v_even, v_odd = (stats[:, :, k] for k in (1, 4, 2, 5))
            done(nc.vector.tensor_tensor(ln_a[:, :], m_even, m_odd, ALU.subtract))
            done(nc.vector.tensor_tensor(mean[:, :], m_even, m_odd, ALU.add))
            done(nc.vector.tensor_scalar(mean[:, :], mean[:, :], 0.5, None, ALU.mult))
            done(nc.vector.tensor_tensor(ln_a[:, :], ln_a[:, :], ln_a[:, :], ALU.mult))
            done(nc.vector.tensor_tensor(ln_b[:, :], v_even, v_odd, ALU.add))
            done(nc.vector.tensor_scalar(ln_b[:, :], ln_b[:, :], 1.0 / H, EPS, ALU.mult, ALU.add))
            done(nc.vector.scalar_tensor_tensor(out=ln_b[:, :], in0=ln_a[:, :], scalar=0.25, in1=ln_b[:, :],
                                                op0=ALU.mult, op1=ALU.add))
            assert n_prep[0] == STEP_LN
            dve.wait_ge(ln_std, 1)
            done(nc.vector.reciprocal(rstd[:, :], ln_b[:, :]))

            def encode(c, j):
                wait(dve, transposed, c)
                for t in range(j):
                    k = c * (CHUNK // P) + t
                    one = bass.ds(k, 1)
                    last = nc.vector.tensor_scalar(x_norm[:, t * H:(t + 1) * H], x_rows[:, bass.ds(k * H, H)],
                                                   mean[:, one], rstd[:, one], ALU.subtract, ALU.mult)
                last.then_inc(normed, 1)

            def store_h0(c, j):
                n = j * P
                dve.wait_ge(h0_ready, c + 1)
                nc.vector.tensor_copy(state[:, bass.ds(c * CHUNK, n)], h_new[:, 0:n]).then_inc(h_stored, 1)
                dve.wait_ge(table_sum, c + 1)
                wait(dve, table_stored, c * 16)
                nc.vector.tensor_copy(table_stage[:, 0:n], table_ps[:, 0:n]).then_inc(table_out, 1)

            encode(0, CHUNK // P)
            with dve.Fori(0, LAST - 1) as c:
                encode(c + 1, CHUNK // P)
                store_h0(c, CHUNK // P)
            encode(LAST, LAST_J)
            store_h0(LAST - 1, CHUNK // P)
            store_h0(LAST, LAST_J)

            def select(layer, c, s, n_tiles):
                wait(dve, summed, layer * GROUPS + c * STEPS + (s - 1))
                for t in range(n_tiles):
                    k = s * GT + t
                    last = nc.vector.tensor_scalar(selection[:, s % 2, t, :], cols_f[:, :], dst_stage[:, k:k + 1], None,
                                                   ALU.is_equal)
                last.then_inc(selected, 1)

            def add(layer, c, s):
                at = c * CHUNK + s * GROUP_NODES
                g = layer * GROUPS + c * STEPS + s
                part = agg_ps[s % 2]
                old = WINDOW - GROUP_NODES
                dve.wait_ge(summed, g + 1)
                wait(dve, agg_added, 2 * g)
                if isinstance(c, int) and c == 0 and s == 0:
                    nc.vector.tensor_copy(agg[:, 0:old], part[:, 0:old]).then_inc(agg_added, 1)
                else:
                    cols = agg[:, bass.ds(at, old)]
                    nc.vector.tensor_tensor(cols, cols, part[:, 0:old], ALU.add).then_inc(agg_added, 1)
                nc.vector.tensor_copy(agg[:, bass.ds(at + old, GROUP_NODES)], part[:, old:WINDOW]).then_inc(agg_added, 1)

            def gru_first(v, c, j):
                n = j * P
                dve.wait_ge(gates_rz, 2 * v + 1)
                dve.wait_ge(gates_ps, 4 * v + 3)
                wait(dve, cand, v)
                nc.vector.scalar_tensor_tensor(out=pre_n[:, 0:n], in0=hn_ps[:, 0:n], scalar=b[:, B_HH + N:B_HH + N + 1],
                                               in1=gate_r[:, 0:n], op0=ALU.add, op1=ALU.mult).then_inc(gru, 1)
                dve.wait_ge(gru, 5 * v + 1)
                dve.wait_ge(gates_ps, 4 * v + 4)
                nc.vector.tensor_tensor(pre_n[:, 0:n], pre_n[:, 0:n], in_ps[:, 0:n], ALU.add).then_inc(gru, 1)

            def gru_second(v, c, j, in_state):
                n = j * P
                old = state[:, bass.ds(c * CHUNK, n)]
                dve.wait_ge(cand, v + 1)
                nc.vector.tensor_tensor(diff[:, 0:n], old, gate_n[:, 0:n], ALU.subtract).then_inc(gru, 1)
                dve.wait_ge(gru, 5 * v + 3)
                dve.wait_ge(gates_rz, 2 * v + 2)
                nc.vector.tensor_tensor(diff[:, 0:n], diff[:, 0:n], gate_z[:, 0:n], ALU.mult).then_inc(gru, 1)
                dve.wait_ge(gru, 5 * v + 4)
                if in_state:
                    dve.wait_ge(table_sum, v + CHUNKS)
                    dve.wait_ge(h_stored, v + CHUNKS)
                nc.vector.tensor_tensor(h_new[:, 0:n], diff[:, 0:n], gate_n[:, 0:n], ALU.add).then_inc(gru, 1)

            def decode(v, c, j):
                n = j * P
                dve.wait_ge(dec2_done, c + 1)
                wait(dve, out_stored, 16 * c)
                b2 = b2_all[:, :].rearrange("p (a f) -> p a f", a=1).broadcast_to([P, j, H])
                nc.vector.tensor_tensor(out_stage[:, 0:n].rearrange("p (j f) -> p j f", f=H),
                                        dec_ps[:, 0:n].rearrange("p (j f) -> p j f", f=H), b2, ALU.add).then_inc(dec_biased, 1)
                dve.wait_ge(dec_sig, c + 1)
                dve.wait_ge(x_again, 16 * (c + 1))
                nc.vector.tensor_tensor(out_stage[:, 0:n], out_stage[:, 0:n], x_stage[:, 0:n], ALU.add).then_inc(out_ready, 1)

            def iteration(layer, c, steps):
                last_layer = layer == LAYERS - 1
                v = layer * CHUNKS + c - 1
                before = not (isinstance(c, int) and c == 0)
                wait(dve, selected, layer * GROUPS + c * STEPS)
                n = steps * GT
                nc.vector.tensor_copy(dst_stage[:, 0:n], dst_rel[:, bass.ds(c * (STEPS * GT), n)]).then_inc(dst_staged, 1)
                dve.wait_ge(dst_staged, layer * CHUNKS + c + 1)
                for s in range(steps):
                    select(layer, c, s, tiles_of(c * STEPS + s) if isinstance(c, int) else GT)
                    if s:
                        add(layer, c, s - 1)
                    if before and s == 3:
                        gru_first(v, c - 1, CHUNK // P)
                        if steps <= 4:
                            gru_second(v, c - 1, CHUNK // P, not last_layer)
                    if before and s == 4:
                        gru_second(v, c - 1, CHUNK // P, not last_layer)
                    if before and s == 7 and last_layer:
                        decode(v, c - 1, CHUNK // P)
                add(layer, c, steps - 1)
                if steps <= 4 and last_layer:
                    decode(v, c - 1, CHUNK // P)

            def fast():
                for layer in range(LAYERS):
                    last_layer = layer == LAYERS - 1
                    iteration(layer, 0, STEPS)
                    with dve.Fori(1, LAST) as c:
                        iteration(layer, c, STEPS)
                    iteration(layer, LAST, TAIL_GROUPS)
                    v = layer * CHUNKS + LAST
                    gru_first(v, LAST, LAST_J)
                    gru_second(v, LAST, LAST_J, not last_layer)
                    if last_layer:
                        decode(v, LAST, LAST_J)

            def general():
                def one_tile(layer, k):
                    g = G_STEPS * (layer * TILES + k)
                    wait(dve, g_scattered, 16 * (layer * TILES + k))
                    nc.vector.tensor_copy(tile_dst[:, :], dst_all[:, bass.ds(k, 1)]).then_inc(g_step, 1)
                    dve.wait_ge(g_step, g + 1)
                    nc.vector.tensor_scalar(tile_diag, identity[:, :], tile_dst[:, :], None, ALU.mult).then_inc(g_step, 1)
                    dve.wait_ge(g_product, 2 * (layer * TILES + k) + 1)
                    nc.vector.tensor_scalar(tile_equal, agg_ps[0][:, 0:P], tile_dst[:, :], None, ALU.is_equal).then_inc(g_step, 1)
                    dve.wait_ge(g_step, g + 3)
                    nc.vector.tensor_tensor(tile_before, tile_equal, lower[:, :], ALU.mult).then_inc(g_step, 1)
                    dve.wait_ge(g_step, g + 4)
                    nc.vector.tensor_reduce(tile_dup[:, :], tile_before, AX_X, ALU.add).then_inc(g_step, 1)
                    dve.wait_ge(g_step, g + 5)
                    nc.vector.tensor_scalar(tile_dup[:, :], tile_dup[:, :], 0.0, None, ALU.is_gt).then_inc(g_step, 1)
                    nc.vector.tensor_tensor(tile_row[:, :], dump[:, :], tile_dst[:, :], ALU.subtract).then_inc(g_step, 1)
                    dve.wait_ge(g_step, g + 7)
                    nc.vector.tensor_tensor(tile_row[:, :], tile_row[:, :], tile_dup[:, :], ALU.mult).then_inc(g_step, 1)
                    dve.wait_ge(g_step, g + 8)
                    nc.vector.tensor_tensor(tile_index[:, :], tile_row[:, :], tile_dst[:, :], ALU.add).then_inc(g_step, 1)
                    dve.wait_ge(g_product, 2 * (layer * TILES + k) + 2)
                    nc.vector.tensor_copy(tile_sums, agg_ps[1][:, 0:H]).then_inc(g_step, 1)

                def one_chunk(layer, c, j):
                    n = j * P
                    v = layer * CHUNKS + c
                    dve.wait_ge(g_turned, v + 1)
                    nc.vector.tensor_copy(agg[:, bass.ds(c * CHUNK + MARGIN, n)].rearrange("f (p j) -> f j p", j=j),
                                          agg_ps[0][:, 0:n].rearrange("f (j p) -> f j p", j=j)).then_inc(g_agg, 1)
                    gru_first(v, c, j)
                    gru_second(v, c, j, layer < LAYERS - 1)
                    if layer == LAYERS - 1:
                        decode(v, c, j)

                for layer in range(LAYERS):
                    nc.vector.memset(agg[:, :], 0.0).then_inc(g_zeros, 1)
                    dve.wait_ge(g_cleared, 16 * (layer + 1))
                    one_tile(layer, 0)
                    with dve.Fori(1, TILES) as k:
                        one_tile(layer, k)
                    one_chunk(layer, 0, CHUNK // P)
                    with dve.Fori(1, LAST) as c:
                        one_chunk(layer, c, CHUNK // P)
                    one_chunk(layer, LAST, LAST_J)

            with dve.If(any_outside(dve)):
                general()
            with dve.Else():
                fast()

        @block.tensor
        def _(pe):
            pe.wait_ge(loaded, 16 * 5)
            pe.wait_ge(consts, N_CONSTS)
            pe.wait_ge(prep, STEP_OUTSIDE)
            nc.tensor.matmul(table_ps[0:1, 0:1], outside[:, 0:1], ones_all[:, 0:1], start=True, stop=False)
            nc.tensor.matmul(table_ps[0:1, 0:1], outside[:, 1:2], ones_all[:, 0:1], start=False, stop=True).then_inc(prep_sum, 1)
            nc.tensor.matmul(dec_ps[:, 0:H], ones_all[0:1, :], b2_row[:, :], start=True, stop=True).then_inc(prep_sum, 1)

            def rows_of(target, lhs, weight, j):
                for t in range(j):
                    cols = lhs[:, 0:j * P].rearrange("f (p j) -> f j p", j=j)[:, t, :]
                    last = nc.tensor.matmul(target[:, t * H:(t + 1) * H], cols, weight, start=True, stop=True)
                return last

            def transposes(c, j):
                pe.wait_ge(normed, c + 1)
                wait(pe, xT_ready, c)
                for t in range(j):
                    last = nc.tensor.transpose(tr_ps[:, t * P:(t + 1) * P], x_norm[:, t * H:(t + 1) * H], identity[:, :])
                last.then_inc(transposed, 1)

            def encode(c, j):
                n = j * P
                pe.wait_ge(xT_ready, c + 1)
                wait(pe, encT_ready, c)
                nc.tensor.matmul(enc1_ps[:, 0:n], wblock(W_ENC1), xT[:, 0:n], start=True, stop=True).then_inc(enc1_done, 1)
                pe.wait_ge(encT_ready, c + 1)
                wait(pe, h0_ready, c)
                nc.tensor.matmul(enc2_ps[:, 0:n], wblock(W_ENC2), encT[:, 0:n], start=True, stop=True).then_inc(enc2_done, 1)

            def first_table(c, j):
                pe.wait_ge(h0_ready, c + 1)
                wait(pe, table_out, c)
                rows_of(table_ps, h_new, wblock(W_CONV), j).then_inc(table_sum, 1)

            transposes(0, CHUNK // P)
            with pe.Fori(0, LAST - 1) as c:
                encode(c, CHUNK // P)
                transposes(c + 1, CHUNK // P)
                first_table(c, CHUNK // P)
            encode(LAST - 1, CHUNK // P)
            transposes(LAST, LAST_J)
            first_table(LAST - 1, CHUNK // P)
            encode(LAST, LAST_J)
            first_table(LAST, LAST_J)

            def sum_group(layer, c, s, n_tiles):
                g = layer * GROUPS + c * STEPS + s
                slot = s % SLOTS
                pe.wait_ge(gathered[slot], slot_done(layer, slot, c * (STEPS // SLOTS) + (s // SLOTS + 1)))
                pe.wait_ge(selected, g + 1)
                wait(pe, agg_added, 2 * (g - 1))
                for t in range(n_tiles):
                    last = nc.tensor.matmul(agg_ps[s % 2][:, 0:WINDOW], messages[:, slot, t, :], selection[:, s % 2, t, :],
                                            start=(t == 0), stop=(t == n_tiles - 1))
                last.then_inc(summed, 1)

            def gates(v, c, j, complete, count):
                n = j * P
                a = agg[:, bass.ds(c * CHUNK + MARGIN, n)]
                h = state[:, bass.ds(c * CHUNK, n)]
                pe.wait_ge(complete, count)
                wait(pe, gru, 5 * v)
                wait(pe, gates_rz, 2 * v)
                for gate, bank in ((R, r_ps), (Z, z_ps)):
                    nc.tensor.matmul(bank[:, 0:n], wblock(W_HH + gate), h, start=True, stop=False)
                    nc.tensor.matmul(bank[:, 0:n], wblock(W_IH + gate), a, start=False, stop=True).then_inc(gates_ps, 1)
                nc.tensor.matmul(hn_ps[:, 0:n], wblock(W_HH + N), h, start=True, stop=True).then_inc(gates_ps, 1)
                nc.tensor.matmul(in_ps[:, 0:n], wblock(W_IH + N), a, start=True, stop=True).then_inc(gates_ps, 1)

            def make_table(layer, v, c, j):
                pe.wait_ge(gru, 5 * v + 5)
                pe.wait_ge(table_out, v + CHUNKS)
                rows_of(table_ps, h_new, wblock(W_CONV + layer + 1), j).then_inc(table_sum, 1)

            def decode_first(v, c, j):
                n = j * P
                pe.wait_ge(relu_ready, c + 1)
                wait(pe, decT_ready, c)
                nc.tensor.matmul(table_ps[:, 0:n], wblock(W_DEC1), relu_h[:, 0:n], start=True, stop=True).then_inc(dec1_done, 1)

            def decode_second(v, c, j):
                pe.wait_ge(decT_ready, c + 1)
                wait(pe, dec_biased, c)
                rows_of(dec_ps, decT, wblock(W_DEC2), j).then_inc(dec2_done, 1)

            def iteration(layer, c, steps):
                last_layer = layer == LAYERS - 1
                v = layer * CHUNKS + c - 1
                before = not (isinstance(c, int) and c == 0)
                for s in range(steps):
                    sum_group(layer, c, s, tiles_of(c * STEPS + s) if isinstance(c, int) else GT)
                    if not before:
                        continue
                    if s == 1:
                        gates(v, c - 1, CHUNK // P, agg_added, 2 * (layer * GROUPS + c * STEPS + 1))
                    if s == 4 and not last_layer:
                        make_table(layer, v, c - 1, CHUNK // P)
                    if s == 5 and last_layer:
                        decode_first(v, c - 1, CHUNK // P)
                    if s == 6 and last_layer:
                        decode_second(v, c - 1, CHUNK // P)
                if steps <= 4:
                    if last_layer:
                        decode_first(v, c - 1, CHUNK // P)
                        decode_second(v, c - 1, CHUNK // P)
                    else:
                        make_table(layer, v, c - 1, CHUNK // P)

            def finish(layer, v, c, j):
                if layer < LAYERS - 1:
                    make_table(layer, v, c, j)
                else:
                    decode_first(v, c, j)
                    decode_second(v, c, j)

            def fast():
                for layer in range(LAYERS):
                    iteration(layer, 0, STEPS)
                    with pe.Fori(1, LAST) as c:
                        iteration(layer, c, STEPS)
                    iteration(layer, LAST, TAIL_GROUPS)
                    v = layer * CHUNKS + LAST
                    gates(v, LAST, LAST_J, agg_added, 2 * GROUPS * (layer + 1))
                    finish(layer, v, LAST, LAST_J)

            def general():
                def one_tile(layer, k):
                    pe.wait_ge(g_step, G_STEPS * (layer * TILES + k) + 2)
                    nc.tensor.matmul(agg_ps[0][:, 0:P], ones_all[:, :], tile_diag, start=True, stop=True).then_inc(g_product, 1)
                    pe.wait_ge(g_step, G_STEPS * (layer * TILES + k) + 3)
                    pe.wait_ge(g_gathered, 16 * (layer * TILES + k + 1))
                    nc.tensor.matmul(agg_ps[1][:, 0:H], tile_equal, tile_messages, start=True, stop=True).then_inc(g_product, 1)

                def one_chunk(layer, c, j):
                    v = layer * CHUNKS + c
                    pe.wait_ge(g_rows, 16 * (v + 1))
                    wait(pe, g_agg, v)
                    for t in range(j):
                        last = nc.tensor.transpose(agg_ps[0][:, t * P:(t + 1) * P], sum_rows[:, t * H:(t + 1) * H], identity[:, :])
                    last.then_inc(g_turned, 1)
                    gates(v, c, j, g_agg, v + 1)
                    finish(layer, v, c, j)

                for layer in range(LAYERS):
                    one_tile(layer, 0)
                    with pe.Fori(1, TILES) as k:
                        one_tile(layer, k)
                    one_chunk(layer, 0, CHUNK // P)
                    with pe.Fori(1, LAST) as c:
                        one_chunk(layer, c, CHUNK // P)
                    one_chunk(layer, LAST, LAST_J)

            with pe.If(any_outside(pe)):
                general()
            with pe.Else():
                fast()


def kernel(x, src, dst, L0_gnn_enc_w1, L0_gnn_enc_b1, L0_gnn_enc_w2, L0_gnn_enc_b2, L0_gnn_conv_w, L0_gnn_gru_wih,
           L0_gnn_gru_whh, L0_gnn_gru_bih, L0_gnn_gru_bhh, L0_gnn_dec_w1, L0_gnn_dec_b1, L0_gnn_dec_w2, L0_gnn_dec_b2):
    import numpy as np
    import concourse.bacc as bacc
    from concourse.bass_utils import run_bass_kernel_spmd

    def edges(index, filler):
        padded = np.full(GROUPS * GT * P, filler, np.int32)
        padded[:N_EDGES] = np.asarray(index)
        return np.ascontiguousarray(padded.reshape(-1, P).T)

    x_pad = np.zeros((NODES_PAD, H), np.float32)
    x_pad[:N_NODES] = np.asarray(x)
    blocks = [np.asarray(L0_gnn_enc_w1).T, np.asarray(L0_gnn_enc_w2).T, np.asarray(L0_gnn_gru_wih).T,
              np.asarray(L0_gnn_gru_whh).T, np.asarray(L0_gnn_dec_w1).T, np.asarray(L0_gnn_dec_w2).T]
    blocks += [np.asarray(L0_gnn_conv_w)[layer] for layer in range(LAYERS)]
    bias = [np.asarray(v).reshape(-1, H) for v in (L0_gnn_enc_b1, L0_gnn_enc_b2, L0_gnn_gru_bih, L0_gnn_gru_bhh, L0_gnn_dec_b1)]
    arrays = {
        "x": x_pad,
        "src": edges(src, 0),
        "dst": edges(dst, N_NODES),
        "weights": np.ascontiguousarray(np.concatenate(blocks, axis=1)),
        "biases": np.ascontiguousarray(np.concatenate(bias, axis=0).T),
        "dec_b2": np.asarray(L0_gnn_dec_b2).reshape(1, H),
    }
    nc = bacc.Bacc("TRN2", target_bir_lowering=False, num_devices=1)
    aps = [nc.dram_tensor(f"in_{k}", a.shape, mybir.dt.from_np(a.dtype), kind="ExternalInput").ap() for k, a in arrays.items()]
    out = nc.dram_tensor("out", (NODES_PAD, H), F32, kind="ExternalOutput").ap()
    gnn(nc, *aps, out)
    result = run_bass_kernel_spmd(nc, [{f"in_{k}": a for k, a in arrays.items()}], core_ids=[0])
    return result.results[0]["out"][:N_NODES]
```

```python
from contextlib import ExitStack

import concourse.bass as bass
from concourse import mybir

P = 128
F32 = mybir.dt.float32
BF16 = mybir.dt.bfloat16
FP16 = mybir.dt.float16
FP8 = mybir.dt.float8e4
I32 = mybir.dt.int32
ALU = mybir.AluOpType
ACT = mybir.ActivationFunctionType
AX_X = mybir.AxisListType.X

N_NODES = 12500
N_EDGES = 200000
LAYERS = 5
H = 128
EPS = 1e-5

CHUNK = 512
J = CHUNK // P
CHUNKS = -(-N_NODES // CHUNK)
LAST = CHUNKS - 1
LAST_J = -(-(N_NODES - LAST * CHUNK) // P)
NODES_PAD = LAST * CHUNK + LAST_J * P
BLOCKS = NODES_PAD // P

TILES = -(-N_EDGES // P)
GT = 8
GROUPS = -(-TILES // GT)
GROUP_NODES = NODES_PAD // GROUPS
TILE_NODES = GROUP_NODES // GT
MARGIN = 64
TILE_WINDOW = TILE_NODES + 2 * MARGIN
WINDOW = GROUP_NODES + 2 * MARGIN
OLD = WINDOW - GROUP_NODES
STEPS = CHUNK // GROUP_NODES
ITER_TILES = STEPS * GT
TAIL_GROUPS = GROUPS - LAST * STEPS
SLOTS = 4
TILE_COLS = CHUNKS * ITER_TILES
AGG_COLS = (GROUPS - 1) * GROUP_NODES + WINDOW

HALF = 192
STRIP = 2 * HALF
STRIPS = LAST // 2
DENSE = STRIPS * STRIP
DENSE_CHUNKS = DENSE // CHUNK
BURST = DENSE_CHUNKS + STRIPS
SUB = 16
SUBS = HALF // SUB
SUB_TILES = 4
ALL_SUBS = LAST * SUBS
KEYS = BLOCKS * SUB
PIECES = 4
PARTS = STEPS
SPLITS = 3
SQUARES_LIMIT = 256.0
FIRST_COLS = -(-TILE_COLS // P)


def cuts(n, parts):
    return [(n * i + parts - 1) // parts for i in range(parts + 1)]


PIECE_AT = cuts(BLOCKS, PIECES)
PART_AT = cuts(BLOCKS, PARTS)
PART_BLOCKS = max(b - a for a, b in zip(PART_AT, PART_AT[1:]))
PIECE_BLOCKS = max(b - a for a, b in zip(PIECE_AT, PIECE_AT[1:]))

assert GROUP_NODES * GROUPS == NODES_PAD and GROUPS % SLOTS == 0 and STEPS == 2 * SLOTS and TAIL_GROUPS == SLOTS
assert MARGIN + NODES_PAD <= AGG_COLS and MARGIN <= GROUP_NODES and TILE_NODES * GT == GROUP_NODES
assert DENSE_CHUNKS * CHUNK == DENSE and KEYS < 2048 and PIECE_BLOCKS * SUB <= CHUNK and SUBS % 2 == 0
assert STEPS * (LAST - BURST) == LAST

W_ENC1, W_ENC2, W_IH, W_HH, W_DEC1, W_DEC2, W_CONV = 0, 1, 2, 5, 8, 9, 10
W_BLOCKS = W_CONV + LAYERS
B_ENC1, B_ENC2, B_IH, B_HH, B_DEC1 = 0, 1, 2, 5, 8
B_COLS = 9
R, Z, N = 0, 1, 2
DUMP_ROWS = P
G_STEPS = 10
N_LOADS = 7
PREP_LIMITS, PREP_OUTSIDE, PREP_STATS = 9, 14, 25


def tiles_of(c, s):
    return min(GT, TILES - (c * STEPS + s) * GT) if isinstance(c, int) else GT


def wait(engine, semaphore, value):
    if not isinstance(value, int) or value > 0:
        engine.wait_ge(semaphore, value)


class Counts:

    def __init__(self, layer, dense):
        self.layer, self.dense = layer, dense
        self.v = layer * CHUNKS
        skip = DENSE_CHUNKS * STEPS - 1
        self.group = layer * GROUPS - (skip * layer if dense else 0)
        first = DENSE_CHUNKS - 1
        self.iteration = layer * CHUNKS - (first * layer if dense else 0)
        self.half = 2 * layer * CHUNKS - ((2 * first + 1) * layer if dense else 0)

    def gathered(self, c, s):
        slot = s % SLOTS
        total = sum(tiles_of(g // STEPS, g % STEPS) for g in range(slot, GROUPS, SLOTS))
        skipped = GT * len(range(slot, DENSE_CHUNKS * STEPS - 1, SLOTS))
        before = total * self.layer - (skipped * self.layer if self.dense else 0)
        if isinstance(c, int):
            return 16 * (before + min(total, GT * (c * 2 + s // SLOTS + 1)))
        return 16 * (before + GT * (s // SLOTS + 1)) + c * (2 * 16 * GT)


def gnn(nc, x, src, dst, dst_next, firsts, weights, biases, dec_b2, out):
    table = [nc.dram_tensor(f"table{i}", (NODES_PAD, H), F32, kind="Internal").ap() for i in range(2)]
    states = nc.dram_tensor("states", (CHUNKS, P, CHUNK), F32, kind="Internal").ap()
    adjacency = nc.dram_tensor("adjacency", (2 * STRIPS, P, BLOCKS * HALF // 2), BF16, kind="Internal").ap()
    sums = nc.dram_tensor("sums", (NODES_PAD + DUMP_ROWS, H), F32, kind="Internal").ap()

    def chunk_rows(rows, c, j):
        if j == J:
            return rows[0:LAST * CHUNK, :].rearrange("(c j p) f -> c p j f", p=P, j=J)[c, :, :, :]
        return rows[LAST * CHUNK:NODES_PAD, :].rearrange("(j p) f -> p j f", p=P)

    def by_tile(tile, j):
        return tile[:, 0:j * H].rearrange("p (j f) -> p j f", f=H)

    ctx = ExitStack()
    with ctx:
        def sb(name, shape, dt=F32):
            return ctx.enter_context(nc.sbuf_tensor(name, shape, dt))

        def ps(name):
            return ctx.enter_context(nc.psum_tensor(name, [P, CHUNK], F32))

        def sem(name):
            return ctx.enter_context(nc.semaphore(name))

        agg = sb("agg", [P, AGG_COLS])
        x_rows = agg
        w = sb("w", [P, W_BLOCKS * H])
        b = sb("b", [P, B_COLS])
        b_rz = sb("b_rz", [P, 2])
        b2_row = sb("b2_row", [1, H])
        b2_all = sb("b2_all", [P, H])
        ones_all = sb("ones_all", [P, P])
        no_selection = sb("no_selection", [P, WINDOW])
        identity = sb("identity", [P, P])
        src_all = sb("src_all", [P, TILE_COLS], I32)
        dst_rel = sb("dst_rel", [P, TILE_COLS])
        cols_i = sb("cols_i", [P, TILE_WINDOW], I32)
        cols_f = sb("cols_f", [P, TILE_WINDOW])
        outside = sb("outside", [P, 2])
        irregular = sb("irregular", [P, 3])
        n_outside = sb("n_outside", [1, 1], I32)
        n_irregular = sb("n_irregular", [1, 1], I32)
        src_stage = sb("src_stage", [P, ITER_TILES], I32)
        dst_stage = sb("dst_stage", [P, ITER_TILES])
        messages = sb("messages", [P, SLOTS, GT, H])
        selection = sb("selection", [P, 2, GT, TILE_WINDOW])
        h_old = [sb("h_old0", [P, CHUNK]), sb("h_old1", [P, CHUNK])]
        gate_r = sb("gate_r", [P, CHUNK])
        gate_z = sb("gate_z", [P, CHUNK])
        pre_n = sb("pre_n", [P, CHUNK])
        gate_n = sb("gate_n", [P, CHUNK])
        diff = sb("diff", [P, CHUNK])
        h_new = sb("h_new", [P, CHUNK])
        table_stage = sb("table_stage", [P, CHUNK])
        x_stage = sb("x_stage", [P, CHUNK])
        relu_h, decT, out_stage = gate_r, diff, table_stage
        m_in = [table_stage, x_stage]
        mean = sb("mean", [P, BLOCKS])
        rstd = sb("rstd", [P, BLOCKS])
        ln_a = sb("ln_a", [P, BLOCKS])
        ln_b = sb("ln_b", [P, BLOCKS])
        x_norm, xT, encT = gate_r, gate_z, gate_n
        strip_part = sb("strip_part", [P, 2, 2, PART_BLOCKS * HALF], FP8)
        m_parts = sb("m_parts", [P, BLOCKS * SPLITS * H], BF16)
        parts = m_parts[:, :].rearrange("p (k i f) -> p k i f", i=SPLITS, f=H)
        taken = [0]

        def carve(elements, dt, size):
            at = taken[0]
            taken[0] += (elements * size + 3) // 4 * 2
            assert taken[0] <= BLOCKS * SPLITS * H
            piece = m_parts[:, at:at + elements * size // 2]
            return piece if dt is BF16 else piece.bitcast(dt)

        edge_info = carve(TILE_COLS * 3, F32, 4)
        half_adj = carve(BLOCKS * HALF, FP8, 1)
        key_hot = carve(2 * SUB_TILES * KEYS, BF16, 2).rearrange("p (q t k) -> p q t k", q=2, t=SUB_TILES)
        low_hot = carve(2 * SUB_TILES * P, BF16, 2).rearrange("p (q t k) -> p q t k", q=2, t=SUB_TILES)
        key_cols = carve(KEYS, FP16, 2)
        dst_next_all = key_hot[:, 0, :, :].rearrange("p t k -> p (t k)")[:, 0:2 * TILE_COLS].bitcast(I32)
        info = edge_info.rearrange("p (k i) -> p k i", i=3)
        picked = sb("picked", [P, SUBS * SUB_TILES * 3])
        picked_v = picked[:, :].rearrange("p (q t i) -> p (q t) i", t=SUB_TILES, i=3)
        sub_u = sb("sub_u", [P, SUBS * SUB_TILES])
        sub_in = sb("sub_in", [P, SUBS * SUB_TILES])
        sub_key = sb("sub_key", [P, SUBS * SUB_TILES])
        sub_base_i = sb("sub_base_i", [P, SUBS * SUB_TILES], I32)
        sub_base = sb("sub_base", [P, SUBS * SUB_TILES])
        half_base_i = sb("half_base_i", [P, 2 * STRIPS], I32)
        half_base = sb("half_base", [P, 2 * STRIPS])
        squares = sb("squares", [P, PARTS])
        squares_max = sb("squares_max", [P, PARTS])
        first_i = sb("first_i", [P, FIRST_COLS], I32)
        first_f = sb("first_f", [P, FIRST_COLS])
        start_i = sb("start_i", [1, ALL_SUBS + 1], I32)
        room = messages[:, :, :, :].rearrange("p a t f -> p (a t f)")
        base_i = room[:, 0:TILE_COLS].bitcast(I32)
        base_f = room[:, TILE_COLS:2 * TILE_COLS]
        limits = room[:, 2 * TILE_COLS:2 * TILE_COLS + ALL_SUBS + 1]
        limits_i = gate_r[:, 0:ALL_SUBS + 1].bitcast(I32)
        tmp_i = selection[:, :, :, :].rearrange("p a t f -> p (a t f)")[:, 0:TILE_COLS].bitcast(I32)
        before_limit = [pre_n[:, 0:ALL_SUBS + 1], diff[:, 0:ALL_SUBS + 1]]
        key_cols_i = h_old[0][:, :]
        dst_all = strip_part[:, :, :, :].rearrange("p a h k -> p (a h k)")[:, 0:4 * TILE_COLS].bitcast(I32)
        stats = half_adj[:, 0:BLOCKS * 6 * 4].bitcast(F32).rearrange("p (k s) -> p k s", s=6)
        start_f = gate_z[0:1, 0:ALL_SUBS + 1]
        start_of = gate_n[0:1, 0:ALL_SUBS + 1]
        lower = sb("lower", [P, P])
        dump_i = sb("dump_i", [P, 1], I32)
        dump = sb("dump", [P, 1])
        tile_src = sb("tile_src", [P, 1], I32)
        tile_dst = sb("tile_dst", [P, 1])
        tile_row = sb("tile_row", [P, 1])
        tile_dup = sb("tile_dup", [P, 1])
        tile_index = sb("tile_index", [P, 1], I32)
        tile_diag = selection[:, 0, 0, 0:P]
        tile_equal = selection[:, 0, 1, 0:P]
        tile_before = selection[:, 0, 2, 0:P]
        tile_messages = messages[:, 0, 0, :]
        tile_sums = messages[:, 0, 1, :]
        sum_rows = messages[:, 1, 0:J, :].rearrange("p t f -> p (t f)")

        agg_ps = [ps("agg_ps0"), ps("agg_ps1")]
        r_ps, z_ps, hn_ps, in_ps = ps("r_ps"), ps("z_ps"), ps("hn_ps"), ps("in_ps")
        table_ps, dec_ps = ps("table_ps"), ps("dec_ps")
        tr_ps, enc1_ps, enc2_ps = r_ps, z_ps, hn_ps
        strip_ps = in_ps
        build_ps = [dec_ps, in_ps]

        loaded = sem("loaded")
        x_loaded = sem("x_loaded")
        consts = sem("consts")
        key_iota = sem("key_iota")
        key_taken = sem("key_taken")
        prep = sem("prep")
        hot_limits = sem("hot_limits")
        limit_sum = sem("limit_sum")
        prep_sum = sem("prep_sum")
        n_ready = sem("n_ready")
        ln_std = sem("ln_std")
        normed = sem("normed")
        transposed = sem("transposed")
        xT_ready = sem("xT_ready")
        enc1_done = sem("enc1_done")
        encT_ready = sem("encT_ready")
        enc2_done = sem("enc2_done")
        h0_ready = sem("h0_ready")
        src_staged = sem("src_staged")
        turns = [sem(f"{name}_turns") for name in ("pool", "act", "pe", "sp")]
        gathered = [sem(f"gathered{i}") for i in range(SLOTS)]
        dst_staged = sem("dst_staged")
        selected = sem("selected")
        summed = sem("summed")
        agg_added = sem("agg_added")
        h_loaded = [sem("h_loaded0"), sem("h_loaded1")]
        gates_ps = sem("gates_ps")
        gates_rz = sem("gates_rz")
        cand = sem("cand")
        gru = sem("gru")
        state_stored = sem("state_stored")
        table_sum = sem("table_sum")
        table_out = sem("table_out")
        table_stored = sem("table_stored")
        subs_picked = sem("subs_picked")
        hot = sem("hot")
        built = sem("built")
        adj_out = sem("adj_out")
        adj_squared = sem("adj_squared")
        squares_used = sem("squares_used")
        adj_stored = sem("adj_stored")
        regular_sum = sem("regular_sum")
        regular_ready = sem("regular_ready")
        m_loaded = [sem("m_loaded0"), sem("m_loaded1")]
        split_act = sem("split_act")
        split_dve = sem("split_dve")
        part_loaded = [sem("part_loaded0"), sem("part_loaded1")]
        part_used = sem("part_used")
        strip_out = sem("strip_out")
        relu_ready = sem("relu_ready")
        dec1_done = sem("dec1_done")
        decT_ready = sem("decT_ready")
        dec2_done = sem("dec2_done")
        dec_biased = sem("dec_biased")
        dec_sig = sem("dec_sig")
        x_again = sem("x_again")
        out_ready = sem("out_ready")
        out_stored = sem("out_stored")
        g_zeros = sem("g_zeros")
        g_cleared = sem("g_cleared")
        g_src = sem("g_src")
        g_gathered = sem("g_gathered")
        g_step = sem("g_step")
        g_product = sem("g_product")
        g_scattered = sem("g_scattered")
        g_rows = sem("g_rows")
        g_turned = sem("g_turned")
        g_agg = sem("g_agg")

        block = ctx.enter_context(nc.Block())

        def wblock(k):
            return w[:, k * H:(k + 1) * H]

        def choose(engine, general, gathering, dense):
            engine.wait_ge(n_ready, 1)
            with engine.If(engine.value_load(n_outside[0:1, 0:1], min_val=0, max_val=2 * P) > 0):
                general()
            with engine.Else():
                gathering(Counts(0, False), True)
                engine.wait_ge(regular_ready, 1)
                with engine.If(engine.value_load(n_irregular[0:1, 0:1], min_val=0, max_val=3 * P) > 0):
                    for layer in range(1, LAYERS):
                        gathering(Counts(layer, False), False)
                with engine.Else():
                    for layer in range(1, LAYERS):
                        dense(Counts(layer, True))

        def old_state(k, c, paired):
            if not paired:
                return 0, 16 * (k.v + c + 1)
            evens, odds = (CHUNKS + 1) // 2, CHUNKS // 2
            return (c % 2, 16 * ((CHUNKS + (k.layer - 1) * evens if c % 2 == 0 else (k.layer - 1) * odds) + c // 2 + 1))

        @block.sync
        def _(sp):
            sp.dma_start(x_rows[:, 0:NODES_PAD].rearrange("p (k f) -> p k f", f=H),
                         x.rearrange("(k p) f -> p k f", p=P)).then_inc(x_loaded, 16)

            def store_state(u, c, j, ready, count):
                sp.wait_ge(ready, count)
                sp.dma_start(states[c, :, 0:j * P], h_new[:, 0:j * P]).then_inc(state_stored, 16)

            def store_table(t, u, c, j):
                sp.wait_ge(table_out, u + 1)
                sp.dma_start(chunk_rows(table[t], c, j), by_tile(table_stage, j)).then_inc(table_stored, 16)

            def store_out(c, j):
                wait(sp, out_ready, c)
                sp.dma_start(by_tile(x_stage, j), chunk_rows(x, c, j)).then_inc(x_again, 16)
                sp.wait_ge(out_ready, c + 1)
                sp.dma_start(chunk_rows(out, c, j), by_tile(out_stage, j)).then_inc(out_stored, 16)

            def encoded(c, j):
                store_state(c, c, j, h0_ready, c + 1)
                store_table(0, c, c, j)

            with sp.Fori(0, LAST) as c:
                encoded(c, J)
            encoded(LAST, LAST_J)

            def load_old(v, c, j, buffer, used):
                wait(sp, gru, 5 * (v - used) + 3)
                sp.dma_start(h_old[buffer][:, 0:j * P], states[c, :, 0:j * P]).then_inc(h_loaded[buffer], 16)

            def finish(layer, v, c, j):
                if layer < LAYERS - 1:
                    store_state(v + CHUNKS, c, j, gru, 5 * v + 5)
                    store_table((layer + 1) % 2, v + CHUNKS, c, j)
                else:
                    store_out(c, j)

            def gathering(k, build):
                def iteration(c):
                    if not (isinstance(c, int) and c == 0):
                        if isinstance(c, int) and c == 1:
                            load_first(k)
                        else:
                            load_old(c - 1 + k.v, c - 1, J, 0, 1)
                        finish(k.layer, c - 1 + k.v, c - 1, J)
                    if build:
                        sp.wait_ge(adj_out, (c + 1) * (SUBS * PIECES))
                        sp.dma_start(adjacency[c, :, :], half_adj.bitcast(BF16)).then_inc(adj_stored, 16)

                def load_first(k):
                    sp.dma_start(h_old[0][:, :], states[0, :, :]).then_inc(h_loaded[0], 16)

                sp.wait_ge(state_stored, 16 * CHUNKS * (k.layer + 1))
                iteration(0)
                iteration(1)
                with sp.Fori(2, LAST) as c:
                    iteration(c)
                load_old(k.v + LAST - 1, LAST - 1, J, 0, 1)
                finish(k.layer, k.v + LAST - 1, LAST - 1, J)
                load_old(k.v + LAST, LAST, LAST_J, 0, 1)
                finish(k.layer, k.v + LAST, LAST, LAST_J)

            def dense(k):
                def load_part(i, p):
                    wait(sp, part_used, (k.layer - 1) * STRIPS * PARTS + i * PARTS + (p - 1))
                    a, e = PART_AT[p], PART_AT[p + 1]
                    rows = adjacency.rearrange("(i h) p e -> i p h e", h=2)[i, :, :, a * HALF // 2:e * HALF // 2]
                    sp.dma_start(strip_part[:, p % 2, :, 0:(e - a) * HALF].bitcast(BF16), rows).then_inc(part_loaded[p % 2], 16)

                def load_rows(c, j):
                    n = (k.layer - 1) * CHUNKS + c
                    if c >= 2:
                        sp.wait_ge(split_dve, 2 * (n - 2) + 1)
                    sp.dma_start(by_tile(m_in[c % 2], j), chunk_rows(table[k.layer % 2], c, j)).then_inc(m_loaded[c % 2], 16)

                sp.wait_ge(table_stored, 16 * CHUNKS * (k.layer + 1))
                sp.wait_ge(state_stored, 16 * CHUNKS * (k.layer + 1))
                sp.wait_ge(adj_stored, 16 * LAST)
                load_part(0, 0)
                load_part(0, 1)
                rows = list(range(CHUNKS))
                each = -(-CHUNKS // (PARTS - 1))
                for p in range(2, PARTS + 1):
                    for c in rows[(p - 2) * each:(p - 1) * each]:
                        load_rows(c, J if c < LAST else LAST_J)
                    if p < PARTS:
                        load_part(0, p)
                with sp.Fori(1, STRIPS) as i:
                    for p in range(PARTS):
                        load_part(i, p)
                v = k.v
                load_old(v, 0, J, 0, 1)
                load_old(v + 1, 1, J, 1, 2)
                with sp.Fori(0, (LAST - 2) // 2) as i:
                    for odd in range(2):
                        c = i * 2 + odd
                        finish(k.layer, c + v, c, J)
                        load_old(c + (v + 2), c + 2, J, odd, 2)
                finish(k.layer, v + LAST - 2, LAST - 2, J)
                load_old(v + LAST, LAST, LAST_J, 0, 2)
                finish(k.layer, v + LAST - 1, LAST - 1, J)
                finish(k.layer, v + LAST, LAST, LAST_J)

            def general():
                def one_chunk(layer, c, j):
                    v = c + layer * CHUNKS
                    wait(sp, gru, 5 * (v - 1) + 3)
                    sp.sem_inc(turns[3], 1)
                    wait(sp, g_turned, v)
                    sp.dma_start(h_old[0][:, 0:j * P], states[c, :, 0:j * P]).then_inc(h_loaded[0], 16)
                    sp.dma_start(by_tile(sum_rows, j), chunk_rows(sums[0:NODES_PAD, :], c, j)).then_inc(g_rows, 16)
                    finish(layer, v, c, j)

                for layer in range(LAYERS):
                    sp.wait_ge(state_stored, 16 * CHUNKS * (layer + 1))
                    sp.wait_ge(g_zeros, layer + 1)
                    sp.dma_start(sums.rearrange("(p r) f -> p (r f)", p=P), agg[:, 0:NODES_PAD + DUMP_ROWS]).then_inc(g_cleared, 16)
                    sp.wait_ge(g_scattered, 16 * TILES * (layer + 1))
                    one_chunk(layer, 0, J)
                    with sp.Fori(1, LAST) as c:
                        one_chunk(layer, c, J)
                    one_chunk(layer, LAST, LAST_J)

            choose(sp, general, gathering, dense)
            sp.wait_ge(out_stored, 16 * CHUNKS)

        @block.gpsimd
        def _(pool):
            n_consts = [0]

            def const(instruction):
                n_consts[0] += 1
                instruction.then_inc(consts, 1)

            const(nc.gpsimd.iota(base_i, pattern=[[TILE_NODES, TILE_COLS]], base=-MARGIN, channel_multiplier=0))
            const(nc.gpsimd.iota(limits_i, pattern=[[SUB, ALL_SUBS + 1]], base=0, channel_multiplier=0))
            const(nc.gpsimd.iota(cols_i[:, :], pattern=[[1, TILE_WINDOW]], base=0, channel_multiplier=0))
            const(nc.gpsimd.iota(sub_base_i[:, :], pattern=[[SUB, SUBS], [0, SUB_TILES]], base=0, channel_multiplier=0))
            const(nc.gpsimd.iota(half_base_i[:, :], pattern=[[HALF, 2 * STRIPS]], base=0, channel_multiplier=0))
            const(nc.gpsimd.iota(dump_i[:, :], pattern=[[0, 1]], base=NODES_PAD, channel_multiplier=1))
            const(nc.gpsimd.memset(ones_all[:, :], 1.0))
            const(nc.gpsimd.memset(no_selection[:, :], 0.0))
            const(nc.gpsimd.memset(identity[:, :], 0.0))
            const(nc.gpsimd.memset(lower[:, :], 1.0))
            pool.wait_ge(consts, n_consts[0])
            const(nc.gpsimd.affine_select(out=identity[:, :], in_=identity[:, :], compare_op=ALU.not_equal, fill=1.0,
                                          base=0, pattern=[[-1, P]], channel_multiplier=1))
            const(nc.gpsimd.affine_select(out=lower[:, :], in_=lower[:, :], compare_op=ALU.is_gt, fill=0.0,
                                          base=0, pattern=[[-1, P]], channel_multiplier=1))
            assert n_consts[0] == N_CONSTS
            for at in range(0, KEYS, CHUNK):
                n = min(CHUNK, KEYS - at)
                wait(pool, key_taken, at // CHUNK)
                nc.gpsimd.iota(key_cols_i[:, 0:n].bitcast(I32), pattern=[[1, n]], base=at + 1, channel_multiplier=0).then_inc(key_iota, 1)

            def gather_half(k, c, half, steps):
                n = SLOTS * GT
                at = half * n
                nc.gpsimd.tensor_copy(src_stage[:, at:at + n], src_all[:, bass.ds(c * ITER_TILES + at, n)]).then_inc(src_staged, 1)
                pool.wait_ge(src_staged, c * 2 + (k.half + half + 1))
                pool.sem_inc(turns[0], 1)
                for s in steps:
                    slot = s % SLOTS
                    wait(pool, summed, c * STEPS + (k.group + s - SLOTS + 1))
                    pool.sem_inc(turns[0], 1)
                    for t in range(tiles_of(c, s)):
                        at = s * GT + t
                        nc.gpsimd.indirect_dma_start(
                            messages[:, slot, t, :], None, table[k.layer % 2],
                            bass.IndirectOffsetOnAxis(ap=src_stage[:, at:at + 1], axis=0)).then_inc(gathered[slot], 16)

            def both_halves(k, c):
                gather_half(k, c, 0, range(SLOTS))
                gather_half(k, c, 1, range(SLOTS, STEPS))

            def tail(k):
                gather_half(k, LAST, 0, range(TAIL_GROUPS))
                pool.sem_inc(src_staged, 1)

            def gathering(k, build):
                pool.wait_ge(table_stored, 16 * CHUNKS * (k.layer + 1))
                both_halves(k, 0)
                with pool.Fori(1, LAST) as c:
                    both_halves(k, c)
                tail(k)

            def dense(k):
                pool.wait_ge(table_stored, 16 * CHUNKS * (k.layer + 1))
                gather_half(k, DENSE_CHUNKS - 1, 1, [STEPS - 1])
                with pool.Fori(DENSE_CHUNKS, LAST) as c:
                    both_halves(k, c)
                tail(k)

            def general():
                def one_tile(layer, t):
                    wait(pool, g_scattered, 16 * (layer * TILES + t))
                    pool.sem_inc(turns[0], 1)
                    nc.gpsimd.tensor_copy(tile_src[:, :], src_all[:, bass.ds(t, 1)]).then_inc(g_src, 1)
                    pool.wait_ge(g_src, layer * TILES + t + 1)
                    pool.sem_inc(turns[0], 1)
                    nc.gpsimd.indirect_dma_start(tile_messages, None, table[layer % 2],
                                                 bass.IndirectOffsetOnAxis(ap=tile_src[:, 0:1], axis=0)).then_inc(g_gathered, 16)
                    pool.wait_ge(g_step, G_STEPS * (layer * TILES + t + 1))
                    pool.sem_inc(turns[0], 1)
                    nc.gpsimd.indirect_dma_start(sums, bass.IndirectOffsetOnAxis(ap=tile_index[:, 0:1], axis=0),
                                                 tile_sums, None, compute_op=ALU.add).then_inc(g_scattered, 16)

                for layer in range(LAYERS):
                    pool.wait_ge(table_stored, 16 * CHUNKS * (layer + 1))
                    pool.wait_ge(g_cleared, 16 * (layer + 1))
                    one_tile(layer, 0)
                    with pool.Fori(1, TILES) as t:
                        one_tile(layer, t)

            pool.wait_ge(loaded, 16 * N_LOADS)
            choose(pool, general, gathering, dense)

        def loads_of(k, c, odd):
            per = CHUNKS // 2 if odd else (CHUNKS + 1) // 2
            if isinstance(c, int):
                return 16 * ((k.layer - 1) * per + c // 2 + 1)
            return c * 8 + (16 * ((k.layer - 1) * per + 1) - 8 * odd)

        @block.scalar
        def _(act):
            for to, of in ((dst_all, dst), (dst_next_all, dst_next), (first_i[:, :], firsts), (src_all[:, :], src),
                           (w[:, :], weights), (b[:, :], biases), (b2_row[:, :], dec_b2)):
                act.dma_start(to, of).then_inc(loaded, 16)
            act.wait_ge(prep, PREP_STATS)
            nc.scalar.activation(ln_b[:, :], ln_b[:, :], ACT.Sqrt).then_inc(ln_std, 1)
            act.wait_ge(loaded, 16 * N_LOADS)

            def encode(c, j):
                n = j * P
                act.wait_ge(transposed, c + 1)
                wait(act, enc1_done, c)
                nc.scalar.activation(xT[:, 0:n], tr_ps[:, 0:n], ACT.Relu).then_inc(xT_ready, 1)
                act.wait_ge(enc1_done, c + 1)
                wait(act, enc2_done, c)
                nc.scalar.activation(encT[:, 0:n], enc1_ps[:, 0:n], ACT.Relu,
                                     bias=b[:, B_ENC1:B_ENC1 + 1]).then_inc(encT_ready, 1)
                act.wait_ge(enc2_done, c + 1)
                wait(act, table_sum, c)
                wait(act, state_stored, c * 16)
                nc.scalar.activation(h_new[:, 0:n], enc2_ps[:, 0:n], ACT.Identity,
                                     bias=b[:, B_ENC2:B_ENC2 + 1]).then_inc(h0_ready, 1)

            with act.Fori(0, LAST) as c:
                encode(c, J)
            encode(LAST, LAST_J)

            def gates(v, j):
                n = j * P
                act.wait_ge(gates_ps, 4 * v + 1)
                wait(act, gru, 5 * v)
                nc.scalar.activation(gate_r[:, 0:n], r_ps[:, 0:n], ACT.Sigmoid, bias=b_rz[:, R:R + 1]).then_inc(gates_rz, 1)
                act.wait_ge(gates_ps, 4 * v + 2)
                nc.scalar.activation(gate_z[:, 0:n], z_ps[:, 0:n], ACT.Sigmoid, bias=b_rz[:, Z:Z + 1]).then_inc(gates_rz, 1)

            def candidate(v, j):
                n = j * P
                act.wait_ge(gru, 5 * v + 2)
                nc.scalar.activation(gate_n[:, 0:n], pre_n[:, 0:n], ACT.Tanh, bias=b[:, B_IH + N:B_IH + N + 1]).then_inc(cand, 1)

            def make_table(v, c, j):
                n = j * P
                act.wait_ge(table_sum, v + (CHUNKS + 1))
                act.wait_ge(table_stored, 16 * (v + CHUNKS))
                nc.scalar.activation(table_stage[:, 0:n], table_ps[:, 0:n], ACT.Copy).then_inc(table_out, 1)

            def decode(v, c, j):
                n = j * P
                act.wait_ge(gru, 5 * v + 5)
                wait(act, dec1_done, c)
                nc.scalar.activation(relu_h[:, 0:n], h_new[:, 0:n], ACT.Relu).then_inc(relu_ready, 1)
                act.wait_ge(dec1_done, c + 1)
                wait(act, dec2_done, c)
                nc.scalar.activation(decT[:, 0:n], table_ps[:, 0:n], ACT.Relu, bias=b[:, B_DEC1:B_DEC1 + 1]).then_inc(decT_ready, 1)
                act.wait_ge(dec_biased, c + 1)
                nc.scalar.activation(out_stage[:, 0:n], out_stage[:, 0:n], ACT.Sigmoid).then_inc(dec_sig, 1)

            def chunk(layer, v, c, j):
                gates(v, j)
                candidate(v, j)
                (make_table if layer < LAYERS - 1 else decode)(v, c, j)

            def all_chunks(layer):
                v = layer * CHUNKS
                with act.Fori(0, LAST) as c:
                    chunk(layer, c + v, c, J)
                chunk(layer, v + LAST, LAST, LAST_J)

            def count_edges(c, q):
                for i in range(PIECES):
                    n = (c * SUBS + q) * PIECES + i
                    a, e = PIECE_AT[i], PIECE_AT[i + 1]
                    act.wait_ge(built, n + 1)
                    act.sem_inc(turns[1], 1)
                    to = half_adj.rearrange("p (k d) -> p k d", d=HALF)[:, a:e, q * SUB:(q + 1) * SUB]
                    nc.scalar.activation(to, build_ps[i % 2][:, 0:(e - a) * SUB].rearrange("p (k d) -> p k d", d=SUB),
                                         ACT.Copy, saturate=False).then_inc(adj_out, 1)

            def square(c):
                act.wait_ge(adj_out, (c + 1) * (SUBS * PIECES))
                wait(act, squares_used, c)
                for i in range(PARTS):
                    a, e = PART_AT[i], PART_AT[i + 1]
                    wait(act, adj_squared, c * PARTS + i)
                    act.sem_inc(turns[1], 1)
                    junk = strip_part[:, 0, :, :].rearrange("p h k -> p (h k)")[:, 0:2 * (e - a) * HALF].bitcast(BF16)
                    nc.scalar.activation(junk, half_adj[:, a * HALF:e * HALF], ACT.Square,
                                         accum_out=squares[:, i:i + 1]).then_inc(adj_squared, 1)

            def gathering(k, build):
                if not build:
                    all_chunks(k.layer)
                    return

                def iteration(c):
                    if not (isinstance(c, int) and c == 0):
                        act.wait_ge(adj_stored, c * 16)
                        act.wait_ge(adj_squared, c * PARTS)
                        act.sem_inc(turns[1], 1)
                    q = 0
                    for s in range(STEPS):
                        for _ in range(1 + s % 2):
                            count_edges(c, q)
                            q += 1
                        if s == 1 and not (isinstance(c, int) and c == 0):
                            gates(c - 1 + k.v, J)
                        if s == 2 and not (isinstance(c, int) and c == 0):
                            candidate(c - 1 + k.v, J)
                        if s == 4 and not (isinstance(c, int) and c == 0):
                            make_table(c - 1 + k.v, c - 1, J)
                    square(c)

                iteration(0)
                with act.Fori(1, LAST) as c:
                    iteration(c)
                for c, j in ((LAST - 1, J), (LAST, LAST_J)):
                    chunk(k.layer, k.v + c, c, j)

            def dense(k):
                def split(n, c, odd, j):
                    rows = bass.ds(c * J, j)
                    act.wait_ge(m_loaded[odd], loads_of(k, c, odd))
                    wait(act, part_used, (k.layer - 1) * STRIPS * PARTS)
                    nc.scalar.activation(parts[:, rows, 0, :], by_tile(m_in[odd], j), ACT.Copy).then_inc(split_act, 1)
                    act.wait_ge(split_dve, 2 * n + 1)
                    nc.scalar.activation(parts[:, rows, 1, :], by_tile(diff, j), ACT.Copy).then_inc(split_act, 1)

                n = (k.layer - 1) * CHUNKS
                with act.Fori(0, LAST // 2) as i:
                    split(i * 2 + n, i * 2, 0, J)
                    split(i * 2 + (n + 1), i * 2 + 1, 1, J)
                split(n + LAST, LAST, 0, LAST_J)
                with act.Fori(0, STRIPS) as i:
                    act.wait_ge(part_used, (i + ((k.layer - 1) * STRIPS + 1)) * PARTS)
                    nc.scalar.activation(agg[:, bass.ds(i * STRIP + MARGIN, STRIP)], strip_ps[:, 0:STRIP], ACT.Copy).then_inc(strip_out, 1)
                all_chunks(k.layer)

            def general():
                for layer in range(LAYERS):
                    all_chunks(layer)

            choose(act, general, gathering, dense)

        @block.vector
        def _(dve):
            n_prep = [0]

            def done(instruction):
                n_prep[0] += 1
                instruction.then_inc(prep, 1)
                dve.wait_ge(prep, n_prep[0])

            dve.wait_ge(loaded, 16 * N_LOADS)
            dve.wait_ge(consts, N_CONSTS)
            ops = nc.vector
            done(ops.tensor_tensor(b_rz[:, :], b[:, B_IH:B_IH + 2], b[:, B_HH:B_HH + 2], ALU.add))
            done(ops.tensor_copy(cols_f[:, :], cols_i[:, :]))
            done(ops.tensor_copy(dump[:, :], dump_i[:, :]))
            done(ops.tensor_copy(sub_base[:, :], sub_base_i[:, :]))
            done(ops.tensor_copy(half_base[:, :], half_base_i[:, :]))
            done(ops.tensor_copy(base_f, base_i))
            done(ops.tensor_copy(info[:, :, 0], dst_all))
            done(ops.tensor_copy(first_f[:, :], first_i[:, :]))
            done(ops.tensor_copy(limits, limits_i))
            assert n_prep[0] == PREP_LIMITS
            for i in range(FIRST_COLS):
                wait(dve, limit_sum, i - 1)
                ops.tensor_scalar(before_limit[i % 2], limits, first_f[:, i:i + 1], None, ALU.is_gt).then_inc(hot_limits, 1)
            done(ops.tensor_tensor(dst_rel[:, :], info[:, :, 0], base_f, ALU.subtract))
            done(ops.tensor_reduce(outside[:, 0:1], dst_rel[:, 0:TILES], AX_X, ALU.min))
            done(ops.tensor_reduce(outside[:, 1:2], dst_rel[:, 0:TILES], AX_X, ALU.max))
            done(ops.tensor_scalar(outside[:, 0:1], outside[:, 0:1], 0.0, None, ALU.is_lt))
            done(ops.tensor_scalar(outside[:, 1:2], outside[:, 1:2], float(TILE_WINDOW - 1), None, ALU.is_gt))
            assert n_prep[0] == PREP_OUTSIDE
            dve.wait_ge(prep_sum, 1)
            ops.tensor_copy(n_outside[:, :], table_ps[0:1, 0:1]).then_inc(n_ready, 1)
            dve.wait_ge(prep_sum, 2)
            done(ops.tensor_copy(b2_all[:, :], dec_ps[:, 0:H]))
            done(ops.tensor_tensor(base_f, info[:, :, 0], dst_next_all, ALU.is_gt))
            done(ops.tensor_reduce(irregular[:, 0:1], base_f, AX_X, ALU.max))

            dve.wait_ge(x_loaded, 16)

            def stats_of(c, j):
                for t in range(j):
                    last = ops.bn_stats(stats[:, bass.ds(c * J + t, 1), :].rearrange("p a s -> p (a s)"),
                                        x_rows[:, bass.ds(c * CHUNK + t * H, H)])
                return last

            with dve.Fori(0, LAST) as c:
                stats_of(c, J)
            done(stats_of(LAST, LAST_J))
            m_even, m_odd, v_even, v_odd = (stats[:, :, i] for i in (1, 4, 2, 5))
            done(ops.tensor_tensor(ln_a[:, :], m_even, m_odd, ALU.subtract))
            done(ops.tensor_tensor(mean[:, :], m_even, m_odd, ALU.add))
            done(ops.tensor_scalar(mean[:, :], mean[:, :], 0.5, None, ALU.mult))
            done(ops.tensor_tensor(ln_a[:, :], ln_a[:, :], ln_a[:, :], ALU.mult))
            done(ops.tensor_tensor(ln_b[:, :], v_even, v_odd, ALU.add))
            done(ops.tensor_scalar(ln_b[:, :], ln_b[:, :], 1.0 / H, EPS, ALU.mult, ALU.add))
            done(ops.scalar_tensor_tensor(out=ln_b[:, :], in0=ln_a[:, :], scalar=0.25, in1=ln_b[:, :],
                                          op0=ALU.mult, op1=ALU.add))
            assert n_prep[0] == PREP_STATS
            dve.wait_ge(ln_std, 1)
            done(ops.reciprocal(rstd[:, :], ln_b[:, :]))

            def encode(c, j):
                wait(dve, transposed, c)
                for t in range(j):
                    at = c * J + t
                    one = bass.ds(at, 1)
                    last = ops.tensor_scalar(x_norm[:, t * H:(t + 1) * H], x_rows[:, bass.ds(at * H, H)],
                                             mean[:, one], rstd[:, one], ALU.subtract, ALU.mult)
                last.then_inc(normed, 1)

            def first_table(c, j):
                n = j * P
                dve.wait_ge(table_sum, c + 1)
                wait(dve, table_stored, c * 16)
                ops.tensor_copy(table_stage[:, 0:n], table_ps[:, 0:n]).then_inc(table_out, 1)

            encode(0, J)
            with dve.Fori(0, LAST - 1) as c:
                encode(c + 1, J)
                first_table(c, J)
            encode(LAST, LAST_J)
            first_table(LAST - 1, J)
            first_table(LAST, LAST_J)

            for i, at in enumerate(range(0, KEYS, CHUNK)):
                n = min(CHUNK, KEYS - at)
                dve.wait_ge(key_iota, i + 1)
                ops.tensor_copy(key_cols[:, at:at + n], key_cols_i[:, 0:n].bitcast(I32)).then_inc(key_taken, 1)
            done(ops.tensor_scalar(tmp_i, src_all[:, :], 7, None, ALU.arith_shift_right))
            done(ops.tensor_scalar(info[:, :, 1], tmp_i, float(SUB), 1.0, ALU.mult, ALU.add))
            done(ops.tensor_scalar(tmp_i, src_all[:, :], P - 1, None, ALU.bitwise_and))
            done(ops.tensor_copy(info[:, :, 2], tmp_i))
            dve.wait_ge(prep_sum, 3)
            done(ops.tensor_copy(start_f, agg_ps[0][0:1, 0:ALL_SUBS + 1]))
            done(ops.tensor_scalar(start_of, start_f, -1.0, 0.0, ALU.add, ALU.max))
            done(ops.tensor_copy(start_i[:, :], start_of))
            done(ops.memset(irregular[:, 1:3], 0.0))
            done(ops.tensor_tensor(start_f[0:1, 0:ALL_SUBS], start_f[0:1, 1:ALL_SUBS + 1], start_of[0:1, 0:ALL_SUBS], ALU.subtract))
            done(ops.tensor_reduce(irregular[0:1, 1:2], start_f[0:1, 0:ALL_SUBS], AX_X, ALU.max))
            done(ops.tensor_scalar(irregular[0:1, 1:2], irregular[0:1, 1:2], float(SUB_TILES), None, ALU.is_gt))
            done(ops.memset(squares_max[:, :], 0.0))

            def stage(k, c):
                wait(dve, selected, c * STEPS + k.group)
                ops.tensor_copy(dst_stage[:, :], dst_rel[:, bass.ds(c * ITER_TILES, ITER_TILES)]).then_inc(dst_staged, 1)
                dve.wait_ge(dst_staged, c + (k.iteration + 1))

            def select(k, c, s):
                wait(dve, summed, c * STEPS + (k.group + s - 1))
                for t in range(tiles_of(c, s)):
                    at = s * GT + t
                    last = ops.tensor_scalar(selection[:, s % 2, t, :], cols_f[:, :], dst_stage[:, at:at + 1], None,
                                             ALU.is_equal)
                last.then_inc(selected, 1)

            def select_next(k, c, s, end):
                if s + 1 < STEPS:
                    if not (isinstance(c, int) and c == LAST and s + 1 >= end):
                        select(k, c, s + 1)
                else:
                    stage(k, c + 1)
                    select(k, c + 1, 0)

            def add(k, c, s, first=False):
                at = c * CHUNK + s * GROUP_NODES
                g = c * STEPS + (k.group + s)
                part = agg_ps[s % 2]
                dve.wait_ge(summed, g + 1)
                wait(dve, agg_added, 2 * g)
                cols = agg[:, bass.ds(at, OLD)]
                if first:
                    ops.tensor_copy(cols, part[:, 0:OLD]).then_inc(agg_added, 1)
                else:
                    ops.tensor_tensor(cols, cols, part[:, 0:OLD], ALU.add).then_inc(agg_added, 1)
                ops.tensor_copy(agg[:, bass.ds(at + OLD, GROUP_NODES)], part[:, OLD:WINDOW]).then_inc(agg_added, 1)

            def gru_step(layer, v, j, h, i_n):
                n = j * P
                dve.wait_ge(gates_rz, 2 * v + 1)
                dve.wait_ge(gates_ps, 4 * v + 3)
                wait(dve, cand, v)
                ops.scalar_tensor_tensor(out=pre_n[:, 0:n], in0=hn_ps[:, 0:n], scalar=b[:, B_HH + N:B_HH + N + 1],
                                         in1=gate_r[:, 0:n], op0=ALU.add, op1=ALU.mult).then_inc(gru, 1)
                dve.wait_ge(gru, 5 * v + 1)
                dve.wait_ge(gates_ps, 4 * v + 4)
                ops.tensor_tensor(pre_n[:, 0:n], pre_n[:, 0:n], i_n[:, 0:n], ALU.add).then_inc(gru, 1)
                dve.wait_ge(cand, v + 1)
                if layer == LAYERS - 1:
                    wait(dve, dec2_done, v - layer * CHUNKS)
                ops.tensor_tensor(diff[:, 0:n], h[:, 0:n], gate_n[:, 0:n], ALU.subtract).then_inc(gru, 1)
                dve.wait_ge(gru, 5 * v + 3)
                dve.wait_ge(gates_rz, 2 * v + 2)
                ops.tensor_tensor(diff[:, 0:n], diff[:, 0:n], gate_z[:, 0:n], ALU.mult).then_inc(gru, 1)
                dve.wait_ge(gru, 5 * v + 4)
                if layer < LAYERS - 1:
                    dve.wait_ge(table_sum, v + CHUNKS)
                    dve.wait_ge(state_stored, 16 * (v + CHUNKS))
                else:
                    dve.wait_ge(state_stored, 16 * CHUNKS * LAYERS)
                    dve.wait_ge(table_sum, CHUNKS * LAYERS)
                    wait(dve, relu_ready, v - layer * CHUNKS)
                ops.tensor_tensor(h_new[:, 0:n], diff[:, 0:n], gate_n[:, 0:n], ALU.add).then_inc(gru, 1)

            def decode(c, j):
                n = j * P
                dve.wait_ge(dec2_done, c + 1)
                wait(dve, out_stored, 16 * c)
                b2 = b2_all[:, :].rearrange("p (a f) -> p a f", a=1).broadcast_to([P, j, H])
                ops.tensor_tensor(by_tile(out_stage, j), by_tile(dec_ps, j), b2, ALU.add).then_inc(dec_biased, 1)
                dve.wait_ge(dec_sig, c + 1)
                dve.wait_ge(x_again, 16 * (c + 1))
                ops.tensor_tensor(out_stage[:, 0:n], out_stage[:, 0:n], x_stage[:, 0:n], ALU.add).then_inc(out_ready, 1)

            def pick(c):
                step = c * 5
                wait(dve, hot, c * SUBS)
                for q in range(SUBS):
                    first = dve.value_load(start_i[0:1, bass.ds(c * SUBS + q, 1)], min_val=0, max_val=TILE_COLS - SUB_TILES)
                    n = SUB_TILES * 3
                    last = ops.tensor_copy(picked[:, q * n:(q + 1) * n], edge_info[:, bass.ds(first * 3, n)])
                last.then_inc(subs_picked, 1)
                dve.wait_ge(subs_picked, step + 1)
                ops.scalar_tensor_tensor(out=sub_u[:, :], in0=picked_v[:, :, 0], scalar=half_base[:, bass.ds(c, 1)],
                                         in1=sub_base[:, :], op0=ALU.subtract, op1=ALU.subtract).then_inc(subs_picked, 1)
                dve.wait_ge(subs_picked, step + 2)
                ops.tensor_scalar(sub_in[:, :], sub_u[:, :], 0.0, None, ALU.is_ge).then_inc(subs_picked, 1)
                dve.wait_ge(subs_picked, step + 3)
                ops.scalar_tensor_tensor(out=sub_in[:, :], in0=sub_u[:, :], scalar=float(SUB), in1=sub_in[:, :],
                                         op0=ALU.is_lt, op1=ALU.mult)
                ops.tensor_tensor(sub_u[:, :], sub_u[:, :], picked_v[:, :, 1], ALU.add).then_inc(subs_picked, 1)
                dve.wait_ge(subs_picked, step + 4)
                ops.tensor_tensor(sub_key[:, :], sub_u[:, :], sub_in[:, :], ALU.mult).then_inc(subs_picked, 1)
                dve.wait_ge(subs_picked, step + 5)

            def one_hot(c, q):
                wait(dve, built, (c * SUBS + (q - 1)) * PIECES)
                for t in range(SUB_TILES):
                    at = q * SUB_TILES + t
                    ops.tensor_scalar(key_hot[:, q % 2, t, :], key_cols, sub_key[:, at:at + 1], None, ALU.is_equal)
                    last = ops.tensor_scalar(low_hot[:, q % 2, t, :], cols_f[:, 0:P], picked_v[:, at, 2:3], None, ALU.is_equal)
                last.then_inc(hot, 1)

            def bound(c):
                dve.wait_ge(adj_squared, (c + 1) * PARTS)
                ops.tensor_tensor(squares_max[:, :], squares_max[:, :], squares[:, :], ALU.max).then_inc(squares_used, 1)
                dve.wait_ge(squares_used, c + 1)

            def gathering(k, build):
                last_layer = k.layer == LAYERS - 1
                i_n = r_ps

                def iteration(c, steps):
                    before = not (isinstance(c, int) and c == 0)
                    building = build and not (isinstance(c, int) and c == LAST)
                    v = c + (k.v - 1)
                    if building:
                        pick(c)
                    q = 0
                    for s in range(steps):
                        if building:
                            for _ in range(1 + s % 2):
                                one_hot(c, q)
                                q += 1
                        select_next(k, c, s, steps)
                        add(k, c, s, first=not before and s == 0)
                        if before and s == 2:
                            gru_step(k.layer, v, J, h_old[0], i_n)
                        if before and last_layer and s == min(5, steps - 1):
                            decode(c - 1, J)
                        if before and build and s == 1:
                            bound(c - 1)

                stage(k, 0)
                select(k, 0, 0)
                iteration(0, STEPS)
                with dve.Fori(1, LAST) as c:
                    iteration(c, STEPS)
                iteration(LAST, TAIL_GROUPS)
                if build:
                    ops.tensor_reduce(irregular[:, 2:3], squares_max[:, :], AX_X, ALU.max).then_inc(regular_sum, 1)
                    dve.wait_ge(regular_sum, 1)
                    ops.tensor_scalar(irregular[:, 2:3], irregular[:, 2:3], SQUARES_LIMIT, None, ALU.is_ge).then_inc(regular_sum, 1)
                gru_step(k.layer, k.v + LAST, LAST_J, h_old[0], i_n)
                if build:
                    dve.wait_ge(regular_sum, 3)
                    ops.tensor_copy(n_irregular[:, :], agg_ps[0][0:1, 0:1]).then_inc(regular_ready, 1)
                if last_layer:
                    decode(LAST, LAST_J)

            def dense(k):
                layer = k.layer
                last_layer = layer == LAYERS - 1

                def split(c, j):
                    n = (layer - 1) * CHUNKS + c
                    rows = slice(c * J, c * J + j)
                    dve.wait_ge(split_act, 2 * n + 1)
                    wait(dve, split_dve, 2 * n)
                    ops.tensor_tensor(by_tile(diff, j), by_tile(m_in[c % 2], j), parts[:, rows, 0, :], ALU.subtract).then_inc(split_dve, 1)
                    dve.wait_ge(split_dve, 2 * n + 1)
                    dve.wait_ge(split_act, 2 * n + 2)
                    ops.tensor_tensor(parts[:, rows, 2, :], by_tile(diff, j), parts[:, rows, 1, :], ALU.subtract).then_inc(split_dve, 1)

                c0 = DENSE_CHUNKS
                stage(k, c0 - 1)
                select(k, c0 - 1, STEPS - 1)
                select_next(k, c0 - 1, STEPS - 1, STEPS)
                add(k, c0 - 1, STEPS - 1, first=True)
                each = -(-CHUNKS // (PARTS - 1))
                for s in range(STEPS):
                    for c in range(s * each, min(CHUNKS, (s + 1) * each)):
                        split(c, J if c < LAST else LAST_J)
                    select_next(k, c0, s, STEPS)
                    add(k, c0, s)
                with dve.Fori(c0 + 1, BURST) as c:
                    for s in range(STEPS):
                        select_next(k, c, s, STEPS)
                        add(k, c, s)

                def burst(c, start, end):
                    for s in range(STEPS):
                        select_next(k, c, s, STEPS)
                        if s < end:
                            gru_step(layer, start + s + k.v, J, h_old[s % 2], in_ps)
                        add(k, c, s)
                        if s < end and last_layer:
                            decode(start + s, J)

                if BURST < LAST - 1:
                    with dve.Fori(0, LAST - 1 - BURST) as i:
                        burst(i + BURST, i * STEPS, STEPS)
                burst(LAST - 1, LAST - STEPS, STEPS - 1)
                for s in range(TAIL_GROUPS):
                    select_next(k, LAST, s, TAIL_GROUPS)
                    add(k, LAST, s)
                    if s == 1:
                        gru_step(layer, k.v + LAST - 1, J, h_old[(LAST - 1) % 2], in_ps)
                    if s == 2 and last_layer:
                        decode(LAST - 1, J)
                gru_step(layer, k.v + LAST, LAST_J, h_old[LAST % 2], in_ps)
                if last_layer:
                    decode(LAST, LAST_J)

            def general():
                def one_tile(layer, t):
                    number = layer * TILES + t
                    g = G_STEPS * number
                    wait(dve, g_scattered, 16 * number)
                    ops.tensor_copy(tile_dst[:, :], edge_info[:, bass.ds(t * 3, 1)]).then_inc(g_step, 1)
                    dve.wait_ge(g_step, g + 1)
                    ops.tensor_scalar(tile_diag, identity[:, :], tile_dst[:, :], None, ALU.mult).then_inc(g_step, 1)
                    dve.wait_ge(g_product, 2 * number + 1)
                    ops.tensor_scalar(tile_equal, agg_ps[0][:, 0:P], tile_dst[:, :], None, ALU.is_equal).then_inc(g_step, 1)
                    dve.wait_ge(g_step, g + 3)
                    ops.tensor_tensor(tile_before, tile_equal, lower[:, :], ALU.mult).then_inc(g_step, 1)
                    dve.wait_ge(g_step, g + 4)
                    ops.tensor_reduce(tile_dup[:, :], tile_before, AX_X, ALU.add).then_inc(g_step, 1)
                    dve.wait_ge(g_step, g + 5)
                    ops.tensor_scalar(tile_dup[:, :], tile_dup[:, :], 0.0, None, ALU.is_gt).then_inc(g_step, 1)
                    ops.tensor_tensor(tile_row[:, :], dump[:, :], tile_dst[:, :], ALU.subtract).then_inc(g_step, 1)
                    dve.wait_ge(g_step, g + 7)
                    ops.tensor_tensor(tile_row[:, :], tile_row[:, :], tile_dup[:, :], ALU.mult).then_inc(g_step, 1)
                    dve.wait_ge(g_step, g + 8)
                    ops.tensor_tensor(tile_index[:, :], tile_row[:, :], tile_dst[:, :], ALU.add).then_inc(g_step, 1)
                    dve.wait_ge(g_product, 2 * number + 2)
                    ops.tensor_copy(tile_sums, agg_ps[1][:, 0:H]).then_inc(g_step, 1)

                def one_chunk(layer, c, j):
                    n = j * P
                    v = layer * CHUNKS + c
                    dve.wait_ge(g_turned, v + 1)
                    ops.tensor_copy(agg[:, bass.ds(c * CHUNK + MARGIN, n)], agg_ps[0][:, 0:n]).then_inc(g_agg, 1)
                    gru_step(layer, v, j, h_old[0], r_ps)
                    if layer == LAYERS - 1:
                        decode(c, j)

                for layer in range(LAYERS):
                    ops.memset(agg[:, :], 0.0).then_inc(g_zeros, 1)
                    dve.wait_ge(g_cleared, 16 * (layer + 1))
                    one_tile(layer, 0)
                    with dve.Fori(1, TILES) as t:
                        one_tile(layer, t)
                    one_chunk(layer, 0, J)
                    with dve.Fori(1, LAST) as c:
                        one_chunk(layer, c, J)
                    one_chunk(layer, LAST, LAST_J)

            choose(dve, general, gathering, dense)

        @block.tensor
        def _(pe):
            mm = nc.tensor.matmul
            pe.wait_ge(loaded, 16 * N_LOADS)
            pe.wait_ge(consts, N_CONSTS)
            for i in range(FIRST_COLS):
                pe.wait_ge(hot_limits, i + 1)
                last = mm(agg_ps[0][0:1, 0:ALL_SUBS + 1], ones_all[:, 0:1], before_limit[i % 2],
                          start=(i == 0), stop=(i == FIRST_COLS - 1)).then_inc(limit_sum, 1)
            pe.wait_ge(prep, PREP_OUTSIDE)
            mm(table_ps[0:1, 0:1], outside[:, 0:1], ones_all[:, 0:1], start=True, stop=False)
            mm(table_ps[0:1, 0:1], outside[:, 1:2], ones_all[:, 0:1], start=False, stop=True).then_inc(prep_sum, 1)
            mm(dec_ps[:, 0:H], ones_all[0:1, :], b2_row[:, :], start=True, stop=True).then_inc(prep_sum, 1)
            mm(agg_ps[1][0:1, 0:1], ones_all[:, 0:1], ones_all[:, 0:1], start=True, stop=True).then_inc(prep_sum, 1)

            def rows_of(target, lhs, weight, j):
                for t in range(j):
                    last = mm(target[:, t * H:(t + 1) * H], lhs[:, t * P:(t + 1) * P], weight, start=True, stop=True)
                return last

            def transposes(c, j):
                pe.wait_ge(normed, c + 1)
                wait(pe, xT_ready, c)
                for t in range(j):
                    last = nc.tensor.transpose(tr_ps[:, t * P:(t + 1) * P], x_norm[:, t * H:(t + 1) * H], identity[:, :])
                last.then_inc(transposed, 1)

            def encode(c, j):
                n = j * P
                pe.wait_ge(xT_ready, c + 1)
                wait(pe, encT_ready, c)
                mm(enc1_ps[:, 0:n], wblock(W_ENC1), xT[:, 0:n], start=True, stop=True).then_inc(enc1_done, 1)
                pe.wait_ge(encT_ready, c + 1)
                wait(pe, h0_ready, c)
                mm(enc2_ps[:, 0:n], wblock(W_ENC2), encT[:, 0:n], start=True, stop=True).then_inc(enc2_done, 1)

            def first_table(c, j):
                pe.wait_ge(h0_ready, c + 1)
                wait(pe, table_out, c)
                rows_of(table_ps, h_new, wblock(W_CONV), j).then_inc(table_sum, 1)

            transposes(0, J)
            with pe.Fori(0, LAST - 1) as c:
                encode(c, J)
                transposes(c + 1, J)
                first_table(c, J)
            encode(LAST - 1, J)
            transposes(LAST, LAST_J)
            first_table(LAST - 1, J)
            encode(LAST, LAST_J)
            first_table(LAST, LAST_J)

            def sum_group(k, c, s):
                g = c * STEPS + (k.group + s)
                slot = s % SLOTS
                n_tiles = tiles_of(c, s)
                pe.wait_ge(gathered[slot], k.gathered(c, s))
                pe.wait_ge(selected, g + 1)
                wait(pe, agg_added, 2 * (g - 1))
                for t in range(n_tiles):
                    at = t * TILE_NODES
                    last = mm(agg_ps[s % 2][:, at:at + TILE_WINDOW], messages[:, slot, t, :], selection[:, s % 2, t, :],
                              start=(t == 0), stop=(t == n_tiles - 1), skip_group_check=True)
                if n_tiles < GT:
                    at = n_tiles * TILE_NODES
                    last = mm(agg_ps[s % 2][:, at + MARGIN:WINDOW], messages[:, slot, 0, :], no_selection[:, at + MARGIN:WINDOW],
                              start=False, stop=True, skip_group_check=True)
                last.then_inc(summed, 1)

            def gates(v, c, j, complete, h, h_ready, in_bank):
                n = j * P
                a = agg[:, bass.ds(c * CHUNK + MARGIN, n)]
                pe.wait_ge(*complete)
                pe.wait_ge(*h_ready)
                wait(pe, gates_rz, 2 * v)
                wait(pe, cand, v)
                for gate, bank in ((R, r_ps), (Z, z_ps)):
                    mm(bank[:, 0:n], wblock(W_HH + gate), h[:, 0:n], start=True, stop=False)
                    mm(bank[:, 0:n], wblock(W_IH + gate), a, start=False, stop=True).then_inc(gates_ps, 1)
                mm(hn_ps[:, 0:n], wblock(W_HH + N), h[:, 0:n], start=True, stop=True).then_inc(gates_ps, 1)
                if in_bank is r_ps:
                    pe.wait_ge(gates_rz, 2 * v + 1)
                mm(in_bank[:, 0:n], wblock(W_IH + N), a, start=True, stop=True).then_inc(gates_ps, 1)

            def make_table(layer, v, c, j):
                pe.wait_ge(gru, 5 * v + 5)
                pe.wait_ge(table_out, v + CHUNKS)
                rows_of(table_ps, h_new, wblock(W_CONV + layer + 1), j).then_inc(table_sum, 1)

            def decode_first(c, j):
                n = j * P
                pe.wait_ge(relu_ready, c + 1)
                wait(pe, decT_ready, c)
                mm(table_ps[:, 0:n], wblock(W_DEC1), relu_h[:, 0:n], start=True, stop=True).then_inc(dec1_done, 1)

            def decode_second(c, j):
                pe.wait_ge(decT_ready, c + 1)
                wait(pe, dec_biased, c)
                rows_of(dec_ps, decT, wblock(W_DEC2), j).then_inc(dec2_done, 1)

            def finish(layer, v, c, j):
                if layer < LAYERS - 1:
                    make_table(layer, v, c, j)
                else:
                    decode_first(c, j)
                    decode_second(c, j)

            def build_counts(c, q):
                pe.wait_ge(hot, c * SUBS + (q + 1))
                for i in range(PIECES):
                    n = (c * SUBS + q) * PIECES + i
                    a, e = PIECE_AT[i] * SUB, PIECE_AT[i + 1] * SUB
                    wait(pe, adj_out, n - 1)
                    for t in range(SUB_TILES):
                        last = mm(build_ps[i % 2][:, 0:e - a], low_hot[:, q % 2, t, :], key_hot[:, q % 2, t, a:e],
                                  start=(t == 0), stop=(t == SUB_TILES - 1))
                    last.then_inc(built, 1)

            def gathering(k, build):
                last_layer = k.layer == LAYERS - 1

                def iteration(c, steps):
                    before = not (isinstance(c, int) and c == 0)
                    building = build and not (isinstance(c, int) and c == LAST)
                    v = c + (k.v - 1)
                    q = 0
                    for s in range(steps):
                        if building:
                            for _ in range(1 + s % 2):
                                build_counts(c, q)
                                q += 1
                        sum_group(k, c, s)
                        if before and s == 1:
                            gates(v, c - 1, J, (agg_added, 2 * (c * STEPS) + 2 * (k.group + 1)),
                                  h_old[0], (h_loaded[0], 16 * (v + 1)), r_ps)
                        if before and s == 3:
                            finish(k.layer, v, c - 1, J)

                iteration(0, STEPS)
                with pe.Fori(1, LAST) as c:
                    iteration(c, STEPS)
                iteration(LAST, TAIL_GROUPS)
                v = k.v + LAST
                gates(v, LAST, LAST_J, (agg_added, 2 * (k.group + GROUPS)), h_old[0], (h_loaded[0], 16 * (v + 1)), r_ps)
                if build:
                    pe.wait_ge(regular_sum, 2)
                    for i in range(3):
                        last = mm(agg_ps[0][0:1, 0:1], irregular[:, i:i + 1], ones_all[:, 0:1], start=(i == 0), stop=(i == 2))
                    last.then_inc(regular_sum, 1)
                finish(k.layer, v, LAST, LAST_J)

            def dense(k):
                layer = k.layer

                def sum_strip(i, p):
                    n = (layer - 1) * STRIPS * PARTS + i * PARTS + p
                    a, e = PART_AT[p], PART_AT[p + 1]
                    pe.wait_ge(part_loaded[p % 2], 16 * ((layer - 1) * STRIPS * PARTS // 2 + p // 2 + 1) + i * (16 * PARTS // 2))
                    pe.wait_ge(split_dve, 2 * ((layer - 1) * CHUNKS + -(-e // J)))
                    if p == 0:
                        wait(pe, strip_out, (layer - 1) * STRIPS + i)
                        pe.wait_ge(gru, 5 * k.v)
                    pe.sem_inc(turns[2], 1)
                    for block in range(a, e):
                        counts = strip_part[:, p % 2, :, (block - a) * HALF:(block - a + 1) * HALF]
                        for part in range(SPLITS):
                            last = mm(strip_ps[:, 0:STRIP].rearrange("f (h d) -> f h d", h=2), parts[:, block, part, :], counts,
                                      start=(block == 0 and part == 0), stop=(block == BLOCKS - 1 and part == SPLITS - 1))
                    last.then_inc(part_used, 1)

                def chunk_gates(c, j, odd, complete):
                    evens, odds = (CHUNKS + 1) // 2, CHUNKS // 2
                    before = (layer - 1) * odds if odd else CHUNKS + (layer - 1) * evens
                    ready = c * 8 + (16 * (before + 1) - 8 * odd)
                    gates(c + k.v, c, j, complete, h_old[odd], (h_loaded[odd], ready), in_ps)

                strips = (strip_out, layer * STRIPS)
                sum_group(k, DENSE_CHUNKS - 1, STEPS - 1)
                with pe.Fori(0, STRIPS) as i:
                    for s in range(STEPS):
                        sum_group(k, i + DENSE_CHUNKS, s)
                        sum_strip(i, s)
                chunk_gates(0, J, 0, strips)

                def burst(c, start, end):
                    for s in range(STEPS):
                        sum_group(k, c, s)
                        if s < end:
                            chunk_gates(start + s + 1, J, (s + 1) % 2, after(c))
                        if s <= end:
                            finish(layer, start + s + k.v, start + s, J)

                def after(c):
                    return (agg_added, 2 * (c * STEPS) + 2 * (k.group + 1))

                if BURST < LAST - 1:
                    with pe.Fori(0, LAST - 1 - BURST) as i:
                        burst(i + BURST, i * STEPS, STEPS)
                burst(LAST - 1, LAST - STEPS, STEPS - 2)
                for s in range(TAIL_GROUPS):
                    sum_group(k, LAST, s)
                    if s == 1:
                        chunk_gates(LAST - 1, J, (LAST - 1) % 2, after(LAST))
                    if s == 2:
                        finish(layer, k.v + LAST - 1, LAST - 1, J)
                chunk_gates(LAST, LAST_J, LAST % 2, (agg_added, 2 * (k.group + GROUPS)))
                finish(layer, k.v + LAST, LAST, LAST_J)

            def general():
                def one_tile(layer, t):
                    number = layer * TILES + t
                    pe.wait_ge(g_step, G_STEPS * number + 2)
                    mm(agg_ps[0][:, 0:P], ones_all[:, :], tile_diag, start=True, stop=True).then_inc(g_product, 1)
                    pe.wait_ge(g_step, G_STEPS * number + 3)
                    pe.wait_ge(g_gathered, 16 * (number + 1))
                    mm(agg_ps[1][:, 0:H], tile_equal, tile_messages, start=True, stop=True).then_inc(g_product, 1)

                def one_chunk(layer, c, j):
                    v = layer * CHUNKS + c
                    pe.wait_ge(g_rows, 16 * (v + 1))
                    wait(pe, g_agg, v)
                    for t in range(j):
                        last = nc.tensor.transpose(agg_ps[0][:, t * P:(t + 1) * P], sum_rows[:, t * H:(t + 1) * H], identity[:, :])
                    last.then_inc(g_turned, 1)
                    gates(v, c, j, (g_agg, v + 1), h_old[0], (h_loaded[0], 16 * (v + 1)), r_ps)
                    finish(layer, v, c, j)

                for layer in range(LAYERS):
                    one_tile(layer, 0)
                    with pe.Fori(1, TILES) as t:
                        one_tile(layer, t)
                    one_chunk(layer, 0, J)
                    with pe.Fori(1, LAST) as c:
                        one_chunk(layer, c, J)
                    one_chunk(layer, LAST, LAST_J)

            choose(pe, general, gathering, dense)


N_CONSTS = 12


def kernel(x, src, dst, L0_gnn_enc_w1, L0_gnn_enc_b1, L0_gnn_enc_w2, L0_gnn_enc_b2, L0_gnn_conv_w, L0_gnn_gru_wih,
           L0_gnn_gru_whh, L0_gnn_gru_bih, L0_gnn_gru_bhh, L0_gnn_dec_w1, L0_gnn_dec_b1, L0_gnn_dec_w2, L0_gnn_dec_b2):
    import numpy as np
    import concourse.bacc as bacc
    from concourse.bass_utils import run_bass_kernel_spmd

    def padded(index, filler, n):
        out = np.full(n, filler, np.int32)
        out[:len(index)] = np.asarray(index)
        return out

    def columns(flat):
        return np.ascontiguousarray(flat.reshape(-1, P).T)

    edges = TILE_COLS * P
    dst_pad = padded(dst, N_NODES, edges)
    x_pad = np.zeros((NODES_PAD, H), np.float32)
    x_pad[:N_NODES] = np.asarray(x)
    blocks = [np.asarray(L0_gnn_enc_w1).T, np.asarray(L0_gnn_enc_w2).T, np.asarray(L0_gnn_gru_wih).T,
              np.asarray(L0_gnn_gru_whh).T, np.asarray(L0_gnn_dec_w1).T, np.asarray(L0_gnn_dec_w2).T]
    blocks += [np.asarray(L0_gnn_conv_w)[layer] for layer in range(LAYERS)]
    bias = [np.asarray(v).reshape(-1, H) for v in (L0_gnn_enc_b1, L0_gnn_enc_b2, L0_gnn_gru_bih, L0_gnn_gru_bhh, L0_gnn_dec_b1)]
    arrays = {
        "x": x_pad,
        "src": columns(padded(src, 0, edges)),
        "dst": columns(dst_pad),
        "dst_next": columns(padded(dst_pad[1:], N_NODES, edges)),
        "firsts": columns(padded(dst_pad[::P], N_NODES, FIRST_COLS * P)),
        "weights": np.ascontiguousarray(np.concatenate(blocks, axis=1)),
        "biases": np.ascontiguousarray(np.concatenate(bias, axis=0).T),
        "dec_b2": np.asarray(L0_gnn_dec_b2).reshape(1, H),
    }
    nc = bacc.Bacc("TRN2", target_bir_lowering=False, num_devices=1)
    aps = [nc.dram_tensor(f"in_{k}", a.shape, mybir.dt.from_np(a.dtype), kind="ExternalInput").ap() for k, a in arrays.items()]
    out = nc.dram_tensor("out", (NODES_PAD, H), F32, kind="ExternalOutput").ap()
    gnn(nc, *aps, out)
    result = run_bass_kernel_spmd(nc, [{f"in_{k}": a for k, a in arrays.items()}], core_ids=[0])
    return result.results[0]["out"][:N_NODES]
```

```python
from contextlib import ExitStack

import concourse.bass as bass
from concourse import mybir

P = 128
F32 = mybir.dt.float32
BF16 = mybir.dt.bfloat16
FP16 = mybir.dt.float16
FP8 = mybir.dt.float8e4
I32 = mybir.dt.int32
ALU = mybir.AluOpType
ACT = mybir.ActivationFunctionType
AX_X = mybir.AxisListType.X

N_NODES = 12500
N_EDGES = 200000
LAYERS = 5
H = 128
EPS = 1e-5
X_PARTS = 4

CHUNK = 512
J = CHUNK // P
CHUNKS = -(-N_NODES // CHUNK)
LAST = CHUNKS - 1
LAST_J = -(-(N_NODES - LAST * CHUNK) // P)
NODES_PAD = LAST * CHUNK + LAST_J * P
BLOCKS = NODES_PAD // P

TILES = -(-N_EDGES // P)
GT = 8
GROUPS = -(-TILES // GT)
GROUP_NODES = NODES_PAD // GROUPS
TILE_NODES = GROUP_NODES // GT
MARGIN = 64
TILE_WINDOW = TILE_NODES + 2 * MARGIN
WINDOW = GROUP_NODES + 2 * MARGIN
OLD = WINDOW - GROUP_NODES
STEPS = CHUNK // GROUP_NODES
ITER_TILES = STEPS * GT
TAIL_GROUPS = GROUPS - LAST * STEPS
SLOTS = 4
TILE_COLS = CHUNKS * ITER_TILES
AGG_COLS = (GROUPS - 1) * GROUP_NODES + WINDOW

QUARTER = 96
HALF = 2 * QUARTER
STRIP = 2 * HALF
STRIPS = LAST // 2
DENSE = STRIPS * STRIP
DENSE_CHUNKS = DENSE // CHUNK
BURST = DENSE_CHUNKS + STRIPS
EARLY = STRIP * (STRIPS - 1) // CHUNK
LAG = STRIPS - EARLY
BURST_GROUPS = (0, 1, 2, 4, 5, 6)
BURSTS = LAST - 1 - BURST
REST = LAST - 1 - EARLY - BURSTS * len(BURST_GROUPS)
SUB = 16
SUBS = HALF // SUB
Q_SUBS = QUARTER // SUB
SUB_TILES = 4
ALL_SUBS = LAST * SUBS
KEYS = BLOCKS * SUB
PIECES = 4
PARTS = STEPS
SPLITS = 3
COUNT_SCALE = 0.25
SQUARES_LIMIT = (16 * COUNT_SCALE) ** 2
SQUARES = 8
JUNKS = 4
PICK = SUB_TILES * 3
FIRST_COLS = -(-TILE_COLS // P)


def cuts(n, parts):
    return [(n * i + parts - 1) // parts for i in range(parts + 1)]


X_AT = cuts(LAST, X_PARTS)
PIECE_AT = cuts(BLOCKS, PIECES)
PART_AT = cuts(BLOCKS, PARTS)
PART_BLOCKS = max(b - a for a, b in zip(PART_AT, PART_AT[1:]))
PIECE_BLOCKS = max(b - a for a, b in zip(PIECE_AT, PIECE_AT[1:]))

assert GROUP_NODES * GROUPS == NODES_PAD and GROUPS % SLOTS == 0 and STEPS == 2 * SLOTS and TAIL_GROUPS == SLOTS
assert MARGIN + NODES_PAD <= AGG_COLS and MARGIN <= GROUP_NODES and TILE_NODES * GT == GROUP_NODES
assert DENSE_CHUNKS * CHUNK == DENSE and KEYS < 2048 and PIECE_BLOCKS * SUB <= CHUNK and SUBS % 2 == 0
assert EARLY % 2 == 0 and len(BURST_GROUPS) % 2 == 0 and 0 < REST < STEPS and LAG > 0 and LAST % (2 * X_PARTS) == 0
assert SUB_TILES * P * COUNT_SCALE < 240

W_ENC1, W_ENC2, W_IH, W_HH, W_DEC1, W_DEC2, W_CONV = 0, 1, 2, 5, 8, 9, 10
W_BLOCKS = W_CONV + LAYERS
B_ENC1, B_ENC2, B_IH, B_HH, B_DEC1 = 0, 1, 2, 5, 8
B_COLS = 9
R, Z, N = 0, 1, 2
DUMP_ROWS = P
G_STEPS = 10
N_LOADS = 4
N_EDGE_LOADS = 3
PREP_LIMITS, PREP_OUTSIDE, PREP_BUILD, PREP_STATS = 8, 13, 27, 37
KEY_STEPS = 5


def tiles_of(c, s):
    return min(GT, TILES - (c * STEPS + s) * GT) if isinstance(c, int) else GT


def in_stages(engine, *stages):
    def step(number):
        for s in reversed(range(len(stages))):
            chunk = number - s
            if stages[s] and not (isinstance(chunk, int) and not 0 <= chunk <= LAST):
                stages[s](chunk, LAST_J if isinstance(chunk, int) and chunk == LAST else J)

    first = len(stages)
    for number in range(first):
        step(number)
    with engine.Fori(first, LAST) as number:
        step(number)
    for number in range(LAST, LAST + first):
        step(number)


def early_chunks(engine, last_layer, body):
    if last_layer:
        body(0)
    with engine.Fori(1 if last_layer else 0, EARLY) as c:
        body(c)


def wait(engine, semaphore, value):
    if not isinstance(value, int) or value > 0:
        engine.wait_ge(semaphore, value)


class Counts:

    def __init__(self, layer, dense):
        self.layer, self.dense = layer, dense
        self.v = layer * CHUNKS
        skip = DENSE_CHUNKS * STEPS - 1
        self.group = layer * GROUPS - (skip * layer if dense else 0)
        first = DENSE_CHUNKS - 1
        self.iteration = layer * CHUNKS - (first * layer if dense else 0)
        self.half = 2 * layer * CHUNKS - ((2 * first + 1) * layer if dense else 0)

    def gathered(self, c, s):
        slot = s % SLOTS
        total = sum(tiles_of(g // STEPS, g % STEPS) for g in range(slot, GROUPS, SLOTS))
        skipped = GT * len(range(slot, DENSE_CHUNKS * STEPS - 1, SLOTS))
        before = total * self.layer - (skipped * self.layer if self.dense else 0)
        if isinstance(c, int):
            return 16 * (before + min(total, GT * (c * 2 + s // SLOTS + 1)))
        return 16 * (before + GT * (s // SLOTS + 1)) + c * (2 * 16 * GT)


def gnn(nc, x, src, dst, dst_next, firsts, weights, biases, dec_b2, out):
    table = [nc.dram_tensor(f"table{i}", (NODES_PAD, H), F32, kind="Internal").ap() for i in range(2)]
    states = nc.dram_tensor("states", (CHUNKS, P, CHUNK), F32, kind="Internal").ap()
    adjacency = nc.dram_tensor("adjacency", (4 * STRIPS, P, BLOCKS * QUARTER // 2), BF16, kind="Internal").ap()
    sums = nc.dram_tensor("sums", (NODES_PAD + DUMP_ROWS, H), F32, kind="Internal").ap()

    def chunk_rows(rows, c, j):
        if j == J:
            return rows[0:LAST * CHUNK, :].rearrange("(c j p) f -> c p j f", p=P, j=J)[c, :, :, :]
        return rows[LAST * CHUNK:NODES_PAD, :].rearrange("(j p) f -> p j f", p=P)

    def by_tile(tile, j):
        return tile[:, 0:j * H].rearrange("p (j f) -> p j f", f=H)

    ctx = ExitStack()
    with ctx:
        def sb(name, shape, dt=F32):
            return ctx.enter_context(nc.sbuf_tensor(name, shape, dt))

        def ps(name):
            return ctx.enter_context(nc.psum_tensor(name, [P, CHUNK], F32))

        def sem(name):
            return ctx.enter_context(nc.semaphore(name))

        agg = sb("agg", [P, AGG_COLS])
        x_rows = agg
        w = sb("w", [P, W_BLOCKS * H])
        b = sb("b", [P, B_COLS])
        b_rz = sb("b_rz", [P, 2])
        b2_row = sb("b2_row", [1, H])
        b2_all = sb("b2_all", [P, H])
        ones_all = sb("ones_all", [P, P])
        no_selection = sb("no_selection", [P, WINDOW])
        identity = sb("identity", [P, P])
        src_all = sb("src_all", [P, TILE_COLS], I32)
        dst_rel = sb("dst_rel", [P, TILE_COLS])
        cols_i = sb("cols_i", [P, TILE_WINDOW], I32)
        cols_f = sb("cols_f", [P, TILE_WINDOW])
        outside = sb("outside", [P, 2])
        irregular = sb("irregular", [P, 3])
        n_outside = sb("n_outside", [1, 1], I32)
        n_irregular = sb("n_irregular", [1, 1], I32)
        src_stage = sb("src_stage", [P, ITER_TILES], I32)
        dst_stage = sb("dst_stage", [P, ITER_TILES])
        messages = sb("messages", [P, SLOTS, GT, H])
        selection = sb("selection", [P, 2, GT, TILE_WINDOW])
        h_old = [sb("h_old0", [P, CHUNK]), sb("h_old1", [P, CHUNK])]
        gate_r = sb("gate_r", [P, CHUNK])
        gate_z = sb("gate_z", [P, CHUNK])
        pre_n = sb("pre_n", [P, CHUNK])
        gate_n = sb("gate_n", [P, CHUNK])
        diff = sb("diff", [P, CHUNK])
        h_new = sb("h_new", [P, CHUNK])
        table_stage = sb("table_stage", [P, CHUNK])
        x_stage = sb("x_stage", [P, CHUNK])
        relu_h, decT, out_stage = gate_n, diff, table_stage
        m_in = [table_stage, x_stage]
        mean = sb("mean", [P, BLOCKS])
        rstd = sb("rstd", [P, BLOCKS])
        ln_a = sb("ln_a", [P, BLOCKS])
        ln_b = sb("ln_b", [P, BLOCKS])
        x_norm, xT, encT = gate_r, gate_z, gate_n
        strip_part = sb("strip_part", [P, 2, 4, PART_BLOCKS * QUARTER], FP8)
        m_parts = sb("m_parts", [P, BLOCKS * SPLITS * H], BF16)
        parts = m_parts[:, :].rearrange("p (k i f) -> p k i f", i=SPLITS, f=H)
        taken = [0]

        def carve(elements, dt, size):
            at = taken[0]
            taken[0] += (elements * size + 3) // 4 * 2
            assert taken[0] <= BLOCKS * SPLITS * H
            piece = m_parts[:, at:at + elements * size // 2]
            return piece if dt is BF16 else piece.bitcast(dt)

        edge_info = carve(TILE_COLS * 3, F32, 4)
        half_adj = carve(BLOCKS * HALF, FP8, 1).rearrange("p (u e) -> p u e", u=2)
        key_hot = carve(2 * SUB_TILES * KEYS, BF16, 2).rearrange("p (q t k) -> p q t k", q=2, t=SUB_TILES)
        low_hot = carve(2 * SUB_TILES * P, BF16, 2).rearrange("p (q t k) -> p q t k", q=2, t=SUB_TILES)
        key_cols = carve(KEYS, FP16, 2)
        squares = carve(2 * SQUARES, F32, 4)
        squares_max = carve(SQUARES, F32, 4)
        dst_next_all = key_hot[:, 0, :, :].rearrange("p t k -> p (t k)")[:, 0:2 * TILE_COLS].bitcast(I32)
        info = edge_info.rearrange("p (k i) -> p k i", i=3)
        picked = sb("picked", [P, SUBS * PICK])
        picked_v = picked[:, :].rearrange("p (q t i) -> p (q t) i", t=SUB_TILES, i=3)
        sub_u = sb("sub_u", [P, SUBS * SUB_TILES])
        sub_in = sb("sub_in", [P, SUBS * SUB_TILES])
        sub_key = sb("sub_key", [P, SUBS * SUB_TILES])
        sub_base_i = sb("sub_base_i", [P, SUBS * SUB_TILES], I32)
        sub_base = sb("sub_base", [P, SUBS * SUB_TILES])
        half_base_i = sb("half_base_i", [P, 2 * STRIPS], I32)
        half_base = sb("half_base", [P, 2 * STRIPS])
        first_i = sb("first_i", [P, FIRST_COLS], I32)
        first_f = sb("first_f", [P, FIRST_COLS])
        start_i = sb("start_i", [1, ALL_SUBS + 1], I32)
        room = messages[:, :, :, :].rearrange("p a t f -> p (a t f)")
        base_i = room[:, 0:TILE_COLS].bitcast(I32)
        base_f = room[:, TILE_COLS:2 * TILE_COLS]
        limits = room[:, 2 * TILE_COLS:2 * TILE_COLS + ALL_SUBS + 1]
        limits_i = gate_r[:, 0:ALL_SUBS + 1].bitcast(I32)
        tmp_i = selection[:, :, :, :].rearrange("p a t f -> p (a t f)")[:, 0:TILE_COLS].bitcast(I32)
        before_limit = [pre_n[:, 0:ALL_SUBS + 1], diff[:, 0:ALL_SUBS + 1]]
        key_cols_i = h_old[0][:, :]
        dst_all = strip_part[:, :, :, :].rearrange("p a h k -> p (a h k)")[:, 0:4 * TILE_COLS].bitcast(I32)
        junk = strip_part[:, :, :, :].rearrange("p a h k -> p (a h k)").bitcast(BF16)
        stats = half_adj[:, 0, 0:BLOCKS * 6 * 4].bitcast(F32).rearrange("p (k s) -> p k s", s=6)
        start_f = gate_z[0:1, 0:ALL_SUBS + 1]
        start_of = gate_n[0:1, 0:ALL_SUBS + 1]
        lower = sb("lower", [P, P])
        dump_i = sb("dump_i", [P, 1], I32)
        dump = sb("dump", [P, 1])
        tile_src = sb("tile_src", [P, 1], I32)
        tile_dst = sb("tile_dst", [P, 1])
        tile_row = sb("tile_row", [P, 1])
        tile_dup = sb("tile_dup", [P, 1])
        tile_index = sb("tile_index", [P, 1], I32)
        tile_diag = selection[:, 0, 0, 0:P]
        tile_equal = selection[:, 0, 1, 0:P]
        tile_before = selection[:, 0, 2, 0:P]
        tile_messages = messages[:, 0, 0, :]
        tile_sums = messages[:, 0, 1, :]
        sum_rows = messages[:, 1, 0:J, :].rearrange("p t f -> p (t f)")

        agg_ps = [ps("agg_ps0"), ps("agg_ps1")]
        r_ps, z_ps, hn_ps, in_ps = ps("r_ps"), ps("z_ps"), ps("hn_ps"), ps("in_ps")
        table_ps, dec_ps = ps("table_ps"), ps("dec_ps")
        tr_ps, enc1_ps, enc2_ps = r_ps, z_ps, hn_ps
        strip_ps = in_ps
        build_ps = [dec_ps, in_ps]

        edges_loaded = sem("edges_loaded")
        loaded = sem("loaded")
        x_loaded = [sem(f"x_loaded{i}") for i in range(X_PARTS)]
        consts = sem("consts")
        key_iota = sem("key_iota")
        key_taken = sem("key_taken")
        prep = sem("prep")
        hot_limits = sem("hot_limits")
        limit_sum = sem("limit_sum")
        prep_sum = sem("prep_sum")
        n_ready = sem("n_ready")
        ln_std = sem("ln_std")
        normed = sem("normed")
        transposed = sem("transposed")
        xT_ready = sem("xT_ready")
        enc1_done = sem("enc1_done")
        encT_ready = sem("encT_ready")
        enc2_done = sem("enc2_done")
        h0_ready = sem("h0_ready")
        src_staged = sem("src_staged")
        turns = [sem(f"{name}_turns") for name in ("pool", "act", "pe", "sp")]
        gathered = [sem(f"gathered{i}") for i in range(SLOTS)]
        dst_staged = sem("dst_staged")
        selected = sem("selected")
        summed = sem("summed")
        agg_added = sem("agg_added")
        h_loaded = [sem("h_loaded0"), sem("h_loaded1")]
        gates_ps = sem("gates_ps")
        gates_rz = sem("gates_rz")
        cand = sem("cand")
        gru = sem("gru")
        state_stored = sem("state_stored")
        table_sum = sem("table_sum")
        table_out = sem("table_out")
        table_stored = sem("table_stored")
        picked_loaded = [sem("picked_loaded0"), sem("picked_loaded1")]
        keyed = sem("keyed")
        hot = sem("hot")
        built = sem("built")
        adj_out = sem("adj_out")
        adj_squared = sem("adj_squared")
        squares_used = sem("squares_used")
        adj_stored = [sem("adj_stored0"), sem("adj_stored1")]
        regular_sum = sem("regular_sum")
        regular_ready = sem("regular_ready")
        m_loaded = [sem("m_loaded0"), sem("m_loaded1")]
        split_act = sem("split_act")
        split_dve = sem("split_dve")
        part_loaded = [sem("part_loaded0"), sem("part_loaded1")]
        part_used = sem("part_used")
        strip_out = sem("strip_out")
        relu_ready = sem("relu_ready")
        dec1_done = sem("dec1_done")
        decT_ready = sem("decT_ready")
        dec2_done = sem("dec2_done")
        dec_biased = sem("dec_biased")
        dec_sig = sem("dec_sig")
        x_again = sem("x_again")
        out_ready = sem("out_ready")
        out_stored = sem("out_stored")
        g_zeros = sem("g_zeros")
        g_cleared = sem("g_cleared")
        g_src = sem("g_src")
        g_gathered = sem("g_gathered")
        g_step = sem("g_step")
        g_product = sem("g_product")
        g_scattered = sem("g_scattered")
        g_rows = sem("g_rows")
        g_turned = sem("g_turned")
        g_agg = sem("g_agg")

        block = ctx.enter_context(nc.Block())

        def wblock(k):
            return w[:, k * H:(k + 1) * H]

        def choose(engine, general, gathering, dense):
            engine.wait_ge(n_ready, 1)
            with engine.If(engine.value_load(n_outside[0:1, 0:1], min_val=0, max_val=2 * P) > 0):
                general()
            with engine.Else():
                gathering(Counts(0, False), True)
                engine.wait_ge(regular_ready, 1)
                with engine.If(engine.value_load(n_irregular[0:1, 0:1], min_val=0, max_val=3 * P) > 0):
                    for layer in range(1, LAYERS):
                        gathering(Counts(layer, False), False)
                with engine.Else():
                    for layer in range(1, LAYERS):
                        dense(Counts(layer, True))

        def old_loads(k, c, buffer):
            turns_of = (LAST - EARLY) // 2
            if buffer == 0:
                before = CHUNKS + (k.layer - 1) * (EARLY + turns_of + 1)
                return c * 8 + (16 * (before + EARLY + 1) - 8 * EARLY)
            return c * 8 + (16 * ((k.layer - 1) * turns_of + 1) - 8 * (EARLY + 1))

        def early_loads(k, c):
            before = CHUNKS + (k.layer - 1) * (EARLY + (LAST - EARLY) // 2 + 1)
            return c * 16 + 16 * (before + 1)

        @block.sync
        def _(sp):
            for to, of in ((dst_all, dst), (first_i[:, :], firsts), (dst_next_all, dst_next)):
                sp.dma_start(to, of).then_inc(edges_loaded, 16)
            for i in range(X_PARTS):
                a, e = X_AT[i] * J, (X_AT[i + 1] * J if i < X_PARTS - 1 else BLOCKS)
                sp.dma_start(x_rows[:, a * H:e * H].rearrange("p (k f) -> p k f", f=H),
                             x[a * P:e * P, :].rearrange("(k p) f -> p k f", p=P)).then_inc(x_loaded[i], 16)

            def store_state(u, c, j, ready, count):
                sp.wait_ge(ready, count)
                sp.dma_start(states[c, :, 0:j * P], h_new[:, 0:j * P]).then_inc(state_stored, 16)

            def store_table(t, u, c, j):
                sp.wait_ge(table_out, u + 1)
                sp.dma_start(chunk_rows(table[t], c, j), by_tile(table_stage, j)).then_inc(table_stored, 16)

            def load_x(c, j):
                wait(sp, out_ready, c)
                sp.dma_start(by_tile(x_stage, j), chunk_rows(x, c, j)).then_inc(x_again, 16)

            def store_out(c, j):
                sp.wait_ge(out_ready, c + 1)
                sp.dma_start(chunk_rows(out, c, j), by_tile(out_stage, j)).then_inc(out_stored, 16)

            def encoded(c, j):
                store_state(c, c, j, h0_ready, c + 1)
                store_table(0, c, c, j)

            with sp.Fori(0, LAST) as c:
                encoded(c, J)
            encoded(LAST, LAST_J)

            def load_old(v, c, j, buffer, used):
                wait(sp, gru, 5 * (v - used) + 3)
                sp.dma_start(h_old[buffer][:, 0:j * P], states[c, :, 0:j * P]).then_inc(h_loaded[buffer], 16)

            def finish(layer, v, c, j):
                if layer < LAYERS - 1:
                    store_state(v + CHUNKS, c, j, gru, 5 * v + 5)
                    store_table((layer + 1) % 2, v + CHUNKS, c, j)
                else:
                    load_x(c, j)
                    store_out(c, j)

            def pick(c, u):
                for q in range(u * Q_SUBS, (u + 1) * Q_SUBS):
                    first = sp.value_load(start_i[0:1, bass.ds(c * SUBS + q, 1)], min_val=0, max_val=TILE_COLS - SUB_TILES)
                    sp.dma_start(picked[:, q * PICK:(q + 1) * PICK],
                                 edge_info[:, bass.ds(first * 3, PICK)]).then_inc(picked_loaded[u], 16)

            def store_quarter(c, u):
                sp.wait_ge(adj_out, (c * 2 + (u + 1)) * (Q_SUBS * PIECES))
                sp.dma_start(adjacency[bass.ds(c * 2 + u, 1), :, :].rearrange("a p e -> (a p) e"),
                             half_adj[:, u, :].bitcast(BF16)).then_inc(adj_stored[u], 16)

            def gathering(k, build):
                def iteration(c, more=True):
                    if build:
                        wait(sp, hot, c * SUBS)
                        pick(c, 1)
                    if not (isinstance(c, int) and c == 0):
                        if isinstance(c, int) and c == 1:
                            load_first(k)
                        else:
                            load_old(c - 1 + k.v, c - 1, J, 0, 1)
                        finish(k.layer, c - 1 + k.v, c - 1, J)
                    if build:
                        if more:
                            sp.wait_ge(hot, c * SUBS + Q_SUBS)
                            pick(c + 1, 0)
                        store_quarter(c, 0)
                        store_quarter(c, 1)

                def load_first(k):
                    sp.dma_start(h_old[0][:, :], states[0, :, :]).then_inc(h_loaded[0], 16)

                sp.wait_ge(state_stored, 16 * CHUNKS * (k.layer + 1))
                if build:
                    sp.wait_ge(prep, PREP_BUILD)
                    pick(0, 0)
                iteration(0)
                iteration(1)
                with sp.Fori(2, LAST - 1) as c:
                    iteration(c)
                iteration(LAST - 1, more=False)
                load_old(k.v + LAST - 1, LAST - 1, J, 0, 1)
                finish(k.layer, k.v + LAST - 1, LAST - 1, J)
                load_old(k.v + LAST, LAST, LAST_J, 0, 1)
                finish(k.layer, k.v + LAST, LAST, LAST_J)

            def dense(k):
                def load_part(i, p):
                    wait(sp, part_used, (k.layer - 1) * STRIPS * PARTS + i * PARTS + (p - 1))
                    a, e = PART_AT[p], PART_AT[p + 1]
                    rows = adjacency.rearrange("(i h) p e -> i p h e", h=4)[i, :, :, a * QUARTER // 2:e * QUARTER // 2]
                    sp.dma_start(strip_part[:, p % 2, :, 0:(e - a) * QUARTER].bitcast(BF16), rows).then_inc(part_loaded[p % 2], 16)

                def load_rows(c, j):
                    n = (k.layer - 1) * CHUNKS + c
                    if c >= 2:
                        sp.wait_ge(split_dve, 2 * (n - 2) + 1)
                    sp.dma_start(by_tile(m_in[c % 2], j), chunk_rows(table[k.layer % 2], c, j)).then_inc(m_loaded[c % 2], 16)

                sp.wait_ge(table_stored, 16 * CHUNKS * (k.layer + 1))
                sp.wait_ge(state_stored, 16 * CHUNKS * (k.layer + 1))
                for u in range(2):
                    sp.wait_ge(adj_stored[u], 16 * LAST)
                load_part(0, 0)
                load_part(0, 1)
                each = -(-CHUNKS // (PARTS - 1))
                for p in range(1, PARTS + 1):
                    for c in range(0 if p == 1 else p * each - each, min(CHUNKS, p * each)):
                        load_rows(c, J if c < LAST else LAST_J)
                    if 2 <= p < PARTS:
                        load_part(0, p)
                v = k.v
                last_layer = k.layer == LAYERS - 1

                if LAG > 1:
                    with sp.Fori(1, LAG) as i:
                        for p in range(PARTS):
                            load_part(i, p)
                def early(c):
                    load_old(c + v, c, J, 0, 1)
                    for p in range(PARTS):
                        load_part(c + LAG, p)
                        if p == 5:
                            if last_layer:
                                load_x(c, J)
                            else:
                                store_state(c + (v + CHUNKS), c, J, gru, (c + v) * 5 + 5)
                    if last_layer:
                        store_out(c, J)
                    else:
                        store_table((k.layer + 1) % 2, c + (v + CHUNKS), c, J)

                early_chunks(sp, last_layer, early)
                load_old(v + EARLY, EARLY, J, 0, 1)
                load_old(v + EARLY + 1, EARLY + 1, J, 1, 2)
                with sp.Fori(0, (LAST - 2 - EARLY) // 2) as i:
                    for odd in range(2):
                        c = i * 2 + (EARLY + odd)
                        load_old(c + (v + 2), c + 2, J, odd, 2)
                        finish(k.layer, c + v, c, J)
                load_old(v + LAST, LAST, LAST_J, 0, 2)
                finish(k.layer, v + LAST - 2, LAST - 2, J)
                finish(k.layer, v + LAST - 1, LAST - 1, J)
                finish(k.layer, v + LAST, LAST, LAST_J)

            def general():
                def one_chunk(layer, c, j):
                    v = c + layer * CHUNKS
                    wait(sp, gru, 5 * (v - 1) + 3)
                    sp.sem_inc(turns[3], 1)
                    wait(sp, g_turned, v)
                    sp.dma_start(h_old[0][:, 0:j * P], states[c, :, 0:j * P]).then_inc(h_loaded[0], 16)
                    sp.dma_start(by_tile(sum_rows, j), chunk_rows(sums[0:NODES_PAD, :], c, j)).then_inc(g_rows, 16)
                    finish(layer, v, c, j)

                for layer in range(LAYERS):
                    sp.wait_ge(state_stored, 16 * CHUNKS * (layer + 1))
                    sp.wait_ge(g_zeros, layer + 1)
                    sp.dma_start(sums.rearrange("(p r) f -> p (r f)", p=P), agg[:, 0:NODES_PAD + DUMP_ROWS]).then_inc(g_cleared, 16)
                    sp.wait_ge(g_scattered, 16 * TILES * (layer + 1))
                    one_chunk(layer, 0, J)
                    with sp.Fori(1, LAST) as c:
                        one_chunk(layer, c, J)
                    one_chunk(layer, LAST, LAST_J)

            choose(sp, general, gathering, dense)
            sp.wait_ge(out_stored, 16 * CHUNKS)

        @block.gpsimd
        def _(pool):
            n_consts = [0]

            def const(instruction):
                n_consts[0] += 1
                instruction.then_inc(consts, 1)

            const(nc.gpsimd.iota(base_i, pattern=[[TILE_NODES, TILE_COLS]], base=-MARGIN, channel_multiplier=0))
            const(nc.gpsimd.iota(limits_i, pattern=[[SUB, ALL_SUBS + 1]], base=0, channel_multiplier=0))
            const(nc.gpsimd.iota(cols_i[:, :], pattern=[[1, TILE_WINDOW]], base=0, channel_multiplier=0))
            const(nc.gpsimd.iota(sub_base_i[:, :], pattern=[[SUB, SUBS], [0, SUB_TILES]], base=0, channel_multiplier=0))
            const(nc.gpsimd.iota(half_base_i[:, :], pattern=[[HALF, 2 * STRIPS]], base=0, channel_multiplier=0))
            const(nc.gpsimd.iota(dump_i[:, :], pattern=[[0, 1]], base=NODES_PAD, channel_multiplier=1))
            const(nc.gpsimd.memset(ones_all[:, :], 1.0))
            const(nc.gpsimd.memset(no_selection[:, :], 0.0))
            const(nc.gpsimd.memset(identity[:, :], 0.0))
            const(nc.gpsimd.memset(lower[:, :], 1.0))
            pool.wait_ge(consts, n_consts[0])
            const(nc.gpsimd.affine_select(out=identity[:, :], in_=identity[:, :], compare_op=ALU.not_equal, fill=1.0,
                                          base=0, pattern=[[-1, P]], channel_multiplier=1))
            const(nc.gpsimd.affine_select(out=lower[:, :], in_=lower[:, :], compare_op=ALU.is_gt, fill=0.0,
                                          base=0, pattern=[[-1, P]], channel_multiplier=1))
            assert n_consts[0] == N_CONSTS
            for at in range(0, KEYS, CHUNK):
                n = min(CHUNK, KEYS - at)
                wait(pool, key_taken, at // CHUNK)
                nc.gpsimd.iota(key_cols_i[:, 0:n].bitcast(I32), pattern=[[1, n]], base=at + 1, channel_multiplier=0).then_inc(key_iota, 1)

            def gather_half(k, c, half, steps):
                pool.wait_ge(src_staged, c * 2 + (k.half + half + 1))
                pool.sem_inc(turns[0], 1)
                for s in steps:
                    slot = s % SLOTS
                    wait(pool, summed, c * STEPS + (k.group + s - SLOTS + 1))
                    pool.sem_inc(turns[0], 1)
                    for t in range(tiles_of(c, s)):
                        at = s * GT + t
                        nc.gpsimd.indirect_dma_start(
                            messages[:, slot, t, :], None, table[k.layer % 2],
                            bass.IndirectOffsetOnAxis(ap=src_stage[:, at:at + 1], axis=0)).then_inc(gathered[slot], 16)

            def both_halves(k, c):
                gather_half(k, c, 0, range(SLOTS))
                gather_half(k, c, 1, range(SLOTS, STEPS))

            def tail(k):
                gather_half(k, LAST, 0, range(TAIL_GROUPS))

            def gathering(k, build):
                pool.wait_ge(table_stored, 16 * CHUNKS * (k.layer + 1))
                both_halves(k, 0)
                with pool.Fori(1, LAST) as c:
                    both_halves(k, c)
                tail(k)

            def dense(k):
                pool.wait_ge(table_stored, 16 * CHUNKS * (k.layer + 1))
                gather_half(k, DENSE_CHUNKS - 1, 1, [STEPS - 1])
                with pool.Fori(DENSE_CHUNKS, LAST) as c:
                    both_halves(k, c)
                tail(k)

            def general():
                def one_tile(layer, t):
                    wait(pool, g_scattered, 16 * (layer * TILES + t))
                    pool.sem_inc(turns[0], 1)
                    nc.gpsimd.tensor_copy(tile_src[:, :], src_all[:, bass.ds(t, 1)]).then_inc(g_src, 1)
                    pool.wait_ge(g_src, layer * TILES + t + 1)
                    pool.sem_inc(turns[0], 1)
                    nc.gpsimd.indirect_dma_start(tile_messages, None, table[layer % 2],
                                                 bass.IndirectOffsetOnAxis(ap=tile_src[:, 0:1], axis=0)).then_inc(g_gathered, 16)
                    pool.wait_ge(g_step, G_STEPS * (layer * TILES + t + 1))
                    pool.sem_inc(turns[0], 1)
                    nc.gpsimd.indirect_dma_start(sums, bass.IndirectOffsetOnAxis(ap=tile_index[:, 0:1], axis=0),
                                                 tile_sums, None, compute_op=ALU.add).then_inc(g_scattered, 16)

                for layer in range(LAYERS):
                    pool.wait_ge(table_stored, 16 * CHUNKS * (layer + 1))
                    pool.wait_ge(g_cleared, 16 * (layer + 1))
                    one_tile(layer, 0)
                    with pool.Fori(1, TILES) as t:
                        one_tile(layer, t)

            pool.wait_ge(loaded, 16 * N_LOADS)
            choose(pool, general, gathering, dense)

        def loads_of(k, c, odd):
            per = CHUNKS // 2 if odd else (CHUNKS + 1) // 2
            if isinstance(c, int):
                return 16 * ((k.layer - 1) * per + c // 2 + 1)
            return c * 8 + (16 * ((k.layer - 1) * per + 1) - 8 * odd)

        @block.scalar
        def _(act):
            for to, of in ((src_all[:, :], src), (w[:, :], weights), (b[:, :], biases), (b2_row[:, :], dec_b2)):
                act.dma_start(to, of).then_inc(loaded, 16)
            act.wait_ge(prep, PREP_STATS)
            nc.scalar.activation(ln_b[:, :], ln_b[:, :], ACT.Sqrt).then_inc(ln_std, 1)
            act.wait_ge(loaded, 16 * N_LOADS)

            def take_transposes(c, j):
                n = j * P
                act.wait_ge(transposed, c + 1)
                wait(act, enc1_done, c)
                nc.scalar.activation(xT[:, 0:n], tr_ps[:, 0:n], ACT.Relu).then_inc(xT_ready, 1)

            def take_first(c, j):
                n = j * P
                act.wait_ge(enc1_done, c + 1)
                wait(act, enc2_done, c)
                nc.scalar.activation(encT[:, 0:n], enc1_ps[:, 0:n], ACT.Relu,
                                     bias=b[:, B_ENC1:B_ENC1 + 1]).then_inc(encT_ready, 1)

            def take_second(c, j):
                n = j * P
                act.wait_ge(enc2_done, c + 1)
                wait(act, table_sum, c)
                wait(act, state_stored, c * 16)
                nc.scalar.activation(h_new[:, 0:n], enc2_ps[:, 0:n], ACT.Identity,
                                     bias=b[:, B_ENC2:B_ENC2 + 1]).then_inc(h0_ready, 1)

            in_stages(act, take_transposes, take_first, take_second, None)

            def gates(v, j):
                n = j * P
                act.wait_ge(gates_ps, 4 * v + 1)
                wait(act, gru, 5 * v)
                nc.scalar.activation(gate_r[:, 0:n], r_ps[:, 0:n], ACT.Sigmoid, bias=b_rz[:, R:R + 1]).then_inc(gates_rz, 1)
                act.wait_ge(gates_ps, 4 * v + 2)
                nc.scalar.activation(gate_z[:, 0:n], z_ps[:, 0:n], ACT.Sigmoid, bias=b_rz[:, Z:Z + 1]).then_inc(gates_rz, 1)

            def candidate(v, j):
                n = j * P
                act.wait_ge(gru, 5 * v + 2)
                nc.scalar.activation(gate_n[:, 0:n], pre_n[:, 0:n], ACT.Tanh, bias=b[:, B_IH + N:B_IH + N + 1]).then_inc(cand, 1)

            def make_table(v, c, j):
                n = j * P
                act.wait_ge(table_sum, v + (CHUNKS + 1))
                act.wait_ge(table_stored, 16 * (v + CHUNKS))
                nc.scalar.activation(table_stage[:, 0:n], table_ps[:, 0:n], ACT.Copy).then_inc(table_out, 1)

            def relu_state(v, c, j):
                n = j * P
                act.wait_ge(gru, 5 * v + 5)
                wait(act, dec1_done, c)
                nc.scalar.activation(relu_h[:, 0:n], h_new[:, 0:n], ACT.Relu).then_inc(relu_ready, 1)

            def relu_first(c, j):
                n = j * P
                act.wait_ge(dec1_done, c + 1)
                wait(act, dec2_done, c)
                nc.scalar.activation(decT[:, 0:n], table_ps[:, 0:n], ACT.Relu, bias=b[:, B_DEC1:B_DEC1 + 1]).then_inc(decT_ready, 1)

            def sigmoid_out(c, j):
                n = j * P
                act.wait_ge(dec_biased, c + 1)
                nc.scalar.activation(out_stage[:, 0:n], out_stage[:, 0:n], ACT.Sigmoid).then_inc(dec_sig, 1)

            def decode(v, c, j):
                relu_state(v, c, j)
                relu_first(c, j)
                sigmoid_out(c, j)

            def chunk(layer, v, c, j):
                gates(v, j)
                candidate(v, j)
                (make_table if layer < LAYERS - 1 else decode)(v, c, j)

            def all_chunks(layer):
                v = layer * CHUNKS
                chunk(layer, v, 0, J)
                with act.Fori(1, LAST) as c:
                    chunk(layer, c + v, c, J)
                chunk(layer, v + LAST, LAST, LAST_J)

            def count_edges(c, q):
                for i in range(PIECES):
                    n = (c * SUBS + q) * PIECES + i
                    a, e = PIECE_AT[i], PIECE_AT[i + 1]
                    act.wait_ge(built, n + 1)
                    act.sem_inc(turns[1], 1)
                    u, at = q // Q_SUBS, q % Q_SUBS * SUB
                    to = half_adj[:, u, :].rearrange("p (k d) -> p k d", d=QUARTER)[:, a:e, at:at + SUB]
                    nc.scalar.activation(to, build_ps[i % 2][:, 0:(e - a) * SUB].rearrange("p (k d) -> p k d", d=SUB),
                                         ACT.Copy, scale=COUNT_SCALE, saturate=False).then_inc(adj_out, 1)

            def gathering(k, build):
                if not build:
                    all_chunks(k.layer)
                    return

                def square(c, u, i):
                    n = BLOCKS * QUARTER // SQUARES
                    number = (c * 2 + u) * SQUARES + i
                    act.wait_ge(adj_out, (c * 2 + (u + 1)) * (Q_SUBS * PIECES))
                    wait(act, squares_used, c * 2 + (u - 1))
                    wait(act, adj_squared, number - (JUNKS - 1))
                    act.sem_inc(turns[1], 1)
                    at = i % JUNKS * n
                    nc.scalar.activation(junk[:, at:at + n], half_adj[:, u, i * n:(i + 1) * n], ACT.Square,
                                         accum_out=squares[:, u * SQUARES + i:u * SQUARES + i + 1]).then_inc(adj_squared, 1)

                def iteration(c):
                    q = 0
                    for s in range(STEPS):
                        for _ in range(1 + s % 2):
                            if q % Q_SUBS == 0 and not (isinstance(c, int) and c == 0):
                                u = q // Q_SUBS
                                act.wait_ge(adj_stored[u], c * 16)
                                act.wait_ge(adj_squared, c * (2 * SQUARES) + (u - 1) * SQUARES)
                                act.sem_inc(turns[1], 1)
                            count_edges(c, q)
                            q += 1
                            if q == Q_SUBS - 1 and not (isinstance(c, int) and c == 0):
                                candidate(c - 1 + k.v, J)
                        if s == 1 and not (isinstance(c, int) and c == 0):
                            gates(c - 1 + k.v, J)
                        if s == 4 and not (isinstance(c, int) and c == 0):
                            make_table(c - 1 + k.v, c - 1, J)
                        each = SQUARES // 4
                        for i in range(s % 4 * each, (s % 4 + 1) * each):
                            if s >= 4:
                                square(c, 0, i)
                            elif not (isinstance(c, int) and c == 0):
                                square(c - 1, 1, i)

                iteration(0)
                iteration(1)
                with act.Fori(2, LAST) as c:
                    iteration(c)
                for i in range(SQUARES):
                    square(LAST - 1, 1, i)
                for c, j in ((LAST - 1, J), (LAST, LAST_J)):
                    chunk(k.layer, k.v + c, c, j)

            def dense(k):
                def split(n, c, odd, j):
                    rows = bass.ds(c * J, j)
                    act.wait_ge(m_loaded[odd], loads_of(k, c, odd))
                    wait(act, part_used, (k.layer - 1) * STRIPS * PARTS)
                    nc.scalar.activation(parts[:, rows, 0, :], by_tile(m_in[odd], j), ACT.Copy).then_inc(split_act, 1)
                    act.wait_ge(split_dve, 2 * n + 1)
                    nc.scalar.activation(parts[:, rows, 1, :], by_tile(diff, j), ACT.Copy).then_inc(split_act, 1)

                if k.layer == 1:
                    act.sem_inc(strip_out, 1)
                n = (k.layer - 1) * CHUNKS
                with act.Fori(0, LAST // 2) as i:
                    split(i * 2 + n, i * 2, 0, J)
                    split(i * 2 + (n + 1), i * 2 + 1, 1, J)
                split(n + LAST, LAST, 0, LAST_J)
                def strip_sums(i):
                    act.wait_ge(part_used, (i + ((k.layer - 1) * STRIPS + 1)) * PARTS)
                    nc.scalar.activation(agg[:, bass.ds(i * STRIP + MARGIN, STRIP)], strip_ps[:, 0:STRIP], ACT.Copy,
                                         scale=1 / COUNT_SCALE).then_inc(strip_out, 1)

                last_layer = k.layer == LAYERS - 1

                def early(c):
                    chunk(k.layer, c + k.v, c, J)
                    strip_sums(c + LAG)

                with act.Fori(0, LAG) as i:
                    strip_sums(i)
                early_chunks(act, last_layer, early)

                def overlapped(v, c, j, next_j, first=False):
                    candidate(v, j)
                    if last_layer:
                        relu_state(v, c, j)
                        if not first:
                            sigmoid_out(c - 1, J)
                    if next_j:
                        gates(v + 1, next_j)
                    if last_layer:
                        relu_first(c, j)
                    else:
                        make_table(v, c, j)

                gates(k.v + EARLY, J)
                overlapped(k.v + EARLY, EARLY, J, J, first=True)
                with act.Fori(EARLY + 1, LAST - 1) as c:
                    overlapped(c + k.v, c, J, J)
                overlapped(k.v + LAST - 1, LAST - 1, J, LAST_J)
                overlapped(k.v + LAST, LAST, LAST_J, 0)
                if last_layer:
                    sigmoid_out(LAST, LAST_J)

            def general():
                for layer in range(LAYERS):
                    all_chunks(layer)

            choose(act, general, gathering, dense)

        @block.vector
        def _(dve):
            n_prep = [0]

            def done(instruction):
                n_prep[0] += 1
                instruction.then_inc(prep, 1)
                dve.wait_ge(prep, n_prep[0])

            dve.wait_ge(edges_loaded, 16 * N_EDGE_LOADS)
            dve.wait_ge(consts, N_CONSTS)
            ops = nc.vector
            done(ops.tensor_copy(cols_f[:, :], cols_i[:, :]))
            done(ops.tensor_copy(dump[:, :], dump_i[:, :]))
            done(ops.tensor_copy(sub_base[:, :], sub_base_i[:, :]))
            done(ops.tensor_copy(half_base[:, :], half_base_i[:, :]))
            done(ops.tensor_copy(base_f, base_i))
            done(ops.tensor_copy(info[:, :, 0], dst_all))
            done(ops.tensor_copy(first_f[:, :], first_i[:, :]))
            done(ops.tensor_copy(limits, limits_i))
            assert n_prep[0] == PREP_LIMITS
            for i in range(FIRST_COLS):
                wait(dve, limit_sum, i - 1)
                ops.tensor_scalar(before_limit[i % 2], limits, first_f[:, i:i + 1], None, ALU.is_gt).then_inc(hot_limits, 1)
            done(ops.tensor_tensor(dst_rel[:, :], info[:, :, 0], base_f, ALU.subtract))
            done(ops.tensor_reduce(outside[:, 0:1], dst_rel[:, 0:TILES], AX_X, ALU.min))
            done(ops.tensor_reduce(outside[:, 1:2], dst_rel[:, 0:TILES], AX_X, ALU.max))
            done(ops.tensor_scalar(outside[:, 0:1], outside[:, 0:1], 0.0, None, ALU.is_lt))
            done(ops.tensor_scalar(outside[:, 1:2], outside[:, 1:2], float(TILE_WINDOW - 1), None, ALU.is_gt))
            assert n_prep[0] == PREP_OUTSIDE
            dve.wait_ge(prep_sum, 1)
            ops.tensor_copy(n_outside[:, :], table_ps[0:1, 0:1]).then_inc(n_ready, 1)
            done(ops.tensor_tensor(base_f, info[:, :, 0], dst_next_all, ALU.is_gt))
            done(ops.tensor_reduce(irregular[:, 0:1], base_f, AX_X, ALU.max))

            for i, at in enumerate(range(0, KEYS, CHUNK)):
                n = min(CHUNK, KEYS - at)
                dve.wait_ge(key_iota, i + 1)
                ops.tensor_copy(key_cols[:, at:at + n], key_cols_i[:, 0:n].bitcast(I32)).then_inc(key_taken, 1)
            dve.wait_ge(loaded, 16 * N_LOADS)
            done(ops.tensor_scalar(tmp_i, src_all[:, :], 7, None, ALU.arith_shift_right))
            done(ops.tensor_scalar(info[:, :, 1], tmp_i, float(SUB), 1.0, ALU.mult, ALU.add))
            done(ops.tensor_scalar(tmp_i, src_all[:, :], P - 1, None, ALU.bitwise_and))
            done(ops.tensor_copy(info[:, :, 2], tmp_i))
            dve.wait_ge(prep_sum, 2)
            done(ops.tensor_copy(start_f, agg_ps[0][0:1, 0:ALL_SUBS + 1]))
            done(ops.tensor_scalar(start_of, start_f, -1.0, 0.0, ALU.add, ALU.max))
            done(ops.tensor_copy(start_i[:, :], start_of))
            done(ops.memset(irregular[:, 1:3], 0.0))
            done(ops.tensor_tensor(start_f[0:1, 0:ALL_SUBS], start_f[0:1, 1:ALL_SUBS + 1], start_of[0:1, 0:ALL_SUBS], ALU.subtract))
            done(ops.tensor_reduce(irregular[0:1, 1:2], start_f[0:1, 0:ALL_SUBS], AX_X, ALU.max))
            done(ops.tensor_scalar(irregular[0:1, 1:2], irregular[0:1, 1:2], float(SUB_TILES), None, ALU.is_gt))
            done(ops.memset(squares_max, 0.0))
            assert n_prep[0] == PREP_BUILD
            done(ops.tensor_tensor(b_rz[:, :], b[:, B_IH:B_IH + 2], b[:, B_HH:B_HH + 2], ALU.add))
            dve.wait_ge(prep_sum, 3)
            done(ops.tensor_copy(b2_all[:, :], dec_ps[:, 0:H]))

            def stats_of(c, j):
                for t in range(j):
                    last = ops.bn_stats(stats[:, bass.ds(c * J + t, 1), :].rearrange("p a s -> p (a s)"),
                                        x_rows[:, bass.ds(c * CHUNK + t * H, H)])
                return last

            for i in range(X_PARTS):
                dve.wait_ge(x_loaded[i], 16)
                with dve.Fori(X_AT[i] // 2, X_AT[i + 1] // 2) as pair:
                    stats_of(pair * 2, J)
                    stats_of(pair * 2 + 1, J)
            done(stats_of(LAST, LAST_J))
            m_even, m_odd, v_even, v_odd = (stats[:, :, i] for i in (1, 4, 2, 5))
            done(ops.tensor_tensor(ln_a[:, :], m_even, m_odd, ALU.subtract))
            done(ops.tensor_tensor(mean[:, :], m_even, m_odd, ALU.add))
            done(ops.tensor_scalar(mean[:, :], mean[:, :], 0.5, None, ALU.mult))
            done(ops.tensor_tensor(ln_a[:, :], ln_a[:, :], ln_a[:, :], ALU.mult))
            done(ops.tensor_tensor(ln_b[:, :], v_even, v_odd, ALU.add))
            done(ops.tensor_scalar(ln_b[:, :], ln_b[:, :], 1.0 / H, EPS, ALU.mult, ALU.add))
            done(ops.scalar_tensor_tensor(out=ln_b[:, :], in0=ln_a[:, :], scalar=0.25, in1=ln_b[:, :],
                                          op0=ALU.mult, op1=ALU.add))
            assert n_prep[0] == PREP_STATS
            dve.wait_ge(ln_std, 1)
            done(ops.reciprocal(rstd[:, :], ln_b[:, :]))

            def normalize(c, j):
                wait(dve, transposed, c)
                for t in range(j):
                    at = c * J + t
                    one = bass.ds(at, 1)
                    last = ops.tensor_scalar(x_norm[:, t * H:(t + 1) * H], x_rows[:, bass.ds(at * H, H)],
                                             mean[:, one], rstd[:, one], ALU.subtract, ALU.mult)
                last.then_inc(normed, 1)

            def first_table(c, j):
                n = j * P
                dve.wait_ge(table_sum, c + 1)
                wait(dve, table_stored, c * 16)
                ops.tensor_copy(table_stage[:, 0:n], table_ps[:, 0:n]).then_inc(table_out, 1)

            in_stages(dve, normalize, None, None, first_table)

            def stage(k, c):
                wait(dve, selected, c * STEPS + k.group)
                ops.tensor_copy(dst_stage[:, :], dst_rel[:, bass.ds(c * ITER_TILES, ITER_TILES)]).then_inc(dst_staged, 1)
                dve.wait_ge(dst_staged, c + (k.iteration + 1))

            def select(k, c, s):
                wait(dve, summed, c * STEPS + (k.group + s - 1))
                for t in range(tiles_of(c, s)):
                    at = s * GT + t
                    last = ops.tensor_scalar(selection[:, s % 2, t, :], cols_f[:, :], dst_stage[:, at:at + 1], None,
                                             ALU.is_equal)
                last.then_inc(selected, 1)

            def select_next(k, c, s, end):
                if s + 1 < STEPS:
                    if not (isinstance(c, int) and c == LAST and s + 1 >= end):
                        select(k, c, s + 1)
                else:
                    stage(k, c + 1)
                    select(k, c + 1, 0)

            def stage_src(c, half):
                n = SLOTS * GT
                at = half * n
                ops.tensor_copy(src_stage[:, at:at + n], src_all[:, bass.ds(c * ITER_TILES + at, n)]).then_inc(src_staged, 1)

            def add(k, c, s, first=False):
                at = c * CHUNK + s * GROUP_NODES
                g = c * STEPS + (k.group + s)
                part = agg_ps[s % 2]
                dve.wait_ge(summed, g + 1)
                wait(dve, agg_added, 2 * g)
                cols = agg[:, bass.ds(at, OLD)]
                if first:
                    ops.tensor_copy(cols, part[:, 0:OLD]).then_inc(agg_added, 1)
                else:
                    ops.tensor_tensor(cols, cols, part[:, 0:OLD], ALU.add).then_inc(agg_added, 1)
                ops.tensor_copy(agg[:, bass.ds(at + OLD, GROUP_NODES)], part[:, OLD:WINDOW]).then_inc(agg_added, 1)
                if (s + 1) % SLOTS == 0 and not (isinstance(c, int) and c == LAST):
                    stage_src(c + 1, s // SLOTS)

            def gru_step(layer, v, j, h, i_n):
                before_candidate(v, j, i_n)
                after_candidate(layer, v, j, h)

            def before_candidate(v, j, i_n):
                n = j * P
                dve.wait_ge(gates_rz, 2 * v + 1)
                dve.wait_ge(gates_ps, 4 * v + 3)
                wait(dve, cand, v)
                ops.scalar_tensor_tensor(out=pre_n[:, 0:n], in0=hn_ps[:, 0:n], scalar=b[:, B_HH + N:B_HH + N + 1],
                                         in1=gate_r[:, 0:n], op0=ALU.add, op1=ALU.mult).then_inc(gru, 1)
                dve.wait_ge(gru, 5 * v + 1)
                dve.wait_ge(gates_ps, 4 * v + 4)
                ops.tensor_tensor(pre_n[:, 0:n], pre_n[:, 0:n], i_n[:, 0:n], ALU.add).then_inc(gru, 1)

            def after_candidate(layer, v, j, h):
                n = j * P
                dve.wait_ge(cand, v + 1)
                if layer == LAYERS - 1:
                    wait(dve, dec2_done, v - layer * CHUNKS)
                ops.tensor_tensor(diff[:, 0:n], h[:, 0:n], gate_n[:, 0:n], ALU.subtract).then_inc(gru, 1)
                dve.wait_ge(gru, 5 * v + 3)
                dve.wait_ge(gates_rz, 2 * v + 2)
                ops.tensor_tensor(diff[:, 0:n], diff[:, 0:n], gate_z[:, 0:n], ALU.mult).then_inc(gru, 1)
                dve.wait_ge(gru, 5 * v + 4)
                if layer < LAYERS - 1:
                    dve.wait_ge(table_sum, v + CHUNKS)
                    dve.wait_ge(state_stored, 16 * (v + CHUNKS))
                else:
                    dve.wait_ge(state_stored, 16 * CHUNKS * LAYERS)
                    dve.wait_ge(table_sum, CHUNKS * LAYERS)
                    wait(dve, relu_ready, v - layer * CHUNKS)
                ops.tensor_tensor(h_new[:, 0:n], diff[:, 0:n], gate_n[:, 0:n], ALU.add).then_inc(gru, 1)

            def decode(c, j):
                n = j * P
                dve.wait_ge(dec2_done, c + 1)
                wait(dve, out_stored, 16 * c)
                b2 = b2_all[:, :].rearrange("p (a f) -> p a f", a=1).broadcast_to([P, j, H])
                ops.tensor_tensor(by_tile(out_stage, j), by_tile(dec_ps, j), b2, ALU.add).then_inc(dec_biased, 1)
                dve.wait_ge(dec_sig, c + 1)
                dve.wait_ge(x_again, 16 * (c + 1))
                ops.tensor_tensor(out_stage[:, 0:n], out_stage[:, 0:n], x_stage[:, 0:n], ALU.add).then_inc(out_ready, 1)

            def keys(c, u):
                step = (c * 2 + u) * KEY_STEPS
                at = slice(u * Q_SUBS * SUB_TILES, (u + 1) * Q_SUBS * SUB_TILES)
                dve.wait_ge(picked_loaded[u], (c + 1) * (16 * Q_SUBS))
                wait(dve, hot, c * SUBS)
                ops.scalar_tensor_tensor(out=sub_u[:, at], in0=picked_v[:, at, 0], scalar=half_base[:, bass.ds(c, 1)],
                                         in1=sub_base[:, at], op0=ALU.subtract, op1=ALU.subtract).then_inc(keyed, 1)
                dve.wait_ge(keyed, step + 1)
                ops.tensor_scalar(sub_in[:, at], sub_u[:, at], 0.0, None, ALU.is_ge).then_inc(keyed, 1)
                dve.wait_ge(keyed, step + 2)
                ops.scalar_tensor_tensor(out=sub_in[:, at], in0=sub_u[:, at], scalar=float(SUB), in1=sub_in[:, at],
                                         op0=ALU.is_lt, op1=ALU.mult).then_inc(keyed, 1)
                dve.wait_ge(keyed, step + 3)
                ops.tensor_tensor(sub_u[:, at], sub_u[:, at], picked_v[:, at, 1], ALU.add).then_inc(keyed, 1)
                dve.wait_ge(keyed, step + 4)
                ops.tensor_tensor(sub_key[:, at], sub_u[:, at], sub_in[:, at], ALU.mult).then_inc(keyed, 1)
                dve.wait_ge(keyed, step + KEY_STEPS)

            def one_hot(c, q):
                wait(dve, built, (c * SUBS + (q - 1)) * PIECES)
                for t in range(SUB_TILES):
                    at = q * SUB_TILES + t
                    ops.tensor_scalar(key_hot[:, q % 2, t, :], key_cols, sub_key[:, at:at + 1], None, ALU.is_equal)
                    last = ops.tensor_scalar(low_hot[:, q % 2, t, :], cols_f[:, 0:P], picked_v[:, at, 2:3], None, ALU.is_equal)
                last.then_inc(hot, 1)

            def bound(c, u):
                dve.wait_ge(adj_squared, (c * 2 + (u + 1)) * SQUARES)
                ops.tensor_tensor(squares_max, squares_max, squares[:, u * SQUARES:(u + 1) * SQUARES], ALU.max).then_inc(squares_used, 1)
                dve.wait_ge(squares_used, c * 2 + (u + 1))

            def gathering(k, build):
                last_layer = k.layer == LAYERS - 1

                def iteration(c, steps):
                    before = not (isinstance(c, int) and c == 0)
                    building = build and not (isinstance(c, int) and c == LAST)
                    v = c + (k.v - 1)
                    q = 0
                    for s in range(steps):
                        if building:
                            for _ in range(1 + s % 2):
                                if q % Q_SUBS == 0:
                                    keys(c, q // Q_SUBS)
                                one_hot(c, q)
                                q += 1
                        if before and build and s == 1:
                            bound(c - 1, 0)
                        select_next(k, c, s, steps)
                        add(k, c, s, first=not before and s == 0)
                        if before and s == 2:
                            before_candidate(v, J, r_ps)
                        if before and s == 3:
                            after_candidate(k.layer, v, J, h_old[0])
                        if before and last_layer and s == min(5, steps - 1):
                            decode(c - 1, J)
                        if before and building and s == 6:
                            bound(c - 1, 1)

                stage_src(0, 0)
                stage_src(0, 1)
                stage(k, 0)
                select(k, 0, 0)
                iteration(0, STEPS)
                iteration(1, STEPS)
                with dve.Fori(2, LAST) as c:
                    iteration(c, STEPS)
                iteration(LAST, TAIL_GROUPS)
                if build:
                    bound(LAST - 1, 1)
                    ops.tensor_reduce(irregular[:, 2:3], squares_max, AX_X, ALU.max).then_inc(regular_sum, 1)
                    dve.wait_ge(regular_sum, 1)
                    ops.tensor_scalar(irregular[:, 2:3], irregular[:, 2:3], SQUARES_LIMIT, None, ALU.is_ge).then_inc(regular_sum, 1)
                gru_step(k.layer, k.v + LAST, LAST_J, h_old[0], r_ps)
                if build:
                    dve.wait_ge(regular_sum, 3)
                    ops.tensor_copy(n_irregular[:, :], agg_ps[0][0:1, 0:1]).then_inc(regular_ready, 1)
                if last_layer:
                    decode(LAST, LAST_J)

            def dense(k):
                layer = k.layer
                last_layer = layer == LAYERS - 1

                def split(c, j):
                    n = (layer - 1) * CHUNKS + c
                    rows = slice(c * J, c * J + j)
                    dve.wait_ge(split_act, 2 * n + 1)
                    wait(dve, split_dve, 2 * n)
                    ops.tensor_tensor(by_tile(diff, j), by_tile(m_in[c % 2], j), parts[:, rows, 0, :], ALU.subtract).then_inc(split_dve, 1)
                    dve.wait_ge(split_dve, 2 * n + 1)
                    dve.wait_ge(split_act, 2 * n + 2)
                    ops.tensor_tensor(parts[:, rows, 2, :], by_tile(diff, j), parts[:, rows, 1, :], ALU.subtract).then_inc(split_dve, 1)

                c0 = DENSE_CHUNKS
                stage_src(c0 - 1, 1)
                stage_src(c0, 0)
                stage(k, c0 - 1)
                select(k, c0 - 1, STEPS - 1)
                select_next(k, c0 - 1, STEPS - 1, STEPS)
                each = -(-CHUNKS // (PARTS - 1))
                for s in range(STEPS):
                    for c in range(s * each, min(CHUNKS, (s + 1) * each)):
                        split(c, J if c < LAST else LAST_J)
                    if s == 0:
                        add(k, c0 - 1, STEPS - 1, first=True)
                    select_next(k, c0, s, STEPS)
                    add(k, c0, s)
                if LAG > 1:
                    with dve.Fori(c0 + 1, c0 + LAG) as c:
                        for s in range(STEPS):
                            select_next(k, c, s, STEPS)
                            add(k, c, s)
                def early(chunk):
                    c = chunk + (c0 + LAG)
                    for s in range(STEPS):
                        select_next(k, c, s, STEPS)
                        add(k, c, s)
                        if s == 2:
                            gru_step(layer, chunk + k.v, J, h_old[0], r_ps)
                        if s == 6 and last_layer:
                            decode(chunk, J)

                early_chunks(dve, last_layer, early)

                def late(c, j, buffer, first=False):
                    gru_step(layer, c + k.v, j, h_old[buffer], in_ps)
                    if last_layer and not first:
                        decode(c - 1, J)

                def burst(c, start, groups, first=False):
                    for s in range(STEPS):
                        select_next(k, c, s, STEPS)
                        add(k, c, s)
                        if s in groups:
                            t = groups.index(s)
                            late(start + t, J, t % 2, first=first and t == 0)

                n = len(BURST_GROUPS)
                if BURSTS > 0:
                    burst(BURST, EARLY, BURST_GROUPS, first=True)
                if BURSTS > 1:
                    with dve.Fori(1, BURSTS) as i:
                        burst(i + BURST, i * n + EARLY, BURST_GROUPS)
                burst(LAST - 1, EARLY + BURSTS * n, tuple(range(REST)), first=BURSTS == 0)
                for s in range(TAIL_GROUPS):
                    if s != 2:
                        select_next(k, LAST, s, TAIL_GROUPS)
                    add(k, LAST, s)
                    if s == 1:
                        select_next(k, LAST, 2, TAIL_GROUPS)
                        late(LAST - 1, J, 1)
                late(LAST, LAST_J, 0)
                if last_layer:
                    decode(LAST, LAST_J)

            def general():
                def one_tile(layer, t):
                    number = layer * TILES + t
                    g = G_STEPS * number
                    wait(dve, g_scattered, 16 * number)
                    ops.tensor_copy(tile_dst[:, :], edge_info[:, bass.ds(t * 3, 1)]).then_inc(g_step, 1)
                    dve.wait_ge(g_step, g + 1)
                    ops.tensor_scalar(tile_diag, identity[:, :], tile_dst[:, :], None, ALU.mult).then_inc(g_step, 1)
                    dve.wait_ge(g_product, 2 * number + 1)
                    ops.tensor_scalar(tile_equal, agg_ps[0][:, 0:P], tile_dst[:, :], None, ALU.is_equal).then_inc(g_step, 1)
                    dve.wait_ge(g_step, g + 3)
                    ops.tensor_tensor(tile_before, tile_equal, lower[:, :], ALU.mult).then_inc(g_step, 1)
                    dve.wait_ge(g_step, g + 4)
                    ops.tensor_reduce(tile_dup[:, :], tile_before, AX_X, ALU.add).then_inc(g_step, 1)
                    dve.wait_ge(g_step, g + 5)
                    ops.tensor_scalar(tile_dup[:, :], tile_dup[:, :], 0.0, None, ALU.is_gt).then_inc(g_step, 1)
                    ops.tensor_tensor(tile_row[:, :], dump[:, :], tile_dst[:, :], ALU.subtract).then_inc(g_step, 1)
                    dve.wait_ge(g_step, g + 7)
                    ops.tensor_tensor(tile_row[:, :], tile_row[:, :], tile_dup[:, :], ALU.mult).then_inc(g_step, 1)
                    dve.wait_ge(g_step, g + 8)
                    ops.tensor_tensor(tile_index[:, :], tile_row[:, :], tile_dst[:, :], ALU.add).then_inc(g_step, 1)
                    dve.wait_ge(g_product, 2 * number + 2)
                    ops.tensor_copy(tile_sums, agg_ps[1][:, 0:H]).then_inc(g_step, 1)

                def one_chunk(layer, c, j):
                    n = j * P
                    v = layer * CHUNKS + c
                    dve.wait_ge(g_turned, v + 1)
                    ops.tensor_copy(agg[:, bass.ds(c * CHUNK + MARGIN, n)], agg_ps[0][:, 0:n]).then_inc(g_agg, 1)
                    gru_step(layer, v, j, h_old[0], r_ps)
                    if layer == LAYERS - 1:
                        decode(c, j)

                for layer in range(LAYERS):
                    ops.memset(agg[:, :], 0.0).then_inc(g_zeros, 1)
                    dve.wait_ge(g_cleared, 16 * (layer + 1))
                    one_tile(layer, 0)
                    with dve.Fori(1, TILES) as t:
                        one_tile(layer, t)
                    one_chunk(layer, 0, J)
                    with dve.Fori(1, LAST) as c:
                        one_chunk(layer, c, J)
                    one_chunk(layer, LAST, LAST_J)

            choose(dve, general, gathering, dense)

        @block.tensor
        def _(pe):
            mm = nc.tensor.matmul
            pe.wait_ge(consts, N_CONSTS)
            for i in range(FIRST_COLS):
                pe.wait_ge(hot_limits, i + 1)
                last = mm(agg_ps[0][0:1, 0:ALL_SUBS + 1], ones_all[:, 0:1], before_limit[i % 2],
                          start=(i == 0), stop=(i == FIRST_COLS - 1)).then_inc(limit_sum, 1)
            pe.wait_ge(prep, PREP_OUTSIDE)
            mm(table_ps[0:1, 0:1], outside[:, 0:1], ones_all[:, 0:1], start=True, stop=False)
            mm(table_ps[0:1, 0:1], outside[:, 1:2], ones_all[:, 0:1], start=False, stop=True).then_inc(prep_sum, 1)
            mm(agg_ps[1][0:1, 0:1], ones_all[:, 0:1], ones_all[:, 0:1], start=True, stop=True).then_inc(prep_sum, 1)
            pe.wait_ge(loaded, 16 * N_LOADS)
            mm(dec_ps[:, 0:H], ones_all[0:1, :], b2_row[:, :], start=True, stop=True).then_inc(prep_sum, 1)

            def rows_of(target, lhs, weight, j):
                for t in range(j):
                    last = mm(target[:, t * H:(t + 1) * H], lhs[:, t * P:(t + 1) * P], weight, start=True, stop=True)
                return last

            def transposes(c, j):
                pe.wait_ge(normed, c + 1)
                wait(pe, xT_ready, c)
                for t in range(j):
                    last = nc.tensor.transpose(tr_ps[:, t * P:(t + 1) * P], x_norm[:, t * H:(t + 1) * H], identity[:, :])
                last.then_inc(transposed, 1)

            def first_product(c, j):
                n = j * P
                pe.wait_ge(xT_ready, c + 1)
                wait(pe, encT_ready, c)
                mm(enc1_ps[:, 0:n], wblock(W_ENC1), xT[:, 0:n], start=True, stop=True).then_inc(enc1_done, 1)

            def second_product(c, j):
                n = j * P
                pe.wait_ge(encT_ready, c + 1)
                wait(pe, h0_ready, c)
                mm(enc2_ps[:, 0:n], wblock(W_ENC2), encT[:, 0:n], start=True, stop=True).then_inc(enc2_done, 1)

            def first_table(c, j):
                pe.wait_ge(h0_ready, c + 1)
                wait(pe, table_out, c)
                rows_of(table_ps, h_new, wblock(W_CONV), j).then_inc(table_sum, 1)

            in_stages(pe, transposes, first_product, second_product, first_table)

            def sum_group(k, c, s):
                g = c * STEPS + (k.group + s)
                slot = s % SLOTS
                n_tiles = tiles_of(c, s)
                pe.wait_ge(gathered[slot], k.gathered(c, s))
                pe.wait_ge(selected, g + 1)
                wait(pe, agg_added, 2 * (g - 1))
                for t in range(n_tiles):
                    at = t * TILE_NODES
                    last = mm(agg_ps[s % 2][:, at:at + TILE_WINDOW], messages[:, slot, t, :], selection[:, s % 2, t, :],
                              start=(t == 0), stop=(t == n_tiles - 1), skip_group_check=True)
                if n_tiles < GT:
                    at = n_tiles * TILE_NODES
                    last = mm(agg_ps[s % 2][:, at + MARGIN:WINDOW], messages[:, slot, 0, :], no_selection[:, at + MARGIN:WINDOW],
                              start=False, stop=True, skip_group_check=True)
                last.then_inc(summed, 1)

            def gates(v, c, j, complete, h, h_ready, in_bank, later=False, alone=True):
                n = j * P
                a = agg[:, bass.ds(c * CHUNK + MARGIN, n)]
                pe.wait_ge(*h_ready)
                wait(pe, gates_rz, 2 * v)
                if alone:
                    wait(pe, cand, v)
                for gate, bank in ((R, r_ps), (Z, z_ps)):
                    mm(bank[:, 0:n], wblock(W_HH + gate), h[:, 0:n], start=True, stop=False)
                pe.wait_ge(*complete)
                for gate, bank in ((R, r_ps), (Z, z_ps)):
                    mm(bank[:, 0:n], wblock(W_IH + gate), a, start=False, stop=True).then_inc(gates_ps, 1)
                if not alone:
                    wait(pe, cand, v)
                mm(hn_ps[:, 0:n], wblock(W_HH + N), h[:, 0:n], start=True, stop=True).then_inc(gates_ps, 1)
                if not later:
                    gate_n_input(v, c, j, in_bank)

            def gate_n_input(v, c, j, in_bank):
                n = j * P
                a = agg[:, bass.ds(c * CHUNK + MARGIN, n)]
                if in_bank is r_ps:
                    pe.wait_ge(gates_rz, 2 * v + 1)
                mm(in_bank[:, 0:n], wblock(W_IH + N), a, start=True, stop=True).then_inc(gates_ps, 1)

            def make_table(layer, v, c, j):
                pe.wait_ge(gru, 5 * v + 5)
                pe.wait_ge(table_out, v + CHUNKS)
                rows_of(table_ps, h_new, wblock(W_CONV + layer + 1), j).then_inc(table_sum, 1)

            def decode_first(c, j):
                n = j * P
                pe.wait_ge(relu_ready, c + 1)
                wait(pe, decT_ready, c)
                mm(table_ps[:, 0:n], wblock(W_DEC1), relu_h[:, 0:n], start=True, stop=True).then_inc(dec1_done, 1)

            def decode_second(c, j):
                pe.wait_ge(decT_ready, c + 1)
                wait(pe, dec_biased, c)
                rows_of(dec_ps, decT, wblock(W_DEC2), j).then_inc(dec2_done, 1)

            def finish(layer, v, c, j):
                if layer < LAYERS - 1:
                    make_table(layer, v, c, j)
                else:
                    decode_first(c, j)
                    decode_second(c, j)

            def build_counts(c, q):
                pe.wait_ge(hot, c * SUBS + (q + 1))
                for i in range(PIECES):
                    n = (c * SUBS + q) * PIECES + i
                    a, e = PIECE_AT[i] * SUB, PIECE_AT[i + 1] * SUB
                    wait(pe, adj_out, n - 1)
                    for t in range(SUB_TILES):
                        last = mm(build_ps[i % 2][:, 0:e - a], low_hot[:, q % 2, t, :], key_hot[:, q % 2, t, a:e],
                                  start=(t == 0), stop=(t == SUB_TILES - 1))
                    last.then_inc(built, 1)

            def gathering(k, build):
                def iteration(c, steps):
                    before = not (isinstance(c, int) and c == 0)
                    building = build and not (isinstance(c, int) and c == LAST)
                    v = c + (k.v - 1)
                    q = 0
                    for s in range(steps):
                        sum_group(k, c, s)
                        if before and s == 2:
                            gate_n_input(v, c - 1, J, r_ps)
                        if building:
                            for _ in range(1 + s % 2):
                                build_counts(c, q)
                                q += 1
                        if before and s == 1:
                            gates(v, c - 1, J, (agg_added, 2 * (c * STEPS) + 2 * (k.group + 1)),
                                  h_old[0], (h_loaded[0], 16 * (v + 1)), r_ps, later=True)
                        if before and s == min(4, steps - 1):
                            finish(k.layer, v, c - 1, J)

                iteration(0, STEPS)
                iteration(1, STEPS)
                with pe.Fori(2, LAST) as c:
                    iteration(c, STEPS)
                iteration(LAST, TAIL_GROUPS)
                v = k.v + LAST
                gates(v, LAST, LAST_J, (agg_added, 2 * (k.group + GROUPS)), h_old[0], (h_loaded[0], 16 * (v + 1)), r_ps)
                if build:
                    pe.wait_ge(regular_sum, 2)
                    for i in range(3):
                        last = mm(agg_ps[0][0:1, 0:1], irregular[:, i:i + 1], ones_all[:, 0:1], start=(i == 0), stop=(i == 2))
                    last.then_inc(regular_sum, 1)
                finish(k.layer, v, LAST, LAST_J)

            def dense(k):
                layer = k.layer
                last_layer = layer == LAYERS - 1

                def sum_strip(i, p):
                    n = (layer - 1) * STRIPS * PARTS + i * PARTS + p
                    a, e = PART_AT[p], PART_AT[p + 1]
                    pe.wait_ge(part_loaded[p % 2], 16 * ((layer - 1) * STRIPS * PARTS // 2 + p // 2 + 1) + i * (16 * PARTS // 2))
                    pe.wait_ge(split_dve, 2 * ((layer - 1) * CHUNKS + -(-e // J)))
                    if p == 0:
                        pe.wait_ge(strip_out, i + ((layer - 1) * STRIPS + 1))
                        pe.wait_ge(gru, 5 * k.v)
                    pe.sem_inc(turns[2], 1)
                    for block in range(a, e):
                        counts = strip_part[:, p % 2, :, (block - a) * QUARTER:(block - a + 1) * QUARTER]
                        for part in range(SPLITS):
                            last = mm(strip_ps[:, 0:STRIP].rearrange("f (h d) -> f h d", h=4), parts[:, block, part, :], counts,
                                      start=(block == 0 and part == 0), stop=(block == BLOCKS - 1 and part == SPLITS - 1))
                    last.then_inc(part_used, 1)

                def chunk_gates(c, j, buffer, complete, alone=False):
                    gates(c + k.v, c, j, complete, h_old[buffer], (h_loaded[buffer], old_loads(k, c, buffer)), in_ps,
                          alone=alone)

                def after(c):
                    return (agg_added, 2 * (c * STEPS) + 2 * (k.group + 1))

                sum_group(k, DENSE_CHUNKS - 1, STEPS - 1)
                with pe.Fori(0, LAG) as i:
                    for s in range(STEPS):
                        sum_group(k, i + DENSE_CHUNKS, s)
                        sum_strip(i, s)
                def early(c):
                    for s in range(STEPS):
                        sum_group(k, c + (DENSE_CHUNKS + LAG), s)
                        if s == 1:
                            gates(c + k.v, c, J, (strip_out, c + ((layer - 1) * STRIPS + LAG + 1)), h_old[0],
                                  (h_loaded[0], early_loads(k, c)), r_ps, later=True)
                        if s == 2:
                            gate_n_input(c + k.v, c, J, r_ps)
                        if s == 4:
                            if last_layer:
                                decode_first(c, J)
                            else:
                                make_table(layer, c + k.v, c, J)
                        if s == 5 and last_layer:
                            decode_second(c, J)
                        sum_strip(c + LAG, s)

                early_chunks(pe, last_layer, early)
                chunk_gates(EARLY, J, 0, (strip_out, layer * STRIPS + 1), alone=True)

                def late(c, j, buffer, first=False, gates_of=None):
                    if last_layer and not first:
                        decode_second(c - 1, J)
                    if gates_of is not None:
                        chunk_gates(c + 1, J, 1 - buffer, after(gates_of))
                    if last_layer:
                        decode_first(c, j)
                    else:
                        make_table(layer, c + k.v, c, j)

                def burst(c, start, groups, first=False, last=False):
                    for s in range(STEPS):
                        sum_group(k, c, s)
                        if s in groups:
                            t = groups.index(s)
                            more = not (last and t == len(groups) - 1)
                            late(start + t, J, t % 2, first=first and t == 0, gates_of=c if more else None)

                n = len(BURST_GROUPS)
                if BURSTS > 0:
                    burst(BURST, EARLY, BURST_GROUPS, first=True)
                if BURSTS > 1:
                    with pe.Fori(1, BURSTS) as i:
                        burst(i + BURST, i * n + EARLY, BURST_GROUPS)
                burst(LAST - 1, EARLY + BURSTS * n, tuple(range(REST)), first=BURSTS == 0, last=True)
                for s in range(TAIL_GROUPS):
                    sum_group(k, LAST, s)
                    if s == 1:
                        chunk_gates(LAST - 1, J, 1, after(LAST))
                        if last_layer:
                            decode_second(LAST - 2, J)
                chunk_gates(LAST, LAST_J, 0, (agg_added, 2 * (k.group + GROUPS)))
                if last_layer:
                    decode_first(LAST - 1, J)
                else:
                    make_table(layer, k.v + LAST - 1, LAST - 1, J)
                late(LAST, LAST_J, 0)
                if last_layer:
                    decode_second(LAST, LAST_J)

            def general():
                def one_tile(layer, t):
                    number = layer * TILES + t
                    pe.wait_ge(g_step, G_STEPS * number + 2)
                    mm(agg_ps[0][:, 0:P], ones_all[:, :], tile_diag, start=True, stop=True).then_inc(g_product, 1)
                    pe.wait_ge(g_step, G_STEPS * number + 3)
                    pe.wait_ge(g_gathered, 16 * (number + 1))
                    mm(agg_ps[1][:, 0:H], tile_equal, tile_messages, start=True, stop=True).then_inc(g_product, 1)

                def one_chunk(layer, c, j):
                    v = layer * CHUNKS + c
                    pe.wait_ge(g_rows, 16 * (v + 1))
                    wait(pe, g_agg, v)
                    for t in range(j):
                        last = nc.tensor.transpose(agg_ps[0][:, t * P:(t + 1) * P], sum_rows[:, t * H:(t + 1) * H], identity[:, :])
                    last.then_inc(g_turned, 1)
                    gates(v, c, j, (g_agg, v + 1), h_old[0], (h_loaded[0], 16 * (v + 1)), r_ps)
                    finish(layer, v, c, j)

                for layer in range(LAYERS):
                    one_tile(layer, 0)
                    with pe.Fori(1, TILES) as t:
                        one_tile(layer, t)
                    one_chunk(layer, 0, J)
                    with pe.Fori(1, LAST) as c:
                        one_chunk(layer, c, J)
                    one_chunk(layer, LAST, LAST_J)

            choose(pe, general, gathering, dense)


N_CONSTS = 12


def kernel(x, src, dst, L0_gnn_enc_w1, L0_gnn_enc_b1, L0_gnn_enc_w2, L0_gnn_enc_b2, L0_gnn_conv_w, L0_gnn_gru_wih,
           L0_gnn_gru_whh, L0_gnn_gru_bih, L0_gnn_gru_bhh, L0_gnn_dec_w1, L0_gnn_dec_b1, L0_gnn_dec_w2, L0_gnn_dec_b2):
    import numpy as np
    import concourse.bacc as bacc
    from concourse.bass_utils import run_bass_kernel_spmd

    def padded(index, filler, n):
        out = np.full(n, filler, np.int32)
        out[:len(index)] = np.asarray(index)
        return out

    def columns(flat):
        return np.ascontiguousarray(flat.reshape(-1, P).T)

    edges = TILE_COLS * P
    dst_pad = padded(dst, N_NODES, edges)
    x_pad = np.zeros((NODES_PAD, H), np.float32)
    x_pad[:N_NODES] = np.asarray(x)
    blocks = [np.asarray(L0_gnn_enc_w1).T, np.asarray(L0_gnn_enc_w2).T, np.asarray(L0_gnn_gru_wih).T,
              np.asarray(L0_gnn_gru_whh).T, np.asarray(L0_gnn_dec_w1).T, np.asarray(L0_gnn_dec_w2).T]
    blocks += [np.asarray(L0_gnn_conv_w)[layer] for layer in range(LAYERS)]
    bias = [np.asarray(v).reshape(-1, H) for v in (L0_gnn_enc_b1, L0_gnn_enc_b2, L0_gnn_gru_bih, L0_gnn_gru_bhh, L0_gnn_dec_b1)]
    arrays = {
        "x": x_pad,
        "src": columns(padded(src, 0, edges)),
        "dst": columns(dst_pad),
        "dst_next": columns(padded(dst_pad[1:], N_NODES, edges)),
        "firsts": columns(padded(dst_pad[::P], N_NODES, FIRST_COLS * P)),
        "weights": np.ascontiguousarray(np.concatenate(blocks, axis=1)),
        "biases": np.ascontiguousarray(np.concatenate(bias, axis=0).T),
        "dec_b2": np.asarray(L0_gnn_dec_b2).reshape(1, H),
    }
    nc = bacc.Bacc("TRN2", target_bir_lowering=False, num_devices=1)
    aps = [nc.dram_tensor(f"in_{k}", a.shape, mybir.dt.from_np(a.dtype), kind="ExternalInput").ap() for k, a in arrays.items()]
    out = nc.dram_tensor("out", (NODES_PAD, H), F32, kind="ExternalOutput").ap()
    gnn(nc, *aps, out)
    result = run_bass_kernel_spmd(nc, [{f"in_{k}": a for k, a in arrays.items()}], core_ids=[0])
    return result.results[0]["out"][:N_NODES]
```
